# Optimizing a Trainium2 kernel written in Bass

```python
import numpy as np
import jax
import jax.numpy as jnp

def _softmax(x, axis=-1):
    return jax.nn.softmax(x, axis=axis)

def _gelu(x):
    return jax.nn.gelu(x, approximate=True)

def _silu(x):
    return jax.nn.silu(x)

def _sigmoid(x):
    return jax.nn.sigmoid(x)

def _layernorm(x, axis=-1, eps=1e-05):
    m = jnp.mean(x, axis=axis, keepdims=True)
    v = jnp.var(x, axis=axis, keepdims=True)
    return (x - m) / jnp.sqrt(v + eps)

def _scatter_add(tgt, idx, src, axis=0):
    return tgt.at[idx].add(src)

def _segment_sum(src, seg, n):
    return jax.ops.segment_sum(src, seg, n)
kernel_name = 'mk_perceiver_d2_seqx_r4_b11586'

def setup_inputs(seed: int=0):
    np.random.seed(seed)
    _w = jnp.asarray

    def _rec_inputs():
        import jax
        import jax.numpy as jnp
        _rk = jax.random.key(seed)
        x = -0.0002928 + 1 * jax.random.normal(jax.random.fold_in(_rk, 1), (128, 32, 256), jnp.float32)
        _lenS = 32 - jax.random.randint(jax.random.fold_in(_rk, 7), (128,), 0, max(1, 32 // 4) + 1, jnp.int32)
        _lenS2 = 257 - jax.random.randint(jax.random.fold_in(_rk, 8), (128,), 0, max(1, 257 // 4) + 1, jnp.int32)
        _ctx_1024P = jax.random.normal(jax.random.fold_in(_rk, 11), (128, 16, 256), jnp.float32)
        _ctx_1024c = jax.random.dirichlet(jax.random.fold_in(_rk, 511), 0.3 * jnp.ones((16,), jnp.float32), (128, 257))
        _ctx_1024t = jnp.einsum('bsk,bkd->bsd', _ctx_1024c, _ctx_1024P)
        _ctx_1024t = _ctx_1024t * jax.lax.rsqrt(jnp.mean(jnp.square(_ctx_1024t)) + 1e-12) * 0.953939
        ctx_1024 = -1.39393e-06 + 0.999914 * (_ctx_1024t + 0.3 * jax.random.normal(jax.random.fold_in(_rk, 611), (128, 257, 256), jnp.float32))
        return (x, ctx_1024)
    x, ctx_1024 = _rec_inputs()

    def _L0_xattn_setup():
        import jax, jax.numpy as jnp
        import numpy as np
        DIM = 256
        NUM_HEADS = 16
        HEAD_DIM = DIM // NUM_HEADS
        key = jax.random.key(seed)
        ks = jax.random.split(key, 11)
        B, N, C = (2, 512, DIM)
        s = 1.0 / np.sqrt(C)
        inp = {'q': jax.random.normal(ks[0], (B, N, C), jnp.float32), 'k': jax.random.normal(ks[1], (B, N, C), jnp.float32), 'v': jax.random.normal(ks[2], (B, N, C), jnp.float32), 'Wq': jax.random.normal(ks[3], (C, C), jnp.float32) * s, 'bq': jnp.zeros((C,), jnp.float32), 'Wk': jax.random.normal(ks[4], (C, C), jnp.float32) * s, 'bk': jnp.zeros((C,), jnp.float32), 'Wv': jax.random.normal(ks[5], (C, C), jnp.float32) * s, 'bv': jnp.zeros((C,), jnp.float32), 'Wo': jax.random.normal(ks[6], (C, C), jnp.float32) * s, 'bo': jnp.zeros((C,), jnp.float32)}
        return inp
    _L0_xattn_all = _L0_xattn_setup()
    _L0_xattn_in = {k: v for k, v in _L0_xattn_all.items() if k in ('Wq', 'bq', 'Wk', 'bk', 'Wv', 'bv', 'Wo', 'bo')}
    del _L0_xattn_all

    def _L0_attn_setup():
        import jax, jax.numpy as jnp
        import numpy as np
        B, T, E, H = (2, 512, 256, 16)
        HD = E // H

        def _xavier(key, shape):
            limit = float(np.sqrt(6.0 / (shape[0] + shape[1])))
            return jax.random.uniform(key, shape, dtype=jnp.float32, minval=-limit, maxval=limit)
        key = jax.random.key(seed)
        kx, kq, kk, kv = jax.random.split(key, 4)
        return {'x': jax.random.normal(kx, (B, T, E), dtype=jnp.float32), 'w_Q': _xavier(kq, (E, E)), 'w_K': _xavier(kk, (E, E)), 'w_V': _xavier(kv, (E, E))}
    _L0_attn_all = _L0_attn_setup()
    _L0_attn_in = {k: v for k, v in _L0_attn_all.items() if k in ('w_Q', 'w_K', 'w_V')}
    del _L0_attn_all

    def _L0_ffn_setup():
        import jax, jax.numpy as jnp
        import numpy as np
        from jax import lax
        DIM = 256
        HID = 512
        E = 8
        K = 2
        B, T = (2, 128)
        key = jax.random.key(seed)
        ks = jax.random.split(key, 5)
        scale = 1.0 / np.sqrt(DIM)
        x = jax.random.normal(ks[0], (B, T, DIM), dtype=jnp.float32)
        router_w = jax.random.normal(ks[1], (E, DIM), dtype=jnp.float32) * scale
        w_gate = jax.random.normal(ks[2], (E, HID, DIM), dtype=jnp.float32) * scale
        w_up = jax.random.normal(ks[3], (E, HID, DIM), dtype=jnp.float32) * scale
        w_down = jax.random.normal(ks[4], (E, DIM, HID), dtype=jnp.float32) * (1.0 / np.sqrt(HID))
        return {'x': x, 'router_w': router_w, 'w_gate': w_gate, 'w_up': w_up, 'w_down': w_down}
    _L0_ffn_all = _L0_ffn_setup()
    _L0_ffn_in = {k: v for k, v in _L0_ffn_all.items() if k in ('router_w', 'w_gate', 'w_up', 'w_down')}
    del _L0_ffn_all

    def _L1_xattn_setup():
        import jax, jax.numpy as jnp
        import numpy as np
        N_HEADS = 16

        def _split(x, n_heads):
            b, s, d = x.shape
            return x.reshape(b, s, n_heads, d // n_heads).transpose(0, 2, 1, 3)
        key = jax.random.key(seed)
        k1, k2, k3, k4, k5 = jax.random.split(key, 5)
        B, S, D = (4, 512, 256)
        q = jax.random.normal(k1, (B, S, D), dtype=jnp.float32)
        k = jax.random.normal(k2, (B, S, D), dtype=jnp.float32)
        v = jax.random.normal(k3, (B, S, D), dtype=jnp.float32)
        Wq = jax.random.normal(k4, (D, D), dtype=jnp.float32) * D ** (-0.5)
        Wo = jax.random.normal(k5, (D, D), dtype=jnp.float32) * D ** (-0.5)
        return {'q': q, 'k': k, 'v': v, 'Wq': Wq, 'Wo': Wo}
    _L1_xattn_all = _L1_xattn_setup()
    _L1_xattn_in = {k: v for k, v in _L1_xattn_all.items() if k in ('Wq', 'Wo')}
    del _L1_xattn_all

    def _L1_attn_setup():
        import jax, jax.numpy as jnp
        import numpy as np
        NUM_HEADS = 16
        HEAD_DIM = 64
        NEG_INF = -1000000000.0

        def rotary_embedding(x, seq_len, head_dim):
            positions = jnp.arange(seq_len)
            dim_pairs = jnp.arange(0, head_dim, 2)
            freqs = 1.0 / 10000.0 ** (dim_pairs / head_dim)
            angles = positions[:, None] * freqs[None, :]
            cos = jnp.cos(angles)[:, None, :]
            sin = jnp.sin(angles)[:, None, :]
            x1 = x[..., ::2]
            x2 = x[..., 1::2]
            out1 = x1 * cos - x2 * sin
            out2 = x1 * sin + x2 * cos
            return jnp.stack([out1, out2], axis=-1).reshape(x.shape)
        key = jax.random.key(seed)
        k1, k2, k3 = jax.random.split(key, 3)
        batch, seq_len, embed_dim = (2, 512, 256)
        x = jax.random.normal(k1, (batch, seq_len, embed_dim), dtype=jnp.float32)
        W_qkv = jax.random.normal(k2, (embed_dim, 3 * NUM_HEADS * HEAD_DIM), dtype=jnp.float32) * 0.02
        W_out = jax.random.normal(k3, (NUM_HEADS * HEAD_DIM, embed_dim), dtype=jnp.float32) * 0.02
        return {'x': x, 'W_qkv': W_qkv, 'W_out': W_out}
    _L1_attn_all = _L1_attn_setup()
    _L1_attn_in = {k: v for k, v in _L1_attn_all.items() if k in ('W_qkv', 'W_out')}
    del _L1_attn_all

    def _L1_ffn_setup():
        import jax, jax.numpy as jnp
        import numpy as np
        EPS = 1e-08
        key = jax.random.key(seed)
        kx, kw = jax.random.split(key)
        x = jax.random.normal(kx, (8, 1024, 256), dtype=jnp.float32)
        weight = jax.random.normal(kw, (256, 256), dtype=jnp.float32) * (1.0 / np.sqrt(256))
        return {'x': x, 'weight': weight}
    _L1_ffn_all = _L1_ffn_setup()
    _L1_ffn_in = {k: v for k, v in _L1_ffn_all.items() if k in ('weight',)}
    del _L1_ffn_all
    return {'x': x, 'ctx_1024': ctx_1024, 'L0_xattn_Wq': _L0_xattn_in['Wq'], 'L0_xattn_bq': _L0_xattn_in['bq'], 'L0_xattn_Wk': _L0_xattn_in['Wk'], 'L0_xattn_bk': _L0_xattn_in['bk'], 'L0_xattn_Wv': _L0_xattn_in['Wv'], 'L0_xattn_bv': _L0_xattn_in['bv'], 'L0_xattn_Wo': _L0_xattn_in['Wo'], 'L0_xattn_bo': _L0_xattn_in['bo'], 'L0_attn_w_Q': _L0_attn_in['w_Q'], 'L0_attn_w_K': _L0_attn_in['w_K'], 'L0_attn_w_V': _L0_attn_in['w_V'], 'L0_ffn_router_w': _L0_ffn_in['router_w'], 'L0_ffn_w_gate': _L0_ffn_in['w_gate'], 'L0_ffn_w_up': _L0_ffn_in['w_up'], 'L0_ffn_w_down': _L0_ffn_in['w_down'], 'L1_xattn_Wq': _L1_xattn_in['Wq'], 'L1_xattn_Wo': _L1_xattn_in['Wo'], 'L1_attn_W_qkv': _L1_attn_in['W_qkv'], 'L1_attn_W_out': _L1_attn_in['W_out'], 'L1_ffn_weight': _L1_ffn_in['weight']}

def reference(x, ctx_1024, L0_xattn_Wq, L0_xattn_bq, L0_xattn_Wk, L0_xattn_bk, L0_xattn_Wv, L0_xattn_bv, L0_xattn_Wo, L0_xattn_bo, L0_attn_w_Q, L0_attn_w_K, L0_attn_w_V, L0_ffn_router_w, L0_ffn_w_gate, L0_ffn_w_up, L0_ffn_w_down, L1_xattn_Wq, L1_xattn_Wo, L1_attn_W_qkv, L1_attn_W_out, L1_ffn_weight):
    import jax
    import jax.numpy as jnp

    def _L0_xattn_ref(q, k, v, Wq, bq, Wk, bk, Wv, bv, Wo, bo):
        import jax, jax.numpy as jnp
        import numpy as np
        DIM = 256
        NUM_HEADS = 16
        HEAD_DIM = DIM // NUM_HEADS
        B, Nq, C = q.shape
        Nkv = k.shape[1]
        H, D = (NUM_HEADS, HEAD_DIM)
        qh = (q @ Wq.T + bq).reshape(B, Nq, H, D).transpose(0, 2, 1, 3)
        kh = (k @ Wk.T + bk).reshape(B, Nkv, H, D).transpose(0, 2, 1, 3)
        vh = (v @ Wv.T + bv).reshape(B, Nkv, H, D).transpose(0, 2, 1, 3)
        scale = D ** (-0.5)
        attn = jax.nn.softmax(jnp.einsum('bhqd,bhkd->bhqk', qh, kh) * scale, axis=-1)
        out = jnp.einsum('bhqk,bhkd->bhqd', attn, vh)
        out = out.transpose(0, 2, 1, 3).reshape(B, Nq, C)
        return out @ Wo.T + bo

    def _L0_attn_ref(x, w_Q, w_K, w_V):
        import jax, jax.numpy as jnp
        import numpy as np
        B, T, E, H = (2, 512, 256, 16)
        HD = E // H

        def _xavier(key, shape):
            limit = float(np.sqrt(6.0 / (shape[0] + shape[1])))
            return jax.random.uniform(key, shape, dtype=jnp.float32, minval=-limit, maxval=limit)
        Bs, Ts, Es = x.shape
        q = (x @ w_Q).reshape(Bs, Ts, H, HD).transpose(0, 2, 1, 3)
        k = (x @ w_K).reshape(Bs, Ts, H, HD).transpose(0, 2, 1, 3)
        v = (x @ w_V).reshape(Bs, Ts, H, HD).transpose(0, 2, 1, 3)
        scores = jnp.einsum('bhtd,bhsd->bhts', q, k) / jnp.sqrt(jnp.asarray(HD, x.dtype))
        probs = jax.nn.softmax(scores, axis=-1)
        attn = jnp.einsum('bhts,bhsd->bhtd', probs, v)
        return attn.transpose(0, 2, 1, 3).reshape(Bs, Ts, H * HD)

    def _L0_ffn_ref(x, router_w, w_gate, w_up, w_down):
        import jax, jax.numpy as jnp
        import numpy as np
        from jax import lax
        DIM = 256
        HID = 512
        E = 8
        K = 2
        B, T = (2, 128)
        Bb, Tt, D = x.shape
        N = Bb * Tt
        xf = x.reshape(N, D)
        logits = xf @ router_w.T
        routing = jax.nn.softmax(logits, axis=-1)
        top_w, top_i = lax.top_k(routing, K)
        top_w = top_w / jnp.sum(top_w, axis=-1, keepdims=True)
        combine = jnp.zeros((N, E), dtype=x.dtype)
        combine = combine.at[jnp.arange(N)[:, None], top_i].add(top_w)
        g = jnp.einsum('nd,ehd->neh', xf, w_gate)
        u = jnp.einsum('nd,ehd->neh', xf, w_up)
        h = jax.nn.silu(g) * u
        y = jnp.einsum('neh,edh->ned', h, w_down)
        out = jnp.einsum('ned,ne->nd', y, combine)
        return out.reshape(Bb, Tt, D)

    def _L1_xattn_ref(q, k, v, Wq, Wo):
        import jax, jax.numpy as jnp
        import numpy as np
        N_HEADS = 16

        def _split(x, n_heads):
            b, s, d = x.shape
            return x.reshape(b, s, n_heads, d // n_heads).transpose(0, 2, 1, 3)
        d_model = q.shape[-1]
        d_k = d_model // N_HEADS
        Q = _split(q @ Wq.T, N_HEADS)
        K = _split(k @ Wq.T, N_HEADS)
        V = _split(v @ Wq.T, N_HEADS)
        scores = jnp.einsum('bhqd,bhkd->bhqk', Q, K) / jnp.sqrt(jnp.asarray(d_k, Q.dtype))
        attn = jax.nn.softmax(scores, axis=-1)
        out = jnp.einsum('bhqk,bhkd->bhqd', attn, V)
        b, h, s, dk = out.shape
        out = out.transpose(0, 2, 1, 3).reshape(b, s, h * dk)
        return out @ Wo.T

    def _L1_attn_ref(x, W_qkv, W_out):
        import jax, jax.numpy as jnp
        import numpy as np
        NUM_HEADS = 16
        HEAD_DIM = 64
        NEG_INF = -1000000000.0

        def rotary_embedding(x, seq_len, head_dim):
            positions = jnp.arange(seq_len)
            dim_pairs = jnp.arange(0, head_dim, 2)
            freqs = 1.0 / 10000.0 ** (dim_pairs / head_dim)
            angles = positions[:, None] * freqs[None, :]
            cos = jnp.cos(angles)[:, None, :]
            sin = jnp.sin(angles)[:, None, :]
            x1 = x[..., ::2]
            x2 = x[..., 1::2]
            out1 = x1 * cos - x2 * sin
            out2 = x1 * sin + x2 * cos
            return jnp.stack([out1, out2], axis=-1).reshape(x.shape)
        batch, seq_len, embed_dim = x.shape
        qkv = jnp.einsum('bse,ef->bsf', x, W_qkv)
        qkv = qkv.reshape(batch, seq_len, 3, NUM_HEADS, HEAD_DIM)
        q, k, v = (qkv[:, :, 0], qkv[:, :, 1], qkv[:, :, 2])
        q = rotary_embedding(q, seq_len, HEAD_DIM)
        k = rotary_embedding(k, seq_len, HEAD_DIM)
        scale = 1.0 / jnp.sqrt(jnp.asarray(HEAD_DIM, dtype=x.dtype))
        scores = jnp.einsum('bqhd,bkhd->bhqk', q, k) * scale
        mask = jnp.tril(jnp.ones((seq_len, seq_len), dtype=bool))[None, None, :, :]
        scores = jnp.where(mask, scores, NEG_INF)
        weights = jax.nn.softmax(scores, axis=-1)
        out = jnp.einsum('bhqk,bkhd->bqhd', weights, v)
        out = out.reshape(batch, seq_len, NUM_HEADS * HEAD_DIM)
        return jnp.einsum('bsf,fe->bse', out, W_out)

    def _L1_ffn_ref(x, weight):
        import jax, jax.numpy as jnp
        import numpy as np
        EPS = 1e-08
        w_scale = jnp.mean(jnp.abs(weight)) + EPS
        u = weight / w_scale
        w_quant = u + jax.lax.stop_gradient(jnp.clip(jnp.round(u), -1.0, 1.0) - u)
        a_scale = jnp.max(jnp.abs(x), axis=-1, keepdims=True) + EPS
        z = jnp.clip(x / a_scale * 127.0, -128.0, 127.0)
        a_quant = z + jax.lax.stop_gradient(jnp.round(z) - z)
        y = jnp.einsum('bsi,oi->bso', a_quant, w_quant)
        y = y * (w_scale * a_scale / 127.0)
        return y
    x = x + _L0_xattn_ref(_layernorm(x, axis=-1), ctx_1024, ctx_1024, L0_xattn_Wq, L0_xattn_bq, L0_xattn_Wk, L0_xattn_bk, L0_xattn_Wv, L0_xattn_bv, L0_xattn_Wo, L0_xattn_bo)
    x = x + _L0_attn_ref(_layernorm(x, axis=-1), L0_attn_w_Q, L0_attn_w_K, L0_attn_w_V)
    x = x + _L0_ffn_ref(_layernorm(x, axis=-1), L0_ffn_router_w, L0_ffn_w_gate, L0_ffn_w_up, L0_ffn_w_down)
    x = x + _L1_xattn_ref(_layernorm(x, axis=-1), ctx_1024, ctx_1024, L1_xattn_Wq, L1_xattn_Wo)
    x = x + _L1_attn_ref(_layernorm(x, axis=-1), L1_attn_W_qkv, L1_attn_W_out)
    x = x + _L1_ffn_ref(_layernorm(x, axis=-1), L1_ffn_weight)
    return x

_drawn_inputs = setup_inputs


def setup_inputs(seed=0):
    import zlib

    import numpy as np

    out = dict(_drawn_inputs(seed))
    spreads = {'L0_xattn_bq': (0.0, 0.1),
     'L0_xattn_bk': (0.0, 0.1),
     'L0_xattn_bv': (0.0, 0.1),
     'L0_xattn_bo': (0.0, 0.1)}
    factors = {}
    for name, (base, spread) in spreads.items():
        noise = np.random.default_rng([zlib.crc32(name.encode()), seed]).standard_normal(out[name].shape)
        drawn = base * np.exp(spread * noise) if base else spread * noise
        out[name] = jnp.asarray(drawn.astype(out[name].dtype))
    for name, factor in factors.items():
        out[name] = (out[name] * factor).astype(out[name].dtype)
    return out
```

```python
from contextlib import ExitStack

import numpy as np

import concourse.bass as bass
from concourse import mybir

F32 = mybir.dt.float32
F32R = mybir.dt.float32r
BF16 = mybir.dt.bfloat16
U32 = mybir.dt.uint32
ALU = mybir.AluOpType
ACT = mybir.ActivationFunctionType
AX_X = mybir.AxisListType.X

P = 128
B, T, D = 128, 32, 256
S = 257
S_EVEN = S + 1
KD = D // P
H = 16
BPG = P // T
G = B * T // P
GPS = 4
SG = G // GPS
BPS = BPG * GPS
HPH = H // KD
XD = D // H
HG = 4
HPG = H // HG
CHUNKS = [(0, 86), (86, 86), (172, 85)]
E, HID = 8, 512
KH = HID // P
D1 = 64
F1 = H * D1
LN_EPS = 1e-5
NEG_INF = -1e9
ROUND = 1.5 * 2.0 ** 23


class Program:

    def __init__(self, nc, stack):
        self.nc, self.stack = nc, stack
        self.sems, self.count, self.done = {}, {}, {}
        self.queues = {e: [] for e in ("tensor", "vector", "scalar", "gpsimd", "sync")}
        self.reached = {e: {} for e in self.queues}

    def do(self, engine, emit, done=None, inc=1):
        sem = None
        if done is not None:
            kind = done[0]
            if kind not in self.sems:
                self.sems[kind] = self.stack.enter_context(self.nc.semaphore(kind))
                self.count[kind] = 0
            self.count[kind] += inc
            assert done not in self.done, done
            self.done[done] = (kind, self.count[kind])
            sem = self.sems[kind]
        self.queues[engine].append((emit, sem, inc))

    def wait(self, engine, *names):
        self.queues[engine].append((None, names, 0))

    def _emit(self, engine, eng):
        reached = self.reached[engine]
        for emit, sem, inc in self.queues[engine]:
            if emit is None:
                for name in sem:
                    kind, value = self.done[name]
                    if reached.get(kind, 0) < value:
                        eng.wait_ge(self.sems[kind], value)
                        reached[kind] = value
                continue
            ins = emit(eng)
            if sem is not None:
                ins.then_inc(sem, inc)
        self.queues[engine] = []

    def run(self):
        with self.nc.Block() as block:
            @block.sync
            def _(eng):
                self._emit("sync", eng)

            @block.gpsimd
            def _(eng):
                self._emit("gpsimd", eng)

            @block.scalar
            def _(eng):
                self._emit("scalar", eng)

            @block.vector
            def _(eng):
                self._emit("vector", eng)

            @block.tensor
            def _(eng):
                self._emit("tensor", eng)

    def dma(self, out, in_, done):
        self.do("sync", lambda e: e.dma_start(out, in_), done, 16)

    def matmul(self, out, lhsT, rhs, start=True, stop=True, done=None):
        self.do("tensor", lambda e: e.matmul(out, lhsT, rhs, start=start, stop=stop), done)

    def transpose(self, out, in_, ident, done=None):
        self.do("tensor", lambda e: e.transpose(out, in_, ident), done)

    def activation(self, out, in_, func, done=None, **kw):
        self.do("scalar", lambda e: e.activation(out, in_, func, **kw), done)

    def tensor_tensor(self, out, in0, in1, op, done=None, engine="vector"):
        self.do(engine, lambda e: e.tensor_tensor(out, in0, in1, op), done)

    def tensor_scalar(self, out, in0, s1, s2, op0, op1=None, done=None):
        if op1 is None:
            self.do("vector", lambda e: e.tensor_scalar(out, in0, s1, s2, op0), done)
        else:
            self.do("vector", lambda e: e.tensor_scalar(out, in0, s1, s2, op0, op1), done)

    def scalar_tensor_tensor(self, out, in0, scalar, in1, op0, op1, done=None):
        self.do("vector", lambda e: e.scalar_tensor_tensor(out=out, in0=in0, scalar=scalar, in1=in1,
                                                           op0=op0, op1=op1), done)

    def reduce(self, out, in_, op, done=None, **kw):
        self.do("vector", lambda e: e.tensor_reduce(out, in_, AX_X, op, **kw), done)

    def reciprocal(self, out, in_, done=None):
        self.do("vector", lambda e: e.reciprocal(out, in_), done)

    def copy(self, out, in_, done=None, engine="vector"):
        self.do(engine, lambda e: e.tensor_copy(out, in_), done)

    def memset(self, out, value, done=None, engine="vector"):
        self.do(engine, lambda e: e.memset(out, value), done)

    def split_product(self, out, lhs, rhs, pieces, done=None):
        steps = []
        for k in range(pieces):
            (lh, ll), (rh, rl) = lhs(k), rhs(k)
            steps += [(lh, rh), (lh, rl), (ll, rh)]
        for n, (a, b) in enumerate(steps):
            last = n == len(steps) - 1
            self.matmul(out, a, b, start=n == 0, stop=last, done=done if last else None)


class Split:

    def __init__(self, nc, stack, name, shape):
        self.hi = stack.enter_context(nc.sbuf_tensor(name + "_hi", shape, F32R))
        self.lo = stack.enter_context(nc.sbuf_tensor(name + "_lo", shape, F32R))

    def fill(self, p, src, at, name, ready, free=(), bias=None):
        hi, lo = at(self.hi), at(self.lo)
        p.wait("scalar", *ready, *free)
        if bias is None:
            p.activation(hi, src, ACT.Copy, done=("hi_" + name[0], *name[1:]))
        else:
            p.activation(hi, src, ACT.Identity, bias=bias, done=("hi_" + name[0], *name[1:]))
        p.wait("vector", *ready, *free, ("hi_" + name[0], *name[1:]))
        if bias is None:
            p.tensor_tensor(lo, src, hi.bitcast(F32), ALU.subtract, done=("lo_" + name[0], *name[1:]))
        else:
            p.scalar_tensor_tensor(lo, src, bias, hi.bitcast(F32), ALU.add, ALU.subtract,
                                   done=("lo_" + name[0], *name[1:]))

    def pair(self, at):
        return at(self.hi), at(self.lo)


def both(kind, *rest):
    return ("hi_" + kind, *rest), ("lo_" + kind, *rest)


class Banks:

    def __init__(self, tiles):
        self.tiles, self.readers, self.n = tiles, [()] * len(tiles), 0

    def take(self, readers):
        slot = self.n % len(self.tiles)
        self.n += 1
        free, self.readers[slot] = self.readers[slot], readers
        return self.tiles[slot], free


class Weights:

    def __init__(self, p, nc, stack, tag, columns):
        self.p, self.nc, self.stack, self.tag = p, nc, stack, tag
        self.stage = stack.enter_context(nc.sbuf_tensor(f"stage_{tag}", [P, columns], F32))
        self.before = ()

    def load(self, name, dram):
        shape = list(dram.shape)
        n = int(np.prod(shape[1:]))
        w = Split(self.nc, self.stack, f"w_{name}_{self.tag}", [P, n])
        self.p.wait("sync", *self.before)
        self.p.dma(self.stage[:, 0:n], dram.rearrange("p a b -> p (a b)"), ("w_in", self.tag, name))
        w.fill(self.p, self.stage[:, 0:n], lambda t: t[:, :], ("w", self.tag, name),
               [("w_in", self.tag, name)])
        self.before = both("w", self.tag, name)
        w.ready = self.before
        w.width = shape[2]
        return w


def part(w, k, c0, c1):
    return w.pair(lambda t: t[:, k * w.width + c0:k * w.width + c1])


class LayerNorm:

    def __init__(self, p, nc, stack, tag, X, consts, dest):
        self.p, self.tag, self.X, self.consts, self.dest = p, tag, X, consts, dest
        t = lambda n, s: stack.enter_context(nc.sbuf_tensor(f"ln_{n}_{tag}", s, F32))
        self.stats = t("stats", [P, GPS, 6])
        self.mv = t("mean_var", [P, GPS, 2])
        self.var = t("var", [P, GPS])
        self.rstd = t("rstd", [P, GPS])
        self.xn = t("xn", [P, GPS, D])

    def normalise(self, s, ready):
        p, tag = self.p, self.tag
        p.wait("vector", *ready)
        for j in range(GPS):
            src = self.X[:, GPS * s + j, :]
            p.do("vector", lambda e, j=j, src=src: e.bn_stats(self.stats[:, j, :], src), ("ln_stats", tag, s, j))
            p.wait("vector", ("ln_stats", tag, s, j))
            p.do("vector", lambda e, j=j: e.bn_aggr(self.mv[:, j, :], self.stats[:, j, :]), ("ln_aggr", tag, s, j))
        p.wait("vector", ("ln_aggr", tag, s, GPS - 1))
        p.tensor_scalar(self.var[:, :], self.mv[:, :, 1], LN_EPS, None, ALU.add, done=("ln_var", tag, s))
        p.wait("gpsimd", ("ln_var", tag, s))
        p.tensor_tensor(self.rstd[:, :], self.var[:, :], self.consts["minus_half"][:, :], ALU.pow,
                        done=("ln_rstd", tag, s), engine="gpsimd")
        p.wait("vector", ("ln_rstd", tag, s))
        if s:
            p.wait("vector", *[("ln_T", tag, s - 1, k) for k in range(KD)])
        for j in range(GPS):
            p.tensor_scalar(self.xn[:, j, :], self.X[:, GPS * s + j, :], self.mv[:, j, 0:1],
                            self.rstd[:, j:j + 1], ALU.subtract, ALU.mult, done=("ln_xn", tag, s, j))

    def turn(self, s, banks, free):
        p, tag = self.p, self.tag
        for k in range(KD):
            bank, bank_free = banks.take(both("xT", tag, s, k))
            p.wait("tensor", ("ln_xn", tag, s, GPS - 1), *bank_free)
            for j in range(GPS):
                p.transpose(bank[:, j * P:(j + 1) * P], self.xn[:, j, k * P:(k + 1) * P],
                            self.consts["ident"][:, :], ("ln_T", tag, s, k) if j == GPS - 1 else None)
            self.dest.fill(p, bank[:, :], lambda t, k=k: self.at(t, s, k), ("xT", tag, s, k),
                           [("ln_T", tag, s, k)], free)

    def at(self, t, s, k):
        return t[:, k, :] if t.shape[2] == GPS * P else t[:, k, s * GPS * P:(s + 1) * GPS * P]


def cross_attention(p, nc, tag, X, ctx, consts, mats, biases, x_ready):
    with ExitStack() as stack:
        def sb(name, shape, dt=F32):
            return stack.enter_context(nc.sbuf_tensor(f"{name}_{tag}", shape, dt))

        def split(name, shape):
            return Split(nc, stack, f"{name}_{tag}", shape)

        loader = Weights(p, nc, stack, tag, KD * D)
        w = {n: loader.load(n, mats[n]) for n in ("q", "k", "v", "o") if n in mats}
        w.setdefault("k", w["q"])
        w.setdefault("v", w["q"])
        all_weights = [r for m in w.values() for r in m.ready]

        xT = split("xT", [P, KD, GPS * P])
        ln = LayerNorm(p, nc, stack, tag, X, consts, xT)
        q32 = sb("q32", [P, GPS * P])
        qT = [split(f"qT{i}", [P, KD, GPS * P]) for i in range(2)]
        q_diag = [split(f"q_diag{i}", [P, KD, HPH * T]) for i in range(2)]
        ctx_in = [sb(f"ctx_in{i}", [P, KD, BPG, S]) for i in range(2)]
        ctxT = [split(f"ctxT{i}", [P, KD, S_EVEN]) for i in range(3)]
        kT = [split(f"kT{i}", [P, KD, S_EVEN]) for i in range(2)]
        v = [split(f"v{i}", [P, len(CHUNKS), D]) for i in range(2)]
        neg_max = [sb(f"neg_max{i}", [P, HG]) for i in range(2)]
        sums = [sb(f"sums{i}", [P, HG]) for i in range(2)]
        inv = [sb(f"inv{i}", [P, HG]) for i in range(2)]
        prob = [sb(f"prob{i}", [P, HG, S]) for i in range(2)]
        probT = [split(f"probT{i}", [P, len(CHUNKS), HG * P]) for i in range(2)]
        masked = sb("masked", [P, KD, HPH, T])
        attn32 = [sb(f"attn32{i}", [P, KD, P]) for i in range(2)]
        attnT = split("attnT", [P, KD, P])

        ps_score = stack.enter_context(nc.psum_tensor(f"ps_score_{tag}", [P, HG, 512], F32))
        probT_banks = Banks([stack.enter_context(nc.psum_tensor(f"ps_pT{i}_{tag}", [P, 512], F32))
                             for i in range(2)])
        banks = Banks([stack.enter_context(nc.psum_tensor(f"ps_{i}_{tag}", [P, 512], F32)) for i in range(2)])

        for i in range(3):
            for t in (ctxT[i].hi, ctxT[i].lo):
                p.memset(t[:, :, S:S_EVEN].bitcast(F32), 0.0, ("pad", tag, i, t.name))
        pads = [("pad", tag, i, t.name) for i in range(3) for t in (ctxT[i].hi, ctxT[i].lo)]
        bias_ready = []
        if biases:
            bq4 = sb("bq4", [P, KD])
            p.wait("vector", ("const_in",))
            p.tensor_scalar(bq4[:, :], biases["q"][:, :], XD ** -0.5, None, ALU.mult, done=("bq4", tag))
            bias_ready = [("bq4", tag)]

        def load_ctx(g):
            if g >= 2:
                p.wait("sync", *both("ctx", tag, (g - 1) * BPG - 1))
            p.dma(ctx_in[g % 2][:, :, :, :], ctx[g], (f"ctx_in{g % 2}", tag, g))

        def split_ctx(b):
            g, j = b // BPG, b % BPG
            free = [("k_ps", tag, b - 3, 1), ("v_ps", tag, b - 3, 1)] if b >= 3 else []
            ctxT[b % 3].fill(p, ctx_in[g % 2][:, :, j, :], lambda t: t[:, :, 0:S], ("ctx", tag, b),
                             [(f"ctx_in{g % 2}", tag, g)], free)

        def project_k(b):
            for m in range(KD):
                bank, free = banks.take(both("k", tag, b, m))
                p.wait("tensor", *both("ctx", tag, b), *free, *all_weights, *pads)
                p.split_product(bank[:, 0:S_EVEN], lambda k: part(w["k"], k, m * P, (m + 1) * P),
                                lambda k: ctxT[b % 3].pair(lambda t: t[:, k, :]), KD, ("k_ps", tag, b, m))
                old = [("score", tag, b - 2, HG - 1)] if b >= 2 else []
                kT[b % 2].fill(p, bank[:, 0:S_EVEN], lambda t: t[:, m, :], ("k", tag, b, m),
                               [("k_ps", tag, b, m)], old, biases["k"][:, m:m + 1] if biases else None)

        def project_v(b):
            for n, cs in enumerate(([0, 1], [2])):
                bank, free = banks.take(both("v", tag, b, n))
                p.wait("tensor", *both("ctx", tag, b), *free)
                for c in cs:
                    c0, sz = CHUNKS[c]
                    p.split_product(bank[0:sz, (c - cs[0]) * D:(c - cs[0] + 1) * D],
                                    lambda k: ctxT[b % 3].pair(lambda t: t[:, k, c0:c0 + sz]),
                                    lambda k: part(w["v"], k, 0, D), KD,
                                    ("v_ps", tag, b, n) if c == cs[-1] else None)
                old = [("pv", tag, b - 2)] if b >= 2 else []
                sz = CHUNKS[cs[0]][1]
                v[b % 2].fill(p, bank[0:sz, 0:len(cs) * D].rearrange("p (c d) -> p c d", d=D),
                              lambda t: t[0:sz, cs[0]:cs[-1] + 1, :], ("v", tag, b, n),
                              [("v_ps", tag, b, n)], old)

        def project_q(s):
            for m in range(KD):
                bank, free = banks.take((("q32", tag, s, m),))
                p.wait("tensor", *[r for k in range(KD) for r in both("xT", tag, s, k)], *free, *all_weights)
                p.split_product(bank[:, :], lambda k: part(w["q"], k, m * P, (m + 1) * P),
                                lambda k: xT.pair(lambda t: t[:, k, :]), KD, ("q_ps", tag, s, m))
                p.wait("vector", ("q_ps", tag, s, m), *bias_ready)
                if (s, m) != (0, 0):
                    p.wait("vector", *both("q", tag, *((s, 0) if m else (s - 1, 1))))
                p.tensor_scalar(q32[:, :], bank[:, :], XD ** -0.5, bq4[:, m:m + 1] if biases else 0.0,
                                ALU.mult, ALU.add, done=("q32", tag, s, m))
                old = [("q_diag_lo", tag, (s - 1) * BPS - 1)] if s >= 2 else []
                qT[s % 2].fill(p, q32[:, :], lambda t: t[:, m, :], ("q", tag, s, m), [("q32", tag, s, m)], old)

        def spread_q(b):
            s, j = b // BPS, b % BPS
            p.wait("gpsimd", *[r for m in range(KD) for r in both("q", tag, s, m)], ("const_in",))
            if b >= 2:
                p.wait("gpsimd", ("score", tag, b - 2, HG - 1))
            shape = [P, KD, HPH, T]
            mask = consts["head_rows"][:, :].unsqueeze(1).unsqueeze(3).to_broadcast(shape)
            for name, src, dst in (("q_diag_hi", qT[s % 2].hi, q_diag[b % 2].hi),
                                   ("q_diag_lo", qT[s % 2].lo, q_diag[b % 2].lo)):
                src = src[:, :, j * T:(j + 1) * T].bitcast(F32).unsqueeze(2).to_broadcast(shape)
                p.tensor_tensor(dst[:, :, :].rearrange("p m (h q) -> p m h q", q=T), src, mask, ALU.mult,
                                done=(name, tag, b), engine="gpsimd")

        def scores(b):
            for hg in range(HG):
                m, c0 = hg // 2, hg % 2 * P
                p.wait("tensor", ("q_diag_lo", tag, b), *both("k", tag, b, m))
                if b:
                    p.wait("tensor", ("exp", tag, b - 1, hg))
                p.split_product(ps_score[:, hg, 0:S_EVEN], lambda k: q_diag[b % 2].pair(lambda t: t[:, m, c0:c0 + P]),
                                lambda k: kT[b % 2].pair(lambda t: t[:, m, :]), 1, ("score", tag, b, hg))
            for n in range(2):
                p.wait("vector", ("score", tag, b, 2 * n + 1))
                if b >= 2:
                    p.wait("vector", ("exp", tag, b - 2, HG - 1))
                p.reduce(neg_max[b % 2][:, 2 * n:2 * n + 2], ps_score[:, 2 * n:2 * n + 2, 0:S], ALU.max,
                         ("neg_max", tag, b, n), negate=True)
            if b >= 2:
                p.wait("scalar", ("prob_T", tag, b - 2, 2), ("inv", tag, b - 2))
            for hg in range(HG):
                p.wait("scalar", ("neg_max", tag, b, hg // 2))
                p.activation(prob[b % 2][:, hg, :], ps_score[:, hg, 0:S], ACT.Exp, ("exp", tag, b, hg),
                             bias=neg_max[b % 2][:, hg:hg + 1], accum_out=sums[b % 2][:, hg:hg + 1])

        def normalise(b):
            p.wait("vector", ("exp", tag, b, HG - 1))
            if b >= 2:
                p.wait("vector", ("prob", tag, b - 2, HG - 1))
            p.reciprocal(inv[b % 2][:, :], sums[b % 2][:, :], ("inv", tag, b))
            p.wait("vector", ("inv", tag, b))
            for hg in range(HG):
                t = prob[b % 2][:, hg, :]
                p.tensor_scalar(t, t, inv[b % 2][:, hg:hg + 1], None, ALU.mult, done=("prob", tag, b, hg))

        def turn_prob(b, c):
            bank, free = probT_banks.take(both("pT", tag, b, c))
            c0, sz = CHUNKS[c]
            p.wait("tensor", ("prob", tag, b, HG - 1), *free)
            for hg in range(HG):
                p.transpose(bank[0:sz, hg * P:(hg + 1) * P], prob[b % 2][:, hg, c0:c0 + sz],
                            consts["ident"][:, :], ("prob_T", tag, b, c) if hg == HG - 1 else None)
            old = [("pv", tag, b - 2)] if b >= 2 else []
            probT[b % 2].fill(p, bank[0:sz, :], lambda t: t[0:sz, c, :], ("pT", tag, b, c),
                              [("prob_T", tag, b, c)], old)

        def weigh_v(b):
            g, j = b // BPG, b % BPG
            bank, free = banks.take((("masked", tag, b),))
            p.wait("tensor", *free, *[r for c in range(3) for r in both("pT", tag, b, c)],
                   *[r for n in range(2) for r in both("v", tag, b, n)])
            for m in range(KD):
                cols = lambda t, c: t[0:CHUNKS[c][1], c, m * P:(m + 1) * P]
                rows = lambda t, c: t[0:CHUNKS[c][1], c, m * HPH * T:(m + 1) * HPH * T]
                p.split_product(bank[:, m * HPH * T:(m + 1) * HPH * T], lambda c: v[b % 2].pair(lambda t: cols(t, c)),
                                lambda c: probT[b % 2].pair(lambda t: rows(t, c)), len(CHUNKS),
                                ("pv", tag, b) if m == KD - 1 else None)
            shape = [P, KD, HPH, T]
            p.wait("vector", ("pv", tag, b), ("const_in",))
            if b:
                p.wait("vector", ("attn32", tag, b - 1))
            p.tensor_tensor(masked[:, :, :, :], bank[:, :].rearrange("p (m h q) -> p m h q", m=KD, q=T),
                            consts["head_rows"][:, :].unsqueeze(1).unsqueeze(3).to_broadcast(shape), ALU.mult,
                            done=("masked", tag, b))
            p.wait("vector", ("masked", tag, b))
            if g >= 2:
                p.wait("vector", *both("attn", tag, g - 2))
            p.reduce(attn32[g % 2][:, :, j * T:(j + 1) * T], masked[:, :, :, :].rearrange("p m h q -> p m q h"),
                     ALU.add, ("attn32", tag, b))

        def split_attn(g):
            old = [("o_ps", tag, g - 1)] if g else []
            if biases:
                for m in range(KD):
                    attnT.fill(p, attn32[g % 2][:, m, :], lambda t: t[:, m, :],
                               ("attn" if m == KD - 1 else "attn_0", tag, g),
                               [("attn32", tag, g * BPG + BPG - 1)], old, biases["v"][:, m:m + 1])
            else:
                attnT.fill(p, attn32[g % 2][:, :, :], lambda t: t[:, :, :], ("attn", tag, g),
                           [("attn32", tag, g * BPG + BPG - 1)], old)

        def project_out(g):
            bank, free = banks.take((("x_out", tag, g),))
            p.wait("tensor", *both("attn", tag, g), *free)
            p.split_product(bank[:, 0:D], lambda k: attnT.pair(lambda t: t[:, k, :]),
                            lambda k: part(w["o"], k, 0, D), KD, ("o_ps", tag, g))
            p.wait("vector", ("o_ps", tag, g))
            p.tensor_tensor(X[:, g, :], X[:, g, :], bank[:, 0:D], ALU.add, done=("x_out", tag, g))
            if biases:
                p.wait("gpsimd", ("x_out", tag, g))
                p.tensor_tensor(X[:, g, :], X[:, g, :], biases["o"][:, :], ALU.add, ("x_bias", tag, g), "gpsimd")

        def free_xT(s):
            return [("q_ps", tag, s - 1, KD - 1)] if s else []

        load_ctx(0)
        load_ctx(1)
        ln.normalise(0, [x_ready(0)])
        ln.turn(0, banks, free_xT(0))
        project_q(0)
        for b in range(2):
            split_ctx(b)
            spread_q(b)
        project_k(0)
        for i in range(B + 1):
            if i < B:
                scores(i)
            if i:
                turn_prob(i - 1, 0)
                turn_prob(i - 1, 1)
            if i + 1 < B:
                project_k(i + 1)
            if i:
                turn_prob(i - 1, 2)
            if i < B:
                normalise(i)
                project_v(i)
            if i + 2 < B:
                split_ctx(i + 2)
                if (i + 3) % BPG == 0 and (i + 3) // BPG + 1 < G:
                    load_ctx((i + 3) // BPG + 1)
            if i >= BPG + 1 and (i - 1) % BPG == 0:
                project_out((i - 1) // BPG - 1)
            if i:
                weigh_v(i - 1)
                if i % BPG == 0:
                    split_attn(i // BPG - 1)
            s = i // BPS + 1
            if s < SG:
                if i % BPS == 4:
                    ln.normalise(s, [x_ready(s)])
                if i % BPS == 6:
                    ln.turn(s, banks, free_xT(s))
                if i % BPS == 8:
                    project_q(s)
            if i + 2 < B:
                spread_q(i + 2)
        project_out(G - 1)
        p.run()


def attend(p, tag, g, qT, kT, v, dv, head_rows, tiles, scale, bound, ready):
    R = P // head_rows
    NH = H // R
    t = tiles
    score = t["score"](g)
    p.wait("tensor", *ready, *t["score_free"](g))
    for n in range(NH):
        for b in range(BPG):
            for r in range(R):
                rows = slice(r * head_rows, (r + 1) * head_rows)
                last = (n, b, r) == (NH - 1, BPG - 1, R - 1)
                p.matmul(score[b * T:(b + 1) * T, r, n, :], qT(g)[rows, n, b * T:(b + 1) * T],
                         kT(g)[rows, n, b * T:(b + 1) * T], done=("s_score", tag, g) if last else None)
    src, grid = score, [P, R, NH, T]
    cell = lambda a: a.rearrange("p (r n q) -> p r n q", r=R, q=T)
    stat = lambda a: a.rearrange("p (r n) -> p r n", r=R)
    p.wait("vector", ("s_score", tag, g))
    e = g % 2
    if g >= 2:
        p.wait("vector", ("s_exp", tag, g - 2), ("s_probT", tag, g - 2), ("s_out", tag, g - 2))
    if bound is not None:
        for r in range(R):
            p.scalar_tensor_tensor(cell(t["sc"][e][:, :])[:, r], score[:, r], scale, bound.unsqueeze(1).to_broadcast([P, NH, T]),
                                   ALU.mult, ALU.min, ("s_masked", tag, g, r))
        p.wait("vector", ("s_masked", tag, g, R - 1))
        src, scale = cell(t["sc"][e][:, :]), 1.0
    p.reduce(stat(t["neg_max"][e][:, :]), src, ALU.max, ("s_max", tag, g), negate=True)
    p.wait("vector", ("s_max", tag, g))
    p.tensor_tensor(cell(t["shifted"][e][:, :]), src,
                    stat(t["neg_max"][e][:, :]).unsqueeze(3).to_broadcast(grid), ALU.add, ("s_shift", tag, g))
    p.wait("scalar", ("s_shift", tag, g))
    p.activation(t["prob"][e][:, :], t["shifted"][e][:, :], ACT.Exp, ("s_exp", tag, g), scale=scale)
    p.wait("vector", ("s_exp", tag, g))
    if g >= 2:
        p.wait("vector", ("s_pv", tag, g - 2))
    p.do("vector", lambda eng: eng.transpose(t["probT"][e][:, :], t["prob"][e][:, :]), ("s_probT", tag, g))
    p.reduce(t["sums"][e][:, :], t["prob"][e][:, :].rearrange("p (h q) -> p h q", q=T), ALU.add, ("s_sum", tag, g))
    p.wait("vector", ("s_sum", tag, g))
    p.reciprocal(t["inv"][e][:, :], t["sums"][e][:, :], ("s_inv", tag, g))


def weigh_self(p, tag, g, v, dv, head_rows, tiles):
    R = P // head_rows
    NH = H // R
    out, free = tiles["out"](g), tiles["out_free"](g)
    probT = tiles["probT"][g % 2]
    p.wait("tensor", ("s_probT", tag, g), *free)
    for h in range(H):
        c0 = (h % R * NH + h // R) * T
        for b in range(BPG):
            rows = slice(b * T, (b + 1) * T)
            p.matmul(out[rows, h, :], probT[rows, c0:c0 + T], v(g)[rows, h * dv:(h + 1) * dv],
                     done=("s_pv", tag, g) if (h, b) == (H - 1, BPG - 1) else None)


def by_head(ap, R):
    return ap.rearrange("p (r n) -> p n r", r=R)


def self_attention_0(p, nc, X, consts, mats):
    tag = "s0"
    with ExitStack() as stack:
        def sb(name, shape, dt=F32):
            return stack.enter_context(nc.sbuf_tensor(f"{name}_{tag}", shape, dt))

        PADW = H * T
        NT = PADW // P
        loader = Weights(p, nc, stack, tag, KD * PADW)
        w = {n: loader.load(n, mats[n]) for n in ("q", "k", "v")}
        ready_w = [r for m in w.values() for r in m.ready]
        xT = [Split(nc, stack, f"xT{i}_{tag}", [P, KD, GPS * P]) for i in range(2)]
        lns = [LayerNorm(p, nc, stack, tag, X, consts, xT[0])]
        ln = lns[0]
        qT = [sb(f"qT{i}", [P, NT, GPS * P]) for i in range(2)]
        kT = [sb(f"kT{i}", [P, NT, GPS * P]) for i in range(2)]
        v = [sb(f"v{i}", [P, D]) for i in range(2)]
        t = {n: [sb(f"{n}{i}", [P, H * T]) for i in range(2)] for n in ("shifted", "prob", "probT")}
        t |= {n: [sb(f"{n}{i}", [P, H]) for i in range(2)] for n in ("neg_max", "sums", "inv")}
        add = [sb(f"add{i}", [P, D]) for i in range(2)]
        ps_score = stack.enter_context(nc.psum_tensor(f"ps_score_{tag}", [P, NT, 512], F32))
        ps_out = stack.enter_context(nc.psum_tensor(f"ps_out_{tag}", [P, 2, 512], F32))
        banks = Banks([stack.enter_context(nc.psum_tensor(f"ps_{i}_{tag}", [P, 512], F32)) for i in range(2)])
        NH = H // NT
        t["score"] = lambda g: ps_score[:, :, 0:NH * T].rearrange("p r (n q) -> p r n q", q=T)
        t["score_free"] = lambda g: [("s_shift", tag, g - 1)] if g else []
        t["out"] = lambda g: ps_out[:, g % 2, 0:D].rearrange("p (h d) -> p h d", d=XD)
        t["out_free"] = lambda g: [("s_out", tag, g - 2)] if g >= 2 else []
        cols = lambda a: (lambda g: a[g // GPS % 2][:, :, g % GPS * P:(g % GPS + 1) * P])
        qg, kg, vg = cols(qT), cols(kT), lambda g: v[g % 2]

        def project(s, name, m):
            dst = {"q": qT, "k": kT}[name][s % 2]
            kind = f"s_{name}T"
            bank, free = banks.take(((kind, tag, s, m),))
            p.wait("tensor", *[r for k in range(KD) for r in both("xT", tag, s, k)], *free, *ready_w)
            p.split_product(bank[:, :], lambda k: part(w[name], k, m * P, (m + 1) * P),
                            lambda k: xT[s % 2].pair(lambda a: a[:, k, :]), KD, (kind + "_ps", tag, s, m))
            p.wait("scalar", (kind + "_ps", tag, s, m))
            if s >= 2:
                p.wait("scalar", ("s_score", tag, (s - 1) * GPS - 1))
            p.activation(dst[:, m, :], bank[:, :], ACT.Copy, (kind, tag, s, m))

        def project_v(g):
            s, j = g // GPS, g % GPS
            bank, free = banks.take((("s_v", tag, g),))
            p.wait("tensor", *[r for k in range(KD) for r in both("xT", tag, s, k)], *free, *ready_w)
            p.split_product(bank[:, 0:D], lambda k: xT[s % 2].pair(lambda a: a[:, k, j * P:(j + 1) * P]),
                            lambda k: part(w["v"], k, 0, D), KD, ("s_v_ps", tag, g))
            p.wait("scalar", ("s_v_ps", tag, g))
            if g >= 2:
                p.wait("scalar", ("s_pv", tag, g - 2))
            p.activation(v[g % 2][:, :], bank[:, 0:D], ACT.Copy, ("s_v", tag, g))

        def finish(g):
            shape = [P, H, XD]
            p.wait("vector", ("s_pv", tag, g), ("s_inv", tag, g))
            if g >= 2:
                p.wait("vector", ("s_x", tag, g - 2))
            inv = by_head(t["inv"][g % 2][:, :], NT)
            p.tensor_tensor(add[g % 2][:, :].rearrange("p (n r d) -> p n r d", r=NT, d=XD),
                            t["out"](g).rearrange("p (n r) d -> p n r d", r=NT),
                            inv.unsqueeze(3).to_broadcast([P, NH, NT, XD]), ALU.mult, ("s_out", tag, g))
            p.wait("gpsimd", ("s_out", tag, g))
            p.tensor_tensor(X[:, g, :], X[:, g, :], add[g % 2][:, :], ALU.add, ("s_x", tag, g), "gpsimd")

        def prepare(s):
            free = [("s_qT_ps", tag, s - 2, NT - 1), ("s_kT_ps", tag, s - 2, NT - 1),
                    ("s_v_ps", tag, (s - 1) * GPS - 1)] if s >= 2 else []
            ln.dest = xT[s % 2]
            ln.normalise(s, [])
            ln.turn(s, banks, free)

        def scores(g):
            s = g // GPS
            ready = [(f"s_{n}T", tag, s, m) for n in "qk" for m in range(NT)]
            attend(p, tag, g, qg, kg, vg, XD, T, t, XD ** -0.5, None, ready)

        prepare(0)
        for n in "qk":
            for m in range(NT):
                project(0, n, m)
        for g in range(G + 1):
            s, j = g // GPS, g % GPS
            if g < G:
                scores(g)
                project_v(g)
            if s + 1 < SG:
                if j == 0:
                    prepare(s + 1)
                if j in (2, 3):
                    for m in range(NT):
                        project(s + 1, "qk"[j - 2], m)
            if g:
                p.wait("tensor", ("s_v", tag, g - 1))
                weigh_self(p, tag, g - 1, vg, XD, T, t)
                finish(g - 1)
        p.run()


def experts(p, nc, X, consts, mats):
    tag = "moe"
    with ExitStack() as outer:
        xT = Split(nc, outer, f"xT_{tag}", [P, KD, B * T])
        share = outer.enter_context(nc.sbuf_tensor("share", [P, G, E], F32))
        with ExitStack() as stack:
            def sb(name, shape, dt=F32):
                return stack.enter_context(nc.sbuf_tensor(f"{name}_{tag}", shape, dt))

            loader = Weights(p, nc, stack, tag, KD * E)
            router = loader.load("router", mats["router"])
            ln = LayerNorm(p, nc, stack, tag, X, consts, xT)
            logitT = [sb(f"logitT{i}", [E, GPS * P]) for i in range(2)]
            logit, prob, hot = (sb(n, [P, G, E]) for n in ("logit", "prob", "hot"))
            top = sb("top", [P, G, 8])
            which = sb("which", [P, G, 8], U32)
            which_f = sb("which_f", [P, G, 8])
            stat = sb("stat", [P, G])
            banks = Banks([stack.enter_context(nc.psum_tensor(f"ps_{i}_{tag}", [P, 512], F32)) for i in range(4)])
            for s in range(SG):
                ln.normalise(s, [])
                ln.turn(s, banks, [])
                bank, free = banks.take((("logitT", s),))
                p.wait("tensor", *[r for k in range(KD) for r in both("xT", tag, s, k)], *free, *router.ready)
                p.split_product(bank[0:E, :], lambda k: part(router, k, 0, E),
                                lambda k: xT.pair(lambda t: t[:, k, s * GPS * P:(s + 1) * GPS * P]), KD,
                                ("logit_ps", s))
                p.wait("scalar", ("logit_ps", s))
                if s >= 2:
                    p.wait("scalar", ("logit_T", s - 2))
                p.activation(logitT[s % 2][:, :], bank[0:E, :], ACT.Copy, ("logitT", s))
                bank, free = banks.take((("logit", s),))
                p.wait("tensor", ("logitT", s), *free)
                for j in range(GPS):
                    p.transpose(bank[:, j * E:(j + 1) * E], logitT[s % 2][:, j * P:(j + 1) * P],
                                consts["ident"][0:E, 0:E], ("logit_T", s) if j == GPS - 1 else None)
                p.wait("scalar", ("logit_T", s))
                p.activation(logit[:, s * GPS:(s + 1) * GPS, :],
                             bank[:, 0:GPS * E].rearrange("p (g e) -> p g e", e=E), ACT.Copy, ("logit", s))
            spread = lambda a: a.unsqueeze(2).to_broadcast([P, G, E])
            p.wait("vector", ("logit", SG - 1))
            p.reduce(stat[:, :], logit[:, :, :], ALU.max, ("route", 0), negate=True)
            p.wait("vector", ("route", 0))
            p.tensor_tensor(logit[:, :, :], logit[:, :, :], spread(stat[:, :]), ALU.add, ("route", 1))
            p.wait("scalar", ("route", 1))
            p.activation(prob[:, :, :], logit[:, :, :], ACT.Exp, ("route_exp",))
            p.wait("vector", ("route_exp",))
            p.reduce(stat[:, :], prob[:, :, :], ALU.add, ("route", 2))
            p.wait("vector", ("route", 2))
            p.reciprocal(stat[:, :], stat[:, :], ("route", 3))
            p.wait("vector", ("route", 3))
            p.tensor_tensor(prob[:, :, :], prob[:, :, :], spread(stat[:, :]), ALU.mult, ("route", 4))
            p.wait("vector", ("route", 4))
            for g in range(G):
                p.do("vector", lambda e, g=g: e.max(top[:, g, :], prob[:, g, :]), ("route_top", g))
            p.wait("vector", ("route_top", G - 1))
            for g in range(G):
                p.do("vector", lambda e, g=g: e.max_index(which[:, g, :], top[:, g, :], prob[:, g, :]),
                     ("route_which", g))
            p.wait("vector", ("route_which", G - 1))
            p.copy(which_f[:, :, 0:2], which[:, :, 0:2], ("route", 5))
            p.tensor_tensor(stat[:, :], top[:, :, 0], top[:, :, 1], ALU.add, ("route", 6))
            p.wait("vector", ("route", 6))
            p.reciprocal(stat[:, :], stat[:, :], ("route", 7))
            p.wait("vector", ("route", 7))
            p.tensor_tensor(top[:, :, 0:2], top[:, :, 0:2], stat[:, :].unsqueeze(2).to_broadcast([P, G, 2]),
                            ALU.mult, ("route", 8))
            p.wait("vector", ("route", 8), ("const_in",))
            number = consts["numbers"][:, :].unsqueeze(1).to_broadcast([P, G, E])
            for n, dst in enumerate((share[:, :, :], hot[:, :, :])):
                p.tensor_tensor(dst, number, spread(which_f[:, :, n]), ALU.is_equal, ("route", 9 + 2 * n))
                p.wait("vector", ("route", 9 + 2 * n))
                p.tensor_tensor(dst, dst, spread(top[:, :, n]), ALU.mult, ("route", 10 + 2 * n))
            p.wait("vector", ("route", 12))
            p.tensor_tensor(share[:, :, :], share[:, :, :], hot[:, :, :], ALU.add, ("share",))
            p.run()

        with ExitStack() as stack:
            def sb(name, shape, dt=F32):
                return stack.enter_context(nc.sbuf_tensor(f"{name}_{tag}", shape, dt))

            WN = KD * HID
            names = ("gate", "up", "down")
            stage = sb("w_stage", [P, 3, WN])
            w = [{n: Split(nc, stack, f"{n}{i}_{tag}", [P, WN]) for n in names} for i in range(2)]
            silu = [sb(f"silu{i}", [P, GPS * P]) for i in range(2)]
            hid32 = [sb(f"hid32{i}", [P, GPS * P]) for i in range(2)]
            hid = [Split(nc, stack, f"hid{i}_{tag}", [P, KH, GPS * P]) for i in range(2)]
            gate_banks, up_banks, y_banks = (
                Banks([stack.enter_context(nc.psum_tensor(f"ps_{n}{i}_{tag}", [P, 512], F32)) for i in range(c)])
                for n, c in (("gate", 2), ("up", 2), ("y", 4)))
            NS = E * SG

            def load(e):
                for i, n in enumerate(names):
                    if e:
                        p.wait("sync", *both(f"w_{n}", e - 1))
                    p.dma(stage[:, i, :], mats[n][e].rearrange("p a b -> p (a b)"), (f"w_{n}_in", e))

            def split_w(e, i):
                n = names[i]
                old = [("y_ps", (e - 1) * SG - 1, GPS - 1)] if e >= 2 else []
                w[e % 2][n].fill(p, stage[:, i, :], lambda t: t[:, :], (f"w_{n}", e), [(f"w_{n}_in", e)], old)

            def gate_up(n, h):
                e, s = n // SG, n % SG
                i = (n * KH + h) % 2
                readers = {"gate": (("silu", n, h),), "up": (("hid32", n, h),)}
                got = {}
                for name, bk in (("gate", gate_banks), ("up", up_banks)):
                    bank, free = bk.take(readers[name])
                    p.wait("tensor", *both(f"w_{name}", e), *free)
                    p.split_product(bank[:, :], lambda k: w[e % 2][name].pair(
                        lambda t: t[:, k * HID + h * P:k * HID + (h + 1) * P]),
                        lambda k: xT.pair(lambda t: t[:, k, s * GPS * P:(s + 1) * GPS * P]), KD, (name + "_ps", n, h))
                    got[name] = bank
                before = ((n * KH + h) - 2) // KH, ((n * KH + h) - 2) % KH
                p.wait("scalar", ("gate_ps", n, h))
                if before[0] >= 0:
                    p.wait("scalar", ("hid32", *before))
                p.activation(silu[i][:, :], got["gate"][:, :], ACT.Silu, ("silu", n, h))
                p.wait("vector", ("silu", n, h), ("up_ps", n, h))
                if before[0] >= 0:
                    p.wait("vector", *both("hid", *before))
                p.tensor_tensor(hid32[i][:, :], got["up"][:, :], silu[i][:, :], ALU.mult, ("hid32", n, h))
                old = [("y_ps", n - 2, GPS - 1)] if n >= 2 else []
                hid[n % 2].fill(p, hid32[i][:, :], lambda t: t[:, h, :], ("hid", n, h), [("hid32", n, h)], old)

            def down(n, j):
                e, s = n // SG, n % SG
                g = s * GPS + j
                bank, free = y_banks.take((("y", n, j),))
                p.wait("tensor", *both("hid", n, KH - 1), *both("w_down", e), *free)
                p.split_product(bank[:, 0:D], lambda k: hid[n % 2].pair(lambda t: t[:, k, j * P:(j + 1) * P]),
                                lambda k: w[e % 2]["down"].pair(lambda t: t[:, k * D:(k + 1) * D]), KH,
                                ("y_ps", n, j))
                p.wait("vector", ("y_ps", n, j))
                if e:
                    p.wait("vector", ("y", n - SG, j))
                p.scalar_tensor_tensor(X[:, g, :], bank[:, 0:D], share[:, g, e:e + 1], X[:, g, :],
                                       ALU.mult, ALU.add, ("y", n, j))

            load(0)
            for i in range(3):
                split_w(0, i)
            load(1)
            for n in range(NS + 1):
                for h in range(KH):
                    if n < NS:
                        gate_up(n, h)
                    if n and h % 2:
                        down(n - 1, h - 1)
                        down(n - 1, h)
                e, s = n // SG + 1, n % SG
                if e < E and 2 <= s < 5:
                    split_w(e, s - 2)
                if s == 6 and e + 1 < E:
                    load(e + 1)
            p.run()


def self_attention_1(p, nc, X, consts, mats):
    tag = "s1"
    with ExitStack() as stack:
        def sb(name, shape, dt=F32):
            return stack.enter_context(nc.sbuf_tensor(f"{name}_{tag}", shape, dt))

        loader = Weights(p, nc, stack, tag, F1 // P * D)
        wqkv = [loader.load(f"qkv{i}", mats["qkv"][i]) for i in range(3)]
        wout = loader.load("out", mats["out"])
        ready_w = [r for m in (*wqkv, wout) for r in m.ready]
        xT = Split(nc, stack, f"xT_{tag}", [P, KD, GPS * P])
        ln = LayerNorm(p, nc, stack, tag, X, consts, xT)
        HB = 512 // D1
        NB = F1 // 512
        turned = [sb(f"turned{i}", [P, HB, D1]) for i in range(2)]
        swapped = [sb(f"swapped{i}", [P, HB, D1]) for i in range(2)]
        rot = [sb(f"rot{i}", [P, HB, D1]) for i in range(2)]
        qT, kT = ([sb(f"{n}{i}", [P, F1 // P, P]) for i in range(2)] for n in ("qT", "kT"))
        v = [sb(f"v{i}", [P, F1]) for i in range(2)]
        t = {n: [sb(f"{n}{i}", [P, H * T]) for i in range(2)] for n in ("sc", "shifted", "prob", "probT")}
        t |= {n: [sb(f"{n}{i}", [P, H]) for i in range(2)] for n in ("neg_max", "sums", "inv")}
        attn = sb("attn", [P, F1])
        attnT = Split(nc, stack, f"attnT_{tag}", [P, F1])
        R = P // D1
        NH = H // R
        ps_score = stack.enter_context(nc.psum_tensor(f"ps_score_{tag}", [P, R, 512], F32))
        ps_out = stack.enter_context(nc.psum_tensor(f"ps_out_{tag}", [P, F1], F32))
        banks = Banks([stack.enter_context(nc.psum_tensor(f"ps_{i}_{tag}", [P, 512], F32)) for i in range(4)])
        t["score"] = lambda g: ps_score[:, :, 0:NH * T].rearrange("p r (n q) -> p r n q", q=T)
        t["score_free"] = lambda g: [("s_masked", tag, g - 1, R - 1)] if g else []
        t["out"] = lambda g: ps_out[:, :].rearrange("p (h d) -> p h d", d=D1)
        t["out_free"] = lambda g: [("s_out", tag, g - 1)] if g else []
        turns = {"n": 0}

        def project(g, i, c):
            s, j = g // GPS, g % GPS
            name = "qkv"[i]
            readers = (("s_v", tag, g, c),) if i == 2 else (("turned", tag, g, i, c), ("swap1", tag, g, i, c))
            bank, free = banks.take(readers)
            p.wait("tensor", *[r for k in range(KD) for r in both("xT", tag, s, k)], *free, *ready_w)
            p.split_product(bank[:, :], lambda k: xT.pair(lambda a: a[:, k, j * P:(j + 1) * P]),
                            lambda k: part(wqkv[i], k, c * 512, (c + 1) * 512), KD, ("s_qkv_ps", tag, g, i, c))
            if i == 2:
                p.wait("scalar", ("s_qkv_ps", tag, g, i, c))
                if g >= 2:
                    p.wait("scalar", ("s_pv", tag, g - 2))
                p.activation(v[g % 2][:, c * 512:(c + 1) * 512], bank[:, :], ACT.Copy, ("s_v", tag, g, c))
                return
            b3 = bank[:, :].rearrange("p (h d) -> p h d", d=D1)
            cos = consts["cos"][:, :].unsqueeze(1).to_broadcast([P, HB, D1])
            e = turns["n"] % 2
            old, turns["n"] = turns.get(e, []), turns["n"] + 1
            p.wait("vector", ("s_qkv_ps", tag, g, i, c), ("const_in",), *old)
            p.tensor_tensor(turned[e][:, :, :], b3, cos, ALU.mult, ("turned", tag, g, i, c))
            for a in range(2):
                sin = consts["sin"][:, a::2].unsqueeze(1).to_broadcast([P, HB, D1 // 2])
                p.tensor_tensor(swapped[e][:, :, a::2], b3[:, :, 1 - a::2], sin, ALU.mult, (f"swap{a}", tag, g, i, c))
            p.wait("gpsimd", ("turned", tag, g, i, c), ("swap1", tag, g, i, c))
            if old:
                p.wait("gpsimd", turns[("T", e)])
            p.tensor_tensor(rot[e][:, :, :], turned[e][:, :, :], swapped[e][:, :, :], ALU.add,
                            ("rot", tag, g, i, c), "gpsimd")
            turns[e] = [("rot", tag, g, i, c)]
            turns[("T", e)] = ("rot_T", tag, g, i, c)
            turns[("src", g, i, c)] = rot[e]

        def turn(g, i, c):
            dst = (qT, kT)[i][g % 2]
            bank, free = banks.take((("s_qkT", tag, g, i, c),))
            src = turns[("src", g, i, c)]
            p.wait("tensor", ("rot", tag, g, i, c), *free)
            for n in range(4):
                p.transpose(bank[:, n * P:(n + 1) * P], src[:, :, :].rearrange("p h d -> p (h d)")[:, n * P:(n + 1) * P],
                            consts["ident"][:, :], ("rot_T", tag, g, i, c) if n == 3 else None)
            p.wait("scalar", ("rot_T", tag, g, i, c))
            if g >= 2:
                p.wait("scalar", ("s_score", tag, g - 2))
            p.activation(dst[:, 4 * c:4 * c + 4, :], bank[:, :].rearrange("p (n q) -> p n q", q=P), ACT.Copy,
                         ("s_qkT", tag, g, i, c))

        def scores(g):
            ready = [("s_qkT", tag, g, 1, NB - 1), ("s_qkT", tag, g, 0, NB - 1)]
            attend(p, tag, g, lambda g: qT[g % 2], lambda g: kT[g % 2], None, D1, D1, t, D1 ** -0.5,
                   consts["causal"][:, :], ready)

        def finish(g):
            p.wait("vector", ("s_pv", tag, g), ("s_inv", tag, g))
            if g:
                p.wait("vector", ("attn_T", tag, g - 1, NB - 1))
            inv = by_head(t["inv"][g % 2][:, :], R)
            p.tensor_tensor(attn[:, :].rearrange("p (n r d) -> p n r d", r=R, d=D1),
                            t["out"](g).rearrange("p (n r) d -> p n r d", r=R),
                            inv.unsqueeze(3).to_broadcast([P, NH, R, D1]), ALU.mult, ("s_out", tag, g))

        def project_out(g):
            for c in range(NB):
                bank, free = banks.take(both("s_attnT", tag, g, c))
                p.wait("tensor", ("s_out", tag, g), *free)
                for n in range(4):
                    p.transpose(bank[:, n * P:(n + 1) * P], attn[:, c * 512 + n * P:c * 512 + (n + 1) * P],
                                consts["ident"][:, :], ("attn_T", tag, g, c) if n == 3 else None)
                old = [("s_o_ps", tag, g - 1)] if g else []
                attnT.fill(p, bank[:, :], lambda a: a[:, c * 512:(c + 1) * 512], ("s_attnT", tag, g, c),
                           [("attn_T", tag, g, c)], old)

        def add_out(g):
            bank, free = banks.take((("s_x", tag, g),))
            p.wait("tensor", *[r for c in range(NB) for r in both("s_attnT", tag, g, c)], *free)
            p.split_product(bank[:, 0:D], lambda k: attnT.pair(lambda a: a[:, k * P:(k + 1) * P]),
                            lambda k: part(wout, k, 0, D), F1 // P, ("s_o_ps", tag, g))
            p.wait("vector", ("s_o_ps", tag, g))
            p.tensor_tensor(X[:, g, :], X[:, g, :], bank[:, 0:D], ALU.add, ("s_x", tag, g))

        for g in range(G + 2):
            if g < G:
                if g % GPS == 0:
                    s = g // GPS
                    ln.normalise(s, [])
                    ln.turn(s, banks, [("s_qkv_ps", tag, g - 1, 2, NB - 1)] if g else [])
                project(g, 0, 0)
                project(g, 0, 1)
            if 1 <= g <= G:
                scores(g - 1)
            if g < G:
                turn(g, 0, 0)
                project(g, 1, 0)
                turn(g, 0, 1)
                project(g, 1, 1)
            if g >= 2:
                project_out(g - 2)
            if g < G:
                project(g, 2, 0)
                turn(g, 1, 0)
            if 1 <= g <= G:
                p.wait("tensor", ("s_v", tag, g - 1, NB - 1))
                weigh_self(p, tag, g - 1, lambda g: v[g % 2], D1, D1, t)
                finish(g - 1)
            if g < G:
                project(g, 2, 1)
                turn(g, 1, 1)
            if g >= 2:
                add_out(g - 2)
        p.run()


def bit_linear(p, nc, X, consts, mats, out):
    tag = "bit"
    with ExitStack() as stack:
        def sb(name, shape, dt=F32):
            return stack.enter_context(nc.sbuf_tensor(f"{name}_{tag}", shape, dt))

        w32 = sb("w32", [P, KD * D])
        row = sb("row", [P, 1])
        scale, inv_scale = sb("scale", [P, 1]), sb("inv_scale", [P, 1])
        wq = sb("wq", [P, KD * D], BF16)
        stats, mv, = sb("stats", [P, G, 6]), sb("mv", [P, G, 2])
        var, rstd, top, inv, back = (sb(n, [P, G]) for n in ("var", "rstd", "top", "inv", "back"))
        xn = [sb(f"xn{i}", [P, D]) for i in range(3)]
        z = [sb(f"z{i}", [P, D]) for i in range(3)]
        zT = [sb(f"zT{i}", [P, D], BF16) for i in range(3)]
        ps_sum = stack.enter_context(nc.psum_tensor(f"ps_sum_{tag}", [P, 512], F32))
        turn_banks, y_banks = (
            Banks([stack.enter_context(nc.psum_tensor(f"ps_{n}{i}_{tag}", [P, 512], F32)) for i in range(2)])
            for n in ("zT", "y"))

        p.dma(w32[:, :], mats["weight"].rearrange("p a b -> p (a b)"), ("w_in", tag))
        p.wait("vector", ("w_in", tag))
        p.reduce(row[:, :], w32[:, :], ALU.add, ("bit_w", 0), apply_absolute_value=True)
        p.wait("tensor", ("bit_w", 0))
        p.matmul(ps_sum[:, 0:1], consts["ones"][:, :], row[:, :], done=("bit_sum",))
        p.wait("vector", ("bit_sum",))
        p.tensor_scalar(scale[:, :], ps_sum[:, 0:1], 1.0 / (D * D), 1e-8, ALU.mult, ALU.add, ("bit_w", 1))
        p.wait("vector", ("bit_w", 1))
        p.reciprocal(inv_scale[:, :], scale[:, :], ("bit_w", 2))
        p.wait("vector", ("bit_w", 2))
        p.tensor_scalar(w32[:, :], w32[:, :], inv_scale[:, 0:1], ROUND, ALU.mult, ALU.add, ("bit_w", 3))
        p.wait("vector", ("bit_w", 3))
        p.tensor_scalar(w32[:, :], w32[:, :], ROUND, 1.0, ALU.subtract, ALU.min, ("bit_w", 4))
        p.wait("vector", ("bit_w", 4))
        p.tensor_scalar(wq[:, :], w32[:, :], -1.0, None, ALU.max, done=("bit_w", 5))

        for g in range(G):
            p.do("vector", lambda e, g=g: e.bn_stats(stats[:, g, :], X[:, g, :]), ("bit_stats", g))
        p.wait("vector", ("bit_stats", G - 1))
        for g in range(G):
            p.do("vector", lambda e, g=g: e.bn_aggr(mv[:, g, :], stats[:, g, :]), ("bit_aggr", g))
        p.wait("vector", ("bit_aggr", G - 1))
        p.tensor_scalar(var[:, :], mv[:, :, 1], LN_EPS, None, ALU.add, done=("bit_var",))
        p.wait("gpsimd", ("bit_var",))
        p.tensor_tensor(rstd[:, :], var[:, :], consts["minus_half"][:, 0:1].to_broadcast([P, G]), ALU.pow,
                        ("bit_rstd",), "gpsimd")
        p.wait("vector", ("bit_rstd",))

        def quantise(g):
            i = g % 3
            if g >= 3:
                p.wait("vector", ("bit_z", g - 3), ("bit_T", g - 3))
            p.tensor_scalar(xn[i][:, :], X[:, g, :], mv[:, g, 0:1], rstd[:, g:g + 1], ALU.subtract, ALU.mult,
                            ("bit_xn", g))
            p.wait("vector", ("bit_xn", g))
            p.reduce(top[:, g:g + 1], xn[i][:, :], ALU.max, ("bit_top", g), apply_absolute_value=True)
            p.wait("vector", ("bit_top", g))
            p.tensor_scalar(top[:, g:g + 1], top[:, g:g + 1], 1e-8, None, ALU.add, done=("bit_a", g))
            p.wait("vector", ("bit_a", g))
            p.reciprocal(inv[:, g:g + 1], top[:, g:g + 1], ("bit_inv", g))
            p.tensor_scalar(back[:, g:g + 1], top[:, g:g + 1], scale[:, 0:1], 1.0 / 127.0, ALU.mult, ALU.mult,
                            ("bit_back", g))
            p.wait("vector", ("bit_inv", g))
            p.tensor_scalar(z[i][:, :], xn[i][:, :], inv[:, g:g + 1], 127.0, ALU.mult, ALU.mult, ("bit_z0", g))
            p.wait("vector", ("bit_z0", g))
            p.tensor_scalar(z[i][:, :], z[i][:, :], 127.0, -128.0, ALU.min, ALU.max, ("bit_z1", g))
            p.wait("vector", ("bit_z1", g))
            p.tensor_scalar(z[i][:, :], z[i][:, :], ROUND, ROUND, ALU.add, ALU.subtract, ("bit_z", g))

        def product(g):
            i = g % 3
            bank, free = turn_banks.take((("bit_zT", g),))
            p.wait("tensor", ("bit_z", g), *free)
            for k in range(KD):
                p.transpose(bank[:, k * P:(k + 1) * P], z[i][:, k * P:(k + 1) * P], consts["ident"][:, :],
                            ("bit_T", g) if k == KD - 1 else None)
            p.wait("scalar", ("bit_T", g))
            if g >= 3:
                p.wait("scalar", ("bit_y_ps", g - 3))
            p.activation(zT[i][:, :], bank[:, 0:D], ACT.Copy, ("bit_zT", g))
            bank, free = y_banks.take((("bit_x", g),))
            p.wait("tensor", ("bit_zT", g), ("bit_w", 5), *free)
            for k in range(KD):
                p.matmul(bank[:, 0:D], zT[i][:, k * P:(k + 1) * P], wq[:, k * D:(k + 1) * D],
                         start=k == 0, stop=k == KD - 1, done=("bit_y_ps", g) if k == KD - 1 else None)
            p.wait("vector", ("bit_y_ps", g), ("bit_back", g))
            p.scalar_tensor_tensor(X[:, g, :], bank[:, 0:D], back[:, g:g + 1], X[:, g, :], ALU.mult, ALU.add,
                                   ("bit_x", g))
            if g % GPS == GPS - 1:
                s = g // GPS
                p.wait("sync", ("bit_x", g))
                p.dma(out[:, s * GPS:(s + 1) * GPS, :], X[:, s * GPS:(s + 1) * GPS, :], ("stored", s))

        for g in range(G + 1):
            if g < G:
                quantise(g)
            if g:
                product(g - 1)
        p.wait("sync", ("stored", SG - 1))
        p.run()


def build(nc, a, out, phases=(1, 2, 3, 4, 5, 6)):
    with ExitStack() as stack:
        def sb(name, shape):
            return stack.enter_context(nc.sbuf_tensor(name, shape, F32))

        p = Program(nc, stack)
        X = sb("X", [P, G, D])
        consts = {n: sb("const_" + n, list(a["c_" + n].shape)) for n in
                  ("ident", "head_rows", "causal", "cos", "sin", "numbers", "ones", "minus_half")}
        biases = {n: sb("bias_" + n, [P, KD] if n != "o" else [P, D]) for n in "qkvo"}

        for n, t in consts.items():
            p.dma(t[:, :], a["c_" + n], ("const", n))
        for n, t in biases.items():
            src = a["b_" + n]
            p.dma(t[:, :], src.partition_broadcast(P) if n == "o" else src, ("const", "bias_" + n))
        p.done[("const_in",)] = ("const", p.count["const"])
        for s in range(SG):
            p.dma(X[:, s * GPS:(s + 1) * GPS, :], a["x"][:, s * GPS:(s + 1) * GPS, :], (f"x_in{s}",))
        for e in ("tensor", "vector", "scalar", "gpsimd"):
            p.wait(e, ("const_in",))

        if 1 in phases:
            cross_attention(p, nc, "x0", X, a["ctx"], consts, {n: a["x0_" + n] for n in "qkvo"}, biases,
                            lambda s: (f"x_in{s}",))
        else:
            for e in ("tensor", "vector", "scalar", "gpsimd"):
                p.wait(e, *[(f"x_in{s}",) for s in range(SG)])
        if 2 in phases:
            self_attention_0(p, nc, X, consts, {n: a["s0_" + n] for n in "qkv"})
        if 3 in phases:
            experts(p, nc, X, consts, {n: a["moe_" + n] for n in ("router", "gate", "up", "down")})
        if 4 in phases:
            cross_attention(p, nc, "x1", X, a["ctx"], consts, {n: a["x1_" + n] for n in "qo"}, None,
                            lambda s: (f"x_in{s}",))
        if 5 in phases:
            self_attention_1(p, nc, X, consts, {n: a["s1_" + n] for n in ("qkv", "out")})
        if 6 in phases:
            bit_linear(p, nc, X, consts, {"weight": a["bit_weight"]}, out)
        else:
            p.dma(out, X[:, :, :], ("stored", 0))
            p.wait("sync", ("stored", 0))
            p.run()


def tables():
    rows = np.arange(P)
    position = rows % T
    freqs = 1.0 / 10000.0 ** (np.arange(0, D1, 2) / D1)
    angle = (np.arange(T)[:, None].astype(np.float32) * freqs[None, :].astype(np.float32))[position]
    sin = np.repeat(np.sin(angle), 2, axis=1)
    sin[:, 0::2] *= -1.0
    big = np.finfo(np.float32).max
    out = {
        "c_ident": np.eye(P),
        "c_head_rows": (rows[:, None] // XD == np.arange(HPH)[None, :]),
        "c_causal": np.where(position[:, None] >= np.arange(T)[None, :], big, NEG_INF),
        "c_cos": np.repeat(np.cos(angle), 2, axis=1),
        "c_sin": sin,
        "c_numbers": np.tile(np.arange(E), (P, 1)),
        "c_ones": np.ones((P, P)),
        "c_minus_half": np.full((P, GPS), -0.5),
    }
    return {n: np.ascontiguousarray(t, dtype=np.float32) for n, t in out.items()}


def lay_out(i):
    def pieces(m):
        return m.reshape(m.shape[0] // P, P, m.shape[1]).transpose(1, 0, 2)

    def padded(m):
        wide = np.zeros((D, H, T), m.dtype)
        wide[:, :, :XD] = m.reshape(D, H, XD)
        return wide.reshape(D, H * T)

    a = {
        "x": i["x"].reshape(G, P, D).transpose(1, 0, 2),
        "ctx": i["ctx_1024"].transpose(0, 2, 1).reshape(G, BPG, KD, P, S).transpose(0, 3, 2, 1, 4),
        "x0_q": pieces(i["L0_xattn_Wq"].T), "x0_k": pieces(i["L0_xattn_Wk"].T),
        "x0_v": pieces(i["L0_xattn_Wv"].T), "x0_o": pieces(i["L0_xattn_Wo"].T),
        "b_q": i["L0_xattn_bq"].reshape(KD, P).T, "b_k": i["L0_xattn_bk"].reshape(KD, P).T,
        "b_v": i["L0_xattn_bv"].reshape(KD, P).T, "b_o": i["L0_xattn_bo"],
        "s0_q": pieces(padded(i["L0_attn_w_Q"])), "s0_k": pieces(padded(i["L0_attn_w_K"])),
        "s0_v": pieces(i["L0_attn_w_V"]),
        "moe_router": pieces(i["L0_ffn_router_w"].T),
        "moe_gate": np.stack([pieces(m.T) for m in i["L0_ffn_w_gate"]]),
        "moe_up": np.stack([pieces(m.T) for m in i["L0_ffn_w_up"]]),
        "moe_down": np.stack([pieces(m.T) for m in i["L0_ffn_w_down"]]),
        "x1_q": pieces(i["L1_xattn_Wq"].T), "x1_o": pieces(i["L1_xattn_Wo"].T),
        "s1_qkv": np.stack([pieces(m) for m in np.split(i["L1_attn_W_qkv"], 3, axis=1)]),
        "s1_out": pieces(i["L1_attn_W_out"]),
        "bit_weight": pieces(i["L1_ffn_weight"].T),
    }
    return {n: np.ascontiguousarray(t) for n, t in a.items()}


def kernel(**inputs):
    import concourse.bacc as _bacc
    from concourse.bass_utils import run_bass_kernel_spmd as _run

    nc = _bacc.Bacc("TRN2", target_bir_lowering=False, num_devices=1)
    arrays = {**lay_out({n: np.asarray(t) for n, t in inputs.items()}), **tables()}
    aps = {n: nc.dram_tensor(n, t.shape, F32, kind="ExternalInput").ap() for n, t in arrays.items()}
    out = nc.dram_tensor("out", (P, G, D), F32, kind="ExternalOutput").ap()
    build(nc, aps, out)
    r = _run(nc, [arrays], core_ids=[0])
    return r.results[0]["out"].transpose(1, 0, 2).reshape(B, T, D)
```

```python
from contextlib import ExitStack

import numpy as np

import concourse.bass as bass
from concourse import mybir

F32 = mybir.dt.float32
F32R = mybir.dt.float32r
BF16 = mybir.dt.bfloat16
U32 = mybir.dt.uint32
ALU = mybir.AluOpType
ACT = mybir.ActivationFunctionType
AX_X = mybir.AxisListType.X

P = 128
B, T, D = 128, 32, 256
S = 257
S_EVEN = S + 1
KD = D // P
H = 16
BPG = P // T
G = B * T // P
GPS = 4
SG = G // GPS
BPS = BPG * GPS
HPH = H // KD
XD = D // H
HG = 4
HPG = H // HG
CHUNKS = S // P
assert S == CHUNKS * P + 1
E, HID = 8, 512
KH = HID // P
D1 = 64
F1 = H * D1
LN_EPS = 1e-5
NEG_INF = -1e9
ROUND = 1.5 * 2.0 ** 23


class Program:

    def __init__(self, nc, stack):
        self.nc, self.stack = nc, stack
        self.sems, self.count, self.done = {}, {}, {}
        self.queues = {e: [] for e in ("tensor", "vector", "scalar", "gpsimd", "sync")}
        self.reached = {e: {} for e in self.queues}

    def do(self, engine, emit, done=None, inc=1):
        sem = None
        if done is not None:
            kind = done[0]
            if kind not in self.sems:
                self.sems[kind] = self.stack.enter_context(self.nc.semaphore(kind))
                self.count[kind] = 0
            self.count[kind] += inc
            assert done not in self.done, done
            self.done[done] = (kind, self.count[kind])
            sem = self.sems[kind]
        self.queues[engine].append((emit, sem, inc))

    def wait(self, engine, *names):
        self.queues[engine].append((None, names, 0))

    def _emit(self, engine, eng):
        reached = self.reached[engine]
        for emit, sem, inc in self.queues[engine]:
            if emit is None:
                for name in sem:
                    kind, value = self.done[name]
                    if reached.get(kind, 0) < value:
                        eng.wait_ge(self.sems[kind], value)
                        reached[kind] = value
                continue
            ins = emit(eng)
            if sem is not None:
                ins.then_inc(sem, inc)
        self.queues[engine] = []

    def run(self):
        with self.nc.Block() as block:
            @block.sync
            def _(eng):
                self._emit("sync", eng)

            @block.gpsimd
            def _(eng):
                self._emit("gpsimd", eng)

            @block.scalar
            def _(eng):
                self._emit("scalar", eng)

            @block.vector
            def _(eng):
                self._emit("vector", eng)

            @block.tensor
            def _(eng):
                self._emit("tensor", eng)

    def dma(self, out, in_, done):
        self.do("sync", lambda e: e.dma_start(out, in_), done, 16)

    def matmul(self, out, lhsT, rhs, start=True, stop=True, done=None):
        self.do("tensor", lambda e: e.matmul(out, lhsT, rhs, start=start, stop=stop), done)

    def transpose(self, out, in_, ident, done=None):
        self.do("tensor", lambda e: e.transpose(out, in_, ident), done)

    def activation(self, out, in_, func, done=None, **kw):
        self.do("scalar", lambda e: e.activation(out, in_, func, **kw), done)

    def tensor_tensor(self, out, in0, in1, op, done=None, engine="vector"):
        self.do(engine, lambda e: e.tensor_tensor(out, in0, in1, op), done)

    def tensor_scalar(self, out, in0, s1, s2, op0, op1=None, done=None):
        if op1 is None:
            self.do("vector", lambda e: e.tensor_scalar(out, in0, s1, s2, op0), done)
        else:
            self.do("vector", lambda e: e.tensor_scalar(out, in0, s1, s2, op0, op1), done)

    def scalar_tensor_tensor(self, out, in0, scalar, in1, op0, op1, done=None):
        self.do("vector", lambda e: e.scalar_tensor_tensor(out=out, in0=in0, scalar=scalar, in1=in1,
                                                           op0=op0, op1=op1), done)

    def reduce(self, out, in_, op, done=None, **kw):
        self.do("vector", lambda e: e.tensor_reduce(out, in_, AX_X, op, **kw), done)

    def reciprocal(self, out, in_, done=None):
        self.do("vector", lambda e: e.reciprocal(out, in_), done)

    def copy(self, out, in_, done=None, engine="vector"):
        self.do(engine, lambda e: e.tensor_copy(out, in_), done)

    def memset(self, out, value, done=None, engine="vector"):
        self.do(engine, lambda e: e.memset(out, value), done)

    def split_product(self, out, lhs, rhs, pieces, done=None):
        steps = []
        for k in range(pieces):
            (lh, ll), (rh, rl) = lhs(k), rhs(k)
            steps += [(lh, rh), (lh, rl), (ll, rh)]
        for n, (a, b) in enumerate(steps):
            last = n == len(steps) - 1
            self.matmul(out, a, b, start=n == 0, stop=last, done=done if last else None)


class Split:

    def __init__(self, nc, stack, name, shape):
        self.hi = stack.enter_context(nc.sbuf_tensor(name + "_hi", shape, F32R))
        self.lo = stack.enter_context(nc.sbuf_tensor(name + "_lo", shape, F32R))

    def fill(self, p, src, at, name, ready, free=(), bias=None, lo_engine="vector"):
        hi, lo = at(self.hi), at(self.lo)
        p.wait("scalar", *ready, *free)
        if bias is None:
            p.activation(hi, src, ACT.Copy, done=("hi_" + name[0], *name[1:]))
        else:
            p.activation(hi, src, ACT.Identity, bias=bias, done=("hi_" + name[0], *name[1:]))
        p.wait(lo_engine, *ready, *free, ("hi_" + name[0], *name[1:]))
        if bias is None:
            p.tensor_tensor(lo, src, hi.bitcast(F32), ALU.subtract, ("lo_" + name[0], *name[1:]), lo_engine)
        else:
            p.scalar_tensor_tensor(lo, src, bias, hi.bitcast(F32), ALU.add, ALU.subtract,
                                   done=("lo_" + name[0], *name[1:]))

    def pair(self, at):
        return at(self.hi), at(self.lo)


def both(kind, *rest):
    return ("hi_" + kind, *rest), ("lo_" + kind, *rest)


class Banks:

    def __init__(self, tiles):
        self.tiles, self.readers, self.n = tiles, [()] * len(tiles), 0

    def take(self, readers):
        slot = self.n % len(self.tiles)
        self.n += 1
        free, self.readers[slot] = self.readers[slot], readers
        return self.tiles[slot], free


class Weights:

    def __init__(self, p, nc, stack, tag, columns):
        self.p, self.nc, self.stack, self.tag = p, nc, stack, tag
        self.stage = stack.enter_context(nc.sbuf_tensor(f"stage_{tag}", [P, columns], F32))
        self.before = ()

    def load(self, name, dram):
        shape = list(dram.shape)
        n = int(np.prod(shape[1:]))
        w = Split(self.nc, self.stack, f"w_{name}_{self.tag}", [P, n])
        self.p.wait("sync", *self.before)
        self.p.dma(self.stage[:, 0:n], dram.rearrange("p a b -> p (a b)"), ("w_in", self.tag, name))
        w.fill(self.p, self.stage[:, 0:n], lambda t: t[:, :], ("w", self.tag, name),
               [("w_in", self.tag, name)])
        self.before = both("w", self.tag, name)
        w.ready = self.before
        w.width = shape[2]
        return w


def part(w, k, c0, c1):
    return w.pair(lambda t: t[:, k * w.width + c0:k * w.width + c1])


class LayerNorm:

    def __init__(self, p, nc, stack, tag, X, consts, dest):
        self.p, self.tag, self.X, self.consts, self.dest = p, tag, X, consts, dest
        t = lambda n, s: stack.enter_context(nc.sbuf_tensor(f"ln_{n}_{tag}", s, F32))
        self.stats = t("stats", [P, GPS, 6])
        self.mv = t("mean_var", [P, GPS, 2])
        self.var = t("var", [P, GPS])
        self.rstd = t("rstd", [P, GPS])
        self.xn = t("xn", [P, GPS, D])

    def normalise(self, s, ready):
        p, tag = self.p, self.tag
        p.wait("vector", *ready)
        for j in range(GPS):
            src = self.X[:, GPS * s + j, :]
            p.do("vector", lambda e, j=j, src=src: e.bn_stats(self.stats[:, j, :], src), ("ln_stats", tag, s, j))
            p.wait("vector", ("ln_stats", tag, s, j))
            p.do("vector", lambda e, j=j: e.bn_aggr(self.mv[:, j, :], self.stats[:, j, :]), ("ln_aggr", tag, s, j))
        p.wait("vector", ("ln_aggr", tag, s, GPS - 1))
        p.tensor_scalar(self.var[:, :], self.mv[:, :, 1], LN_EPS, None, ALU.add, done=("ln_var", tag, s))
        p.wait("gpsimd", ("ln_var", tag, s))
        p.tensor_tensor(self.rstd[:, :], self.var[:, :], self.consts["minus_half"][:, :], ALU.pow,
                        done=("ln_rstd", tag, s), engine="gpsimd")
        p.wait("vector", ("ln_rstd", tag, s))
        if s:
            p.wait("vector", *[("ln_T", tag, s - 1, k) for k in range(KD)])
        for j in range(GPS):
            p.tensor_scalar(self.xn[:, j, :], self.X[:, GPS * s + j, :], self.mv[:, j, 0:1],
                            self.rstd[:, j:j + 1], ALU.subtract, ALU.mult, done=("ln_xn", tag, s, j))

    def turn(self, s, banks, free):
        p, tag = self.p, self.tag
        for k in range(KD):
            bank, bank_free = banks.take(both("xT", tag, s, k))
            p.wait("tensor", ("ln_xn", tag, s, GPS - 1), *bank_free)
            for j in range(GPS):
                p.transpose(bank[:, j * P:(j + 1) * P], self.xn[:, j, k * P:(k + 1) * P],
                            self.consts["ident"][:, :], ("ln_T", tag, s, k) if j == GPS - 1 else None)
            self.dest.fill(p, bank[:, :], lambda t, k=k: self.at(t, s, k), ("xT", tag, s, k),
                           [("ln_T", tag, s, k)], free)

    def at(self, t, s, k):
        return t[:, k, :] if t.shape[2] == GPS * P else t[:, k, s * GPS * P:(s + 1) * GPS * P]


def cross_attention(p, nc, tag, X, ctx, consts, mats, biases, x_ready):
    with ExitStack() as stack:
        def sb(name, shape, dt=F32):
            return stack.enter_context(nc.sbuf_tensor(f"{name}_{tag}", shape, dt))

        def split(name, shape):
            return Split(nc, stack, f"{name}_{tag}", shape)

        loader = Weights(p, nc, stack, tag, KD * D)
        w = {n: loader.load(n, mats[n]) for n in ("q", "k", "v", "o") if n in mats}
        w.setdefault("k", w["q"])
        w.setdefault("v", w["q"])
        all_weights = [r for m in w.values() for r in m.ready]

        xT = split("xT", [P, KD, GPS * P])
        ln = LayerNorm(p, nc, stack, tag, X, consts, xT)
        q32 = sb("q32", [P, GPS * P])
        qT = [split(f"qT{i}", [P, KD, GPS * P]) for i in range(2)]
        q_diag = [split(f"q_diag{i}", [P, KD, HPH * T]) for i in range(2)]
        ctx_in = [sb(f"ctx_in{i}", [P, KD, BPG, S]) for i in range(2)]
        ctxT = [split(f"ctxT{i}", [P, KD, S_EVEN]) for i in range(3)]
        kT = [split(f"kT{i}", [P, KD, S_EVEN]) for i in range(2)]
        v = [split(f"v{i}", [P, CHUNKS, D]) for i in range(3)]
        neg_max = [sb(f"neg_max{i}", [P, HG]) for i in range(2)]
        sums = [sb(f"sums{i}", [P, HG]) for i in range(2)]
        inv = [sb(f"inv{i}", [P, HG]) for i in range(2)]
        prob = [sb(f"prob{i}", [P, HG, S]) for i in range(3)]
        probT = [split(f"probT{i}", [P, CHUNKS, HG * P]) for i in range(2)]
        masked = sb("masked", [P, KD, HPH, T])
        ctx_last = split("ctx_last", [P, KD, BPG])
        v_row = sb("v_row", [BPG, D])
        v_last = sb("v_last", [P, KD, BPG])
        p_last = sb("p_last", [P, HG, BPG])
        last_spread = sb("last_spread", [P, HG * BPG, T])
        last_part = sb("last_part", [P, KD, BPG, T])
        attn32 = [sb(f"attn32{i}", [P, KD, P]) for i in range(2)]
        attnT = split("attnT", [P, KD, P])

        ps_score = stack.enter_context(nc.psum_tensor(f"ps_score_{tag}", [P, HG, 512], F32))
        turn_banks = Banks([stack.enter_context(nc.psum_tensor(f"ps_pT{i}_{tag}", [P, 512], F32))
                             for i in range(2)])
        banks = Banks([stack.enter_context(nc.psum_tensor(f"ps_{i}_{tag}", [P, 512], F32)) for i in range(2)])

        for i in range(3):
            for t in (ctxT[i].hi, ctxT[i].lo):
                p.memset(t[:, :, S:S_EVEN].bitcast(F32), 0.0, ("pad", tag, i, t.name))
        pads = [("pad", tag, i, t.name) for i in range(3) for t in (ctxT[i].hi, ctxT[i].lo)]
        bias_ready = []
        if biases:
            bq4 = sb("bq4", [P, KD])
            p.wait("vector", ("const_in",))
            p.tensor_scalar(bq4[:, :], biases["q"][:, :], XD ** -0.5, None, ALU.mult, done=("bq4", tag))
            bias_ready = [("bq4", tag)]

        def load_ctx(g):
            if g >= 2:
                p.wait("sync", *both("ctx", tag, (g - 1) * BPG - 1), *both("ctx_last", tag, g - 2))
            p.dma(ctx_in[g % 2][:, :, :, :], ctx[g], (f"ctx_in{g % 2}", tag, g))

        def split_ctx(b):
            g, j = b // BPG, b % BPG
            free = [("k_ps", tag, b - 3, 1), ("v_ps", tag, b - 3)] if b >= 3 else []
            ctxT[b % 3].fill(p, ctx_in[g % 2][:, :, j, :], lambda t: t[:, :, 0:S], ("ctx", tag, b),
                             [(f"ctx_in{g % 2}", tag, g)], free, lo_engine="gpsimd")

        def project_k(b, m):
            bank, free = banks.take(both("k", tag, b, m))
            p.wait("tensor", *both("ctx", tag, b), *free, *all_weights, *pads)
            p.split_product(bank[:, 0:S_EVEN], lambda k: part(w["k"], k, m * P, (m + 1) * P),
                            lambda k: ctxT[b % 3].pair(lambda t: t[:, k, :]), KD, ("k_ps", tag, b, m))
            old = [("score", tag, b - 2, HG - 1)] if b >= 2 else []
            kT[b % 2].fill(p, bank[:, 0:S_EVEN], lambda t: t[:, m, :], ("k", tag, b, m),
                           [("k_ps", tag, b, m)], old, biases["k"][:, m:m + 1] if biases else None)

        def project_v(b):
            bank, free = banks.take(both("v", tag, b))
            p.wait("tensor", *both("ctx", tag, b), *free)
            for c in range(CHUNKS):
                p.split_product(bank[:, c * D:(c + 1) * D],
                                lambda k: ctxT[b % 3].pair(lambda t: t[:, k, c * P:(c + 1) * P]),
                                lambda k: part(w["v"], k, 0, D), KD,
                                ("v_ps", tag, b) if c == CHUNKS - 1 else None)
            old = [("pv", tag, b - 3)] if b >= 3 else []
            v[b % 3].fill(p, bank[:, :].rearrange("p (c d) -> p c d", d=D), lambda t: t[:, :, :], ("v", tag, b),
                          [("v_ps", tag, b)], old)

        def split_last(g):
            old = [("last_v_ps", tag, g - 1)] if g else []
            ctx_last.fill(p, ctx_in[g % 2][:, :, :, S - 1], lambda t: t[:, :, :], ("ctx_last", tag, g),
                          [(f"ctx_in{g % 2}", tag, g)], old, lo_engine="gpsimd")

        def project_last(g):
            bank, free = turn_banks.take((("v_row", tag, g),))
            p.wait("tensor", *both("ctx_last", tag, g), *free)
            p.split_product(bank[0:BPG, 0:D], lambda k: ctx_last.pair(lambda t: t[:, k, :]),
                            lambda k: part(w["v"], k, 0, D), KD, ("last_v_ps", tag, g))
            p.wait("scalar", ("last_v_ps", tag, g))
            if g:
                p.wait("scalar", ("v_last_T", tag, g - 1))
            p.activation(v_row[:, :], bank[0:BPG, 0:D], ACT.Copy, ("v_row", tag, g))

        def turn_last(g):
            bank, free = turn_banks.take((("v_last", tag, g),))
            p.wait("tensor", ("v_row", tag, g), *free)
            for m in range(KD):
                p.transpose(bank[:, m * BPG:(m + 1) * BPG], v_row[:, m * P:(m + 1) * P],
                            consts["ident"][0:BPG, 0:BPG], ("v_last_T", tag, g) if m == KD - 1 else None)
            p.wait("scalar", ("v_last_T", tag, g))
            if g:
                p.wait("scalar", ("last_part", tag, g - 1))
            p.activation(v_last[:, :, :], bank[:, 0:KD * BPG].rearrange("p (m b) -> p m b", b=BPG), ACT.Copy,
                         ("v_last", tag, g))

        def keep_last(b):
            g, j = b // BPG, b % BPG
            p.wait("gpsimd", ("prob", tag, b))
            if g:
                p.wait("gpsimd", ("last_spread", tag, g - 1))
            p.copy(p_last[:, :, j], prob[b % 3][:, :, S - 1], ("p_last", tag, b), "gpsimd")

        def spread_last(g):
            shape = [P, HG * BPG, T]
            p.wait("gpsimd", ("p_last", tag, g * BPG + BPG - 1))
            if g:
                p.wait("gpsimd", ("last_ps", tag, g - 1))
            p.tensor_tensor(last_spread[:, :, :], p_last[:, :, :].rearrange("p h b -> p (h b)").unsqueeze(2).to_broadcast(shape),
                            consts["same_query"][:, :].unsqueeze(1).to_broadcast(shape), ALU.mult,
                            ("last_spread", tag, g), "gpsimd")

        def add_last(g):
            bank, free = turn_banks.take((("last_part", tag, g),))
            p.wait("tensor", ("last_spread", tag, g), *free)
            for m in range(KD):
                for n in range(HG // KD):
                    hg = m * (HG // KD) + n
                    last = n == HG // KD - 1
                    p.matmul(bank[:, m * P:(m + 1) * P], consts["head_sum"][:, n * P:(n + 1) * P],
                             last_spread[:, hg * BPG:(hg + 1) * BPG, :], start=n == 0, stop=last,
                             done=("last_ps", tag, g) if last and m == KD - 1 else None)
            shape = [P, KD, BPG, T]
            p.wait("vector", ("last_ps", tag, g), ("v_last", tag, g))
            p.tensor_tensor(last_part[:, :, :, :], bank[:, 0:KD * P].rearrange("p (m b q) -> p m b q", b=BPG, q=T),
                            v_last[:, :, :].unsqueeze(3).to_broadcast(shape), ALU.mult, ("last_part", tag, g))
            p.wait("vector", ("last_part", tag, g), ("attn32", tag, g * BPG + BPG - 1))
            whole = attn32[g % 2][:, :, :].rearrange("p m n -> p (m n)")
            p.tensor_tensor(whole, whole, last_part[:, :, :, :].rearrange("p m b q -> p (m b q)"), ALU.add,
                            ("attn_sum", tag, g))

        def project_q(s):
            for m in range(KD):
                bank, free = turn_banks.take((("q32", tag, s, m),))
                p.wait("tensor", *[r for k in range(KD) for r in both("xT", tag, s, k)], *free, *all_weights)
                p.split_product(bank[:, :], lambda k: part(w["q"], k, m * P, (m + 1) * P),
                                lambda k: xT.pair(lambda t: t[:, k, :]), KD, ("q_ps", tag, s, m))
                p.wait("vector", ("q_ps", tag, s, m), *bias_ready)
                if (s, m) != (0, 0):
                    p.wait("vector", *both("q", tag, *((s, 0) if m else (s - 1, 1))))
                p.tensor_scalar(q32[:, :], bank[:, :], XD ** -0.5, bq4[:, m:m + 1] if biases else 0.0,
                                ALU.mult, ALU.add, done=("q32", tag, s, m))
                old = [("q_diag_lo", tag, (s - 1) * BPS - 1)] if s >= 2 else []
                qT[s % 2].fill(p, q32[:, :], lambda t: t[:, m, :], ("q", tag, s, m), [("q32", tag, s, m)], old)

        def spread_q(b):
            s, j = b // BPS, b % BPS
            p.wait("gpsimd", *[r for m in range(KD) for r in both("q", tag, s, m)], ("const_in",))
            if b >= 2:
                p.wait("gpsimd", ("score", tag, b - 2, HG - 1))
            shape = [P, KD, HPH, T]
            mask = consts["head_rows"][:, :].unsqueeze(1).unsqueeze(3).to_broadcast(shape)
            for name, src, dst in (("q_diag_hi", qT[s % 2].hi, q_diag[b % 2].hi),
                                   ("q_diag_lo", qT[s % 2].lo, q_diag[b % 2].lo)):
                src = src[:, :, j * T:(j + 1) * T].bitcast(F32).unsqueeze(2).to_broadcast(shape)
                p.tensor_tensor(dst[:, :, :].rearrange("p m (h q) -> p m h q", q=T), src, mask, ALU.mult,
                                done=(name, tag, b), engine="gpsimd")

        def scores(b):
            for hg in range(HG):
                m, c0 = hg // 2, hg % 2 * P
                p.wait("tensor", ("q_diag_lo", tag, b), *both("k", tag, b, m))
                if b:
                    p.wait("tensor", ("exp", tag, b - 1, hg))
                p.split_product(ps_score[:, hg, 0:S_EVEN], lambda k: q_diag[b % 2].pair(lambda t: t[:, m, c0:c0 + P]),
                                lambda k: kT[b % 2].pair(lambda t: t[:, m, :]), 1, ("score", tag, b, hg))

        def find_max(b, n):
            p.wait("vector", ("score", tag, b, 2 * n + 1))
            if b >= 2:
                p.wait("vector", ("exp", tag, b - 2, HG - 1))
            p.reduce(neg_max[b % 2][:, 2 * n:2 * n + 2], ps_score[:, 2 * n:2 * n + 2, 0:S], ALU.max,
                     ("neg_max", tag, b, n), negate=True)

        def exponentials(b, n):
            if b >= 2:
                p.wait("scalar", ("inv", tag, b - 2))
            if b >= 3:
                p.wait("scalar", ("prob_T", tag, b - 3, CHUNKS - 1), ("p_last", tag, b - 3))
            p.wait("scalar", ("neg_max", tag, b, n))
            for hg in (2 * n, 2 * n + 1):
                p.activation(prob[b % 3][:, hg, :], ps_score[:, hg, 0:S], ACT.Exp, ("exp", tag, b, hg),
                             bias=neg_max[b % 2][:, hg:hg + 1], accum_out=sums[b % 2][:, hg:hg + 1])

        def normalise(b):
            p.wait("vector", ("exp", tag, b, HG - 1))
            if b >= 2:
                p.wait("vector", ("prob", tag, b - 2))
            p.reciprocal(inv[b % 2][:, :], sums[b % 2][:, :], ("inv", tag, b))
            p.wait("gpsimd", ("inv", tag, b))
            t = prob[b % 3][:, :, :]
            p.tensor_tensor(t, t, inv[b % 2][:, :].unsqueeze(2).to_broadcast([P, HG, S]), ALU.mult,
                            ("prob", tag, b), "gpsimd")

        def turn_prob(b, c):
            bank, free = turn_banks.take(both("pT", tag, b, c))
            p.wait("tensor", ("prob", tag, b), *free)
            for hg in range(HG):
                p.transpose(bank[:, hg * P:(hg + 1) * P], prob[b % 3][:, hg, c * P:(c + 1) * P],
                            consts["ident"][:, :], ("prob_T", tag, b, c) if hg == HG - 1 else None)
            old = [("pv", tag, b - 2)] if b >= 2 else []
            probT[b % 2].fill(p, bank[:, :], lambda t: t[:, c, :], ("pT", tag, b, c),
                              [("prob_T", tag, b, c)], old)

        def weigh_v(b):
            g, j = b // BPG, b % BPG
            bank, free = banks.take((("masked", tag, b),))
            p.wait("tensor", *free, *[r for c in range(CHUNKS) for r in both("pT", tag, b, c)],
                   *both("v", tag, b))
            for m in range(KD):
                cols = lambda t, c: t[:, c, m * P:(m + 1) * P]
                rows = lambda t, c: t[:, c, m * HPH * T:(m + 1) * HPH * T]
                p.split_product(bank[:, m * HPH * T:(m + 1) * HPH * T], lambda c: v[b % 3].pair(lambda t: cols(t, c)),
                                lambda c: probT[b % 2].pair(lambda t: rows(t, c)), CHUNKS,
                                ("pv", tag, b) if m == KD - 1 else None)
            shape = [P, KD, HPH, T]
            p.wait("vector", ("pv", tag, b), ("const_in",))
            if b:
                p.wait("vector", ("attn32", tag, b - 1))
            p.tensor_tensor(masked[:, :, :, :], bank[:, :].rearrange("p (m h q) -> p m h q", m=KD, q=T),
                            consts["head_rows"][:, :].unsqueeze(1).unsqueeze(3).to_broadcast(shape), ALU.mult,
                            done=("masked", tag, b))
            p.wait("vector", ("masked", tag, b))
            if g >= 2:
                p.wait("vector", *both("attn", tag, g - 2))
            p.reduce(attn32[g % 2][:, :, j * T:(j + 1) * T], masked[:, :, :, :].rearrange("p m h q -> p m q h"),
                     ALU.add, ("attn32", tag, b))

        def split_attn(g):
            old = [("o_ps", tag, g - 1)] if g else []
            if biases:
                for m in range(KD):
                    attnT.fill(p, attn32[g % 2][:, m, :], lambda t: t[:, m, :],
                               ("attn" if m == KD - 1 else "attn_0", tag, g),
                               [("attn_sum", tag, g)], old, biases["v"][:, m:m + 1])
            else:
                attnT.fill(p, attn32[g % 2][:, :, :], lambda t: t[:, :, :], ("attn", tag, g),
                           [("attn_sum", tag, g)], old)

        def project_out(g):
            bank, free = turn_banks.take((("x_out", tag, g),))
            p.wait("tensor", *both("attn", tag, g), *free)
            p.split_product(bank[:, 0:D], lambda k: attnT.pair(lambda t: t[:, k, :]),
                            lambda k: part(w["o"], k, 0, D), KD, ("o_ps", tag, g))
            p.wait("vector", ("o_ps", tag, g))
            p.tensor_tensor(X[:, g, :], X[:, g, :], bank[:, 0:D], ALU.add, done=("x_out", tag, g))
            if biases:
                p.wait("gpsimd", ("x_out", tag, g))
                p.tensor_tensor(X[:, g, :], X[:, g, :], biases["o"][:, :], ALU.add, ("x_bias", tag, g), "gpsimd")

        def free_xT(s):
            return [("q_ps", tag, s - 1, KD - 1)] if s else []

        load_ctx(0)
        load_ctx(1)
        ln.normalise(0, [x_ready(0)])
        ln.turn(0, banks, free_xT(0))
        project_q(0)
        for b in range(2):
            split_ctx(b)
            spread_q(b)
        for m in range(KD):
            project_k(0, m)
        for i in range(B + BPG):
            now, after, before = i < B, i + 1 < B, 2 <= i < B + 2
            for n in range(2):
                if before:
                    turn_prob(i - 2, n)
                if after:
                    project_k(i + 1, n)
                if i + 2 < B and n == 0:
                    split_ctx(i + 2)
                    if (i + 3) % BPG == 0 and (i + 3) // BPG + 1 < G:
                        load_ctx((i + 3) // BPG + 1)
            if now:
                scores(i)
                for n in range(2):
                    find_max(i, n)
                    exponentials(i, n)
            if i + 2 < B:
                spread_q(i + 2)
            g, j = i // BPG, i % BPG
            if now and j == 2:
                project_last(g)
            if j == 3:
                if now:
                    turn_last(g)
                if g >= 1:
                    project_out(g - 1)
            if j == 2 and g >= 1:
                add_last(g - 1)
                split_attn(g - 1)
            s = i // BPS + 1
            if s < SG and i % BPS == 5:
                ln.turn(s, turn_banks, free_xT(s))
            if s < SG and i % BPS == 8:
                project_q(s)
            if before:
                weigh_v(i - 2)
            if now:
                normalise(i)
                project_v(i)
            if now:
                if j == 1:
                    split_last(g)
                keep_last(i)
                if j == BPG - 1:
                    spread_last(g)
            if s < SG and i % BPS == 3:
                ln.normalise(s, [x_ready(s)])
        p.run()


def attend(p, tag, g, qT, kT, v, dv, head_rows, tiles, scale, bound, ready):
    R = P // head_rows
    NH = H // R
    t = tiles
    score = t["score"](g)
    p.wait("tensor", *ready, *t["score_free"](g))
    for n in range(NH):
        for b in range(BPG):
            for r in range(R):
                rows = slice(r * head_rows, (r + 1) * head_rows)
                last = (n, b, r) == (NH - 1, BPG - 1, R - 1)
                p.matmul(score[b * T:(b + 1) * T, r, n, :], qT(g)[rows, n, b * T:(b + 1) * T],
                         kT(g)[rows, n, b * T:(b + 1) * T], done=("s_score", tag, g) if last else None)
    src, grid = score, [P, R, NH, T]
    cell = lambda a: a.rearrange("p (r n q) -> p r n q", r=R, q=T)
    stat = lambda a: a.rearrange("p (r n) -> p r n", r=R)
    p.wait("vector", ("s_score", tag, g))
    e = g % 2
    if g >= 2:
        p.wait("vector", ("s_exp", tag, g - 2), ("s_probT", tag, g - 2), ("s_out", tag, g - 2))
    if bound is not None:
        for r in range(R):
            p.scalar_tensor_tensor(cell(t["sc"][e][:, :])[:, r], score[:, r], scale, bound.unsqueeze(1).to_broadcast([P, NH, T]),
                                   ALU.mult, ALU.min, ("s_masked", tag, g, r))
        p.wait("vector", ("s_masked", tag, g, R - 1))
        src, scale = cell(t["sc"][e][:, :]), 1.0
    p.reduce(stat(t["neg_max"][e][:, :]), src, ALU.max, ("s_max", tag, g), negate=True)
    p.wait("vector", ("s_max", tag, g))
    p.tensor_tensor(cell(t["shifted"][e][:, :]), src,
                    stat(t["neg_max"][e][:, :]).unsqueeze(3).to_broadcast(grid), ALU.add, ("s_shift", tag, g))
    p.wait("scalar", ("s_shift", tag, g))
    p.activation(t["prob"][e][:, :], t["shifted"][e][:, :], ACT.Exp, ("s_exp", tag, g), scale=scale)
    p.wait("vector", ("s_exp", tag, g))
    if g >= 2:
        p.wait("vector", ("s_pv", tag, g - 2))
    p.do("vector", lambda eng: eng.transpose(t["probT"][e][:, :], t["prob"][e][:, :]), ("s_probT", tag, g))
    p.reduce(t["sums"][e][:, :], t["prob"][e][:, :].rearrange("p (h q) -> p h q", q=T), ALU.add, ("s_sum", tag, g))
    p.wait("vector", ("s_sum", tag, g))
    p.reciprocal(t["inv"][e][:, :], t["sums"][e][:, :], ("s_inv", tag, g))


def weigh_self(p, tag, g, v, dv, head_rows, tiles):
    R = P // head_rows
    NH = H // R
    out, free = tiles["out"](g), tiles["out_free"](g)
    probT = tiles["probT"][g % 2]
    p.wait("tensor", ("s_probT", tag, g), *free)
    for h in range(H):
        c0 = (h % R * NH + h // R) * T
        for b in range(BPG):
            rows = slice(b * T, (b + 1) * T)
            p.matmul(out[rows, h, :], probT[rows, c0:c0 + T], v(g)[rows, h * dv:(h + 1) * dv],
                     done=("s_pv", tag, g) if (h, b) == (H - 1, BPG - 1) else None)


def by_head(ap, R):
    return ap.rearrange("p (r n) -> p n r", r=R)


def self_attention_0(p, nc, X, consts, mats):
    tag = "s0"
    with ExitStack() as stack:
        def sb(name, shape, dt=F32):
            return stack.enter_context(nc.sbuf_tensor(f"{name}_{tag}", shape, dt))

        PADW = H * T
        NT = PADW // P
        loader = Weights(p, nc, stack, tag, KD * PADW)
        w = {n: loader.load(n, mats[n]) for n in ("q", "k", "v")}
        ready_w = [r for m in w.values() for r in m.ready]
        xT = [Split(nc, stack, f"xT{i}_{tag}", [P, KD, GPS * P]) for i in range(2)]
        lns = [LayerNorm(p, nc, stack, tag, X, consts, xT[0])]
        ln = lns[0]
        qT = [sb(f"qT{i}", [P, NT, GPS * P]) for i in range(2)]
        kT = [sb(f"kT{i}", [P, NT, GPS * P]) for i in range(2)]
        v = [sb(f"v{i}", [P, D]) for i in range(2)]
        t = {n: [sb(f"{n}{i}", [P, H * T]) for i in range(2)] for n in ("shifted", "prob", "probT")}
        t |= {n: [sb(f"{n}{i}", [P, H]) for i in range(2)] for n in ("neg_max", "sums", "inv")}
        add = [sb(f"add{i}", [P, D]) for i in range(2)]
        ps_score = stack.enter_context(nc.psum_tensor(f"ps_score_{tag}", [P, NT, 512], F32))
        ps_out = stack.enter_context(nc.psum_tensor(f"ps_out_{tag}", [P, 2, 512], F32))
        banks = Banks([stack.enter_context(nc.psum_tensor(f"ps_{i}_{tag}", [P, 512], F32)) for i in range(2)])
        NH = H // NT
        t["score"] = lambda g: ps_score[:, :, 0:NH * T].rearrange("p r (n q) -> p r n q", q=T)
        t["score_free"] = lambda g: [("s_shift", tag, g - 1)] if g else []
        t["out"] = lambda g: ps_out[:, g % 2, 0:D].rearrange("p (h d) -> p h d", d=XD)
        t["out_free"] = lambda g: [("s_out", tag, g - 2)] if g >= 2 else []
        cols = lambda a: (lambda g: a[g // GPS % 2][:, :, g % GPS * P:(g % GPS + 1) * P])
        qg, kg, vg = cols(qT), cols(kT), lambda g: v[g % 2]

        def project(s, name, m):
            dst = {"q": qT, "k": kT}[name][s % 2]
            kind = f"s_{name}T"
            bank, free = banks.take(((kind, tag, s, m),))
            p.wait("tensor", *[r for k in range(KD) for r in both("xT", tag, s, k)], *free, *ready_w)
            p.split_product(bank[:, :], lambda k: part(w[name], k, m * P, (m + 1) * P),
                            lambda k: xT[s % 2].pair(lambda a: a[:, k, :]), KD, (kind + "_ps", tag, s, m))
            p.wait("scalar", (kind + "_ps", tag, s, m))
            if s >= 2:
                p.wait("scalar", ("s_score", tag, (s - 1) * GPS - 1))
            p.activation(dst[:, m, :], bank[:, :], ACT.Copy, (kind, tag, s, m))

        def project_v(g):
            s, j = g // GPS, g % GPS
            bank, free = banks.take((("s_v", tag, g),))
            p.wait("tensor", *[r for k in range(KD) for r in both("xT", tag, s, k)], *free, *ready_w)
            p.split_product(bank[:, 0:D], lambda k: xT[s % 2].pair(lambda a: a[:, k, j * P:(j + 1) * P]),
                            lambda k: part(w["v"], k, 0, D), KD, ("s_v_ps", tag, g))
            p.wait("scalar", ("s_v_ps", tag, g))
            if g >= 2:
                p.wait("scalar", ("s_pv", tag, g - 2))
            p.activation(v[g % 2][:, :], bank[:, 0:D], ACT.Copy, ("s_v", tag, g))

        def finish(g):
            shape = [P, H, XD]
            p.wait("vector", ("s_pv", tag, g), ("s_inv", tag, g))
            if g >= 2:
                p.wait("vector", ("s_x", tag, g - 2))
            inv = by_head(t["inv"][g % 2][:, :], NT)
            p.tensor_tensor(add[g % 2][:, :].rearrange("p (n r d) -> p n r d", r=NT, d=XD),
                            t["out"](g).rearrange("p (n r) d -> p n r d", r=NT),
                            inv.unsqueeze(3).to_broadcast([P, NH, NT, XD]), ALU.mult, ("s_out", tag, g))
            p.wait("gpsimd", ("s_out", tag, g))
            p.tensor_tensor(X[:, g, :], X[:, g, :], add[g % 2][:, :], ALU.add, ("s_x", tag, g), "gpsimd")

        def prepare(s):
            free = [("s_qT_ps", tag, s - 2, NT - 1), ("s_kT_ps", tag, s - 2, NT - 1),
                    ("s_v_ps", tag, (s - 1) * GPS - 1)] if s >= 2 else []
            ln.dest = xT[s % 2]
            ln.normalise(s, [])
            ln.turn(s, banks, free)

        def scores(g):
            s = g // GPS
            ready = [(f"s_{n}T", tag, s, m) for n in "qk" for m in range(NT)]
            attend(p, tag, g, qg, kg, vg, XD, T, t, XD ** -0.5, None, ready)

        prepare(0)
        for n in "qk":
            for m in range(NT):
                project(0, n, m)
        for g in range(G + 1):
            s, j = g // GPS, g % GPS
            if g < G:
                scores(g)
                project_v(g)
            if s + 1 < SG:
                if j == 0:
                    prepare(s + 1)
                if j in (2, 3):
                    for m in range(NT):
                        project(s + 1, "qk"[j - 2], m)
            if g:
                p.wait("tensor", ("s_v", tag, g - 1))
                weigh_self(p, tag, g - 1, vg, XD, T, t)
                finish(g - 1)
        p.run()


def experts(p, nc, X, consts, mats):
    tag = "moe"
    with ExitStack() as outer:
        xT = Split(nc, outer, f"xT_{tag}", [P, KD, B * T])
        share = outer.enter_context(nc.sbuf_tensor("share", [P, G, E], F32))
        with ExitStack() as stack:
            def sb(name, shape, dt=F32):
                return stack.enter_context(nc.sbuf_tensor(f"{name}_{tag}", shape, dt))

            loader = Weights(p, nc, stack, tag, KD * E)
            router = loader.load("router", mats["router"])
            ln = LayerNorm(p, nc, stack, tag, X, consts, xT)
            logitT = [sb(f"logitT{i}", [E, GPS * P]) for i in range(2)]
            logit, prob, hot = (sb(n, [P, G, E]) for n in ("logit", "prob", "hot"))
            top = sb("top", [P, G, 8])
            which = sb("which", [P, G, 8], U32)
            which_f = sb("which_f", [P, G, 8])
            stat = sb("stat", [P, G])
            banks = Banks([stack.enter_context(nc.psum_tensor(f"ps_{i}_{tag}", [P, 512], F32)) for i in range(4)])
            for s in range(SG):
                ln.normalise(s, [])
                ln.turn(s, banks, [])
                bank, free = banks.take((("logitT", s),))
                p.wait("tensor", *[r for k in range(KD) for r in both("xT", tag, s, k)], *free, *router.ready)
                p.split_product(bank[0:E, :], lambda k: part(router, k, 0, E),
                                lambda k: xT.pair(lambda t: t[:, k, s * GPS * P:(s + 1) * GPS * P]), KD,
                                ("logit_ps", s))
                p.wait("scalar", ("logit_ps", s))
                if s >= 2:
                    p.wait("scalar", ("logit_T", s - 2))
                p.activation(logitT[s % 2][:, :], bank[0:E, :], ACT.Copy, ("logitT", s))
                bank, free = banks.take((("logit", s),))
                p.wait("tensor", ("logitT", s), *free)
                for j in range(GPS):
                    p.transpose(bank[:, j * E:(j + 1) * E], logitT[s % 2][:, j * P:(j + 1) * P],
                                consts["ident"][0:E, 0:E], ("logit_T", s) if j == GPS - 1 else None)
                p.wait("scalar", ("logit_T", s))
                p.activation(logit[:, s * GPS:(s + 1) * GPS, :],
                             bank[:, 0:GPS * E].rearrange("p (g e) -> p g e", e=E), ACT.Copy, ("logit", s))
            spread = lambda a: a.unsqueeze(2).to_broadcast([P, G, E])
            p.wait("vector", ("logit", SG - 1))
            p.reduce(stat[:, :], logit[:, :, :], ALU.max, ("route", 0), negate=True)
            p.wait("vector", ("route", 0))
            p.tensor_tensor(logit[:, :, :], logit[:, :, :], spread(stat[:, :]), ALU.add, ("route", 1))
            p.wait("scalar", ("route", 1))
            p.activation(prob[:, :, :], logit[:, :, :], ACT.Exp, ("route_exp",))
            p.wait("vector", ("route_exp",))
            p.reduce(stat[:, :], prob[:, :, :], ALU.add, ("route", 2))
            p.wait("vector", ("route", 2))
            p.reciprocal(stat[:, :], stat[:, :], ("route", 3))
            p.wait("vector", ("route", 3))
            p.tensor_tensor(prob[:, :, :], prob[:, :, :], spread(stat[:, :]), ALU.mult, ("route", 4))
            p.wait("vector", ("route", 4))
            for g in range(G):
                p.do("vector", lambda e, g=g: e.max(top[:, g, :], prob[:, g, :]), ("route_top", g))
            p.wait("vector", ("route_top", G - 1))
            for g in range(G):
                p.do("vector", lambda e, g=g: e.max_index(which[:, g, :], top[:, g, :], prob[:, g, :]),
                     ("route_which", g))
            p.wait("vector", ("route_which", G - 1))
            p.copy(which_f[:, :, 0:2], which[:, :, 0:2], ("route", 5))
            p.tensor_tensor(stat[:, :], top[:, :, 0], top[:, :, 1], ALU.add, ("route", 6))
            p.wait("vector", ("route", 6))
            p.reciprocal(stat[:, :], stat[:, :], ("route", 7))
            p.wait("vector", ("route", 7))
            p.tensor_tensor(top[:, :, 0:2], top[:, :, 0:2], stat[:, :].unsqueeze(2).to_broadcast([P, G, 2]),
                            ALU.mult, ("route", 8))
            p.wait("vector", ("route", 8), ("const_in",))
            number = consts["numbers"][:, :].unsqueeze(1).to_broadcast([P, G, E])
            for n, dst in enumerate((share[:, :, :], hot[:, :, :])):
                p.tensor_tensor(dst, number, spread(which_f[:, :, n]), ALU.is_equal, ("route", 9 + 2 * n))
                p.wait("vector", ("route", 9 + 2 * n))
                p.tensor_tensor(dst, dst, spread(top[:, :, n]), ALU.mult, ("route", 10 + 2 * n))
            p.wait("vector", ("route", 12))
            p.tensor_tensor(share[:, :, :], share[:, :, :], hot[:, :, :], ALU.add, ("share",))
            p.run()

        with ExitStack() as stack:
            def sb(name, shape, dt=F32):
                return stack.enter_context(nc.sbuf_tensor(f"{name}_{tag}", shape, dt))

            WN = KD * HID
            names = ("gate", "up", "down")
            stage = sb("w_stage", [P, 3, WN])
            w = [{n: Split(nc, stack, f"{n}{i}_{tag}", [P, WN]) for n in names} for i in range(2)]
            silu = [sb(f"silu{i}", [P, GPS * P]) for i in range(2)]
            hid32 = [sb(f"hid32{i}", [P, GPS * P]) for i in range(2)]
            hid = [Split(nc, stack, f"hid{i}_{tag}", [P, KH, GPS * P]) for i in range(2)]
            gate_banks, up_banks, y_banks = (
                Banks([stack.enter_context(nc.psum_tensor(f"ps_{n}{i}_{tag}", [P, 512], F32)) for i in range(c)])
                for n, c in (("gate", 2), ("up", 2), ("y", 4)))
            NS = E * SG

            def load(e):
                for i, n in enumerate(names):
                    if e:
                        p.wait("sync", *both(f"w_{n}", e - 1))
                    p.dma(stage[:, i, :], mats[n][e].rearrange("p a b -> p (a b)"), (f"w_{n}_in", e))

            def split_w(e, i):
                n = names[i]
                old = [("y_ps", (e - 1) * SG - 1, GPS - 1)] if e >= 2 else []
                w[e % 2][n].fill(p, stage[:, i, :], lambda t: t[:, :], (f"w_{n}", e), [(f"w_{n}_in", e)], old)

            def gate_up(n, h):
                e, s = n // SG, n % SG
                i = (n * KH + h) % 2
                readers = {"gate": (("silu", n, h),), "up": (("hid32", n, h),)}
                got = {}
                for name, bk in (("gate", gate_banks), ("up", up_banks)):
                    bank, free = bk.take(readers[name])
                    p.wait("tensor", *both(f"w_{name}", e), *free)
                    p.split_product(bank[:, :], lambda k: w[e % 2][name].pair(
                        lambda t: t[:, k * HID + h * P:k * HID + (h + 1) * P]),
                        lambda k: xT.pair(lambda t: t[:, k, s * GPS * P:(s + 1) * GPS * P]), KD, (name + "_ps", n, h))
                    got[name] = bank
                before = ((n * KH + h) - 2) // KH, ((n * KH + h) - 2) % KH
                p.wait("scalar", ("gate_ps", n, h))
                if before[0] >= 0:
                    p.wait("scalar", ("hid32", *before))
                p.activation(silu[i][:, :], got["gate"][:, :], ACT.Silu, ("silu", n, h))
                p.wait("vector", ("silu", n, h), ("up_ps", n, h))
                if before[0] >= 0:
                    p.wait("vector", *both("hid", *before))
                p.tensor_tensor(hid32[i][:, :], got["up"][:, :], silu[i][:, :], ALU.mult, ("hid32", n, h))
                old = [("y_ps", n - 2, GPS - 1)] if n >= 2 else []
                hid[n % 2].fill(p, hid32[i][:, :], lambda t: t[:, h, :], ("hid", n, h), [("hid32", n, h)], old)

            def down(n, j):
                e, s = n // SG, n % SG
                g = s * GPS + j
                bank, free = y_banks.take((("y", n, j),))
                p.wait("tensor", *both("hid", n, KH - 1), *both("w_down", e), *free)
                p.split_product(bank[:, 0:D], lambda k: hid[n % 2].pair(lambda t: t[:, k, j * P:(j + 1) * P]),
                                lambda k: w[e % 2]["down"].pair(lambda t: t[:, k * D:(k + 1) * D]), KH,
                                ("y_ps", n, j))
                p.wait("vector", ("y_ps", n, j))
                if e:
                    p.wait("vector", ("y", n - SG, j))
                p.scalar_tensor_tensor(X[:, g, :], bank[:, 0:D], share[:, g, e:e + 1], X[:, g, :],
                                       ALU.mult, ALU.add, ("y", n, j))

            load(0)
            for i in range(3):
                split_w(0, i)
            load(1)
            for n in range(NS + 1):
                for h in range(KH):
                    if n < NS:
                        gate_up(n, h)
                    if n and h % 2:
                        down(n - 1, h - 1)
                        down(n - 1, h)
                e, s = n // SG + 1, n % SG
                if e < E and 2 <= s < 5:
                    split_w(e, s - 2)
                if s == 6 and e + 1 < E:
                    load(e + 1)
            p.run()


class BitLinear:

    def __init__(self, p, nc, stack, X, consts, weight, banks, out):
        tag = "bit"

        def sb(name, shape, dt=F32):
            return stack.enter_context(nc.sbuf_tensor(f"{name}_{tag}", shape, dt))

        w32 = sb("w32", [P, KD * D])
        row = sb("row", [P, 1])
        scale, inv_scale = sb("scale", [P, 1]), sb("inv_scale", [P, 1])
        wq = sb("wq", [P, KD * D], BF16)
        stats, mv, = sb("stats", [P, G, 6]), sb("mv", [P, G, 2])
        var, rstd, top, inv, back = (sb(n, [P, G]) for n in ("var", "rstd", "top", "inv", "back"))
        xn = [sb(f"xn{i}", [P, GPS, D]) for i in range(2)]
        zT = [sb(f"zT{i}", [P, D], BF16) for i in range(3)]
        sum_bank, sum_free = banks.take((("bit_w", 1),))

        p.dma(w32[:, :], weight.rearrange("p a b -> p (a b)"), ("bit_w_in",))
        p.wait("vector", ("bit_w_in",))
        p.reduce(row[:, :], w32[:, :], ALU.add, ("bit_w", 0), apply_absolute_value=True)
        p.wait("tensor", ("bit_w", 0), *sum_free)
        p.matmul(sum_bank[:, 0:1], consts["ones"][:, :], row[:, :], done=("bit_sum",))
        p.wait("vector", ("bit_sum",))
        p.tensor_scalar(scale[:, :], sum_bank[:, 0:1], 1.0 / (D * D), 1e-8, ALU.mult, ALU.add, ("bit_w", 1))
        p.wait("vector", ("bit_w", 1))
        p.reciprocal(inv_scale[:, :], scale[:, :], ("bit_w", 2))
        p.wait("vector", ("bit_w", 2))
        p.tensor_scalar(w32[:, :], w32[:, :], inv_scale[:, 0:1], ROUND, ALU.mult, ALU.add, ("bit_w", 3))
        p.wait("vector", ("bit_w", 3))
        p.tensor_scalar(w32[:, :], w32[:, :], ROUND, 1.0, ALU.subtract, ALU.min, ("bit_w", 4))
        p.wait("vector", ("bit_w", 4))
        p.tensor_scalar(wq[:, :], w32[:, :], -1.0, None, ALU.max, done=("bit_w", 5))

        def normalise(s, ready):
            groups = range(s * GPS, (s + 1) * GPS)
            p.wait("vector", ready)
            for g in groups:
                p.do("vector", lambda e, g=g: e.bn_stats(stats[:, g, :], X[:, g, :]), ("bit_stats", g))
            p.wait("vector", ("bit_stats", groups[-1]))
            for g in groups:
                p.do("vector", lambda e, g=g: e.bn_aggr(mv[:, g, :], stats[:, g, :]), ("bit_aggr", g))
            sg = slice(groups[0], groups[-1] + 1)
            p.wait("vector", ("bit_aggr", groups[-1]))
            p.tensor_scalar(var[:, sg], mv[:, sg, 1], LN_EPS, None, ALU.add, done=("bit_var", s))
            p.wait("gpsimd", ("bit_var", s))
            p.tensor_tensor(rstd[:, sg], var[:, sg], consts["minus_half"][:, :], ALU.pow, ("bit_rstd", s), "gpsimd")

        def quantise(s):
            groups = range(s * GPS, (s + 1) * GPS)
            sg, i = slice(groups[0], groups[-1] + 1), s % 2
            p.wait("vector", ("bit_rstd", s))
            if s >= 2:
                p.wait("vector", ("bit_T", groups[0] - GPS - 1))
            for j, g in enumerate(groups):
                p.tensor_scalar(xn[i][:, j, :], X[:, g, :], mv[:, g, 0:1], rstd[:, g:g + 1], ALU.subtract, ALU.mult,
                                ("bit_xn", g))
            p.wait("vector", ("bit_xn", groups[-1]))
            p.reduce(top[:, sg], xn[i][:, :, :], ALU.max, ("bit_top", s), apply_absolute_value=True)
            p.wait("vector", ("bit_top", s))
            p.tensor_scalar(top[:, sg], top[:, sg], 1e-8, None, ALU.add, done=("bit_a", s))
            p.wait("vector", ("bit_a", s))
            p.reciprocal(inv[:, sg], top[:, sg], ("bit_inv", s))
            p.tensor_scalar(back[:, sg], top[:, sg], scale[:, 0:1], 1.0 / 127.0, ALU.mult, ALU.mult,
                            ("bit_back", s))

        def round_z(s):
            groups, i = range(s * GPS, (s + 1) * GPS), s % 2
            p.wait("vector", ("bit_inv", s))
            for j, g in enumerate(groups):
                p.tensor_scalar(xn[i][:, j, :], xn[i][:, j, :], inv[:, g:g + 1], 127.0, ALU.mult, ALU.mult,
                                ("bit_z0", g))
            p.wait("vector", ("bit_z0", groups[-1]))
            p.tensor_scalar(xn[i][:, :, :], xn[i][:, :, :], 127.0, -128.0, ALU.min, ALU.max, ("bit_z1", s))
            p.wait("vector", ("bit_z1", s))
            p.tensor_scalar(xn[i][:, :, :], xn[i][:, :, :], ROUND, ROUND, ALU.add, ALU.subtract, ("bit_z", s))

        def product(g):
            i, s, j = g % 3, g // GPS, g % GPS
            bank, free = banks.take((("bit_zT", g),))
            p.wait("tensor", ("bit_z", s), *free)
            for k in range(KD):
                p.transpose(bank[:, k * P:(k + 1) * P], xn[s % 2][:, j, k * P:(k + 1) * P], consts["ident"][:, :],
                            ("bit_T", g) if k == KD - 1 else None)
            p.wait("scalar", ("bit_T", g))
            if g >= 3:
                p.wait("scalar", ("bit_y_ps", g - 3))
            p.activation(zT[i][:, :], bank[:, 0:D], ACT.Copy, ("bit_zT", g))
            bank, free = banks.take((("bit_x", g),))
            p.wait("tensor", ("bit_zT", g), ("bit_w", 5), *free)
            for k in range(KD):
                p.matmul(bank[:, 0:D], zT[i][:, k * P:(k + 1) * P], wq[:, k * D:(k + 1) * D],
                         start=k == 0, stop=k == KD - 1, done=("bit_y_ps", g) if k == KD - 1 else None)
            p.wait("vector", ("bit_y_ps", g), ("bit_back", s))
            p.scalar_tensor_tensor(X[:, g, :], bank[:, 0:D], back[:, g:g + 1], X[:, g, :], ALU.mult, ALU.add,
                                   ("bit_x", g))
            if j == GPS - 1:
                p.wait("sync", ("bit_x", g))
                p.dma(out[:, s * GPS:(s + 1) * GPS, :], X[:, s * GPS:(s + 1) * GPS, :], ("stored", s))

        self.normalise, self.quantise, self.round, self.product = normalise, quantise, round_z, product


def self_attention_1(p, nc, X, consts, mats, out):
    tag = "s1"
    with ExitStack() as stack:
        def sb(name, shape, dt=F32):
            return stack.enter_context(nc.sbuf_tensor(f"{name}_{tag}", shape, dt))

        loader = Weights(p, nc, stack, tag, F1 // P * D)
        wqkv = [loader.load(f"qkv{i}", mats["qkv"][i]) for i in range(3)]
        wout = loader.load("out", mats["out"])
        ready_w = [r for m in (*wqkv, wout) for r in m.ready]
        xT = [Split(nc, stack, f"xT{i}_{tag}", [P, KD, GPS * P]) for i in range(2)]
        ln = LayerNorm(p, nc, stack, tag, X, consts, xT[0])
        HB = 512 // D1
        NB = F1 // 512
        turned = [sb(f"turned{i}", [P, HB, D1]) for i in range(2)]
        swapped = [sb(f"swapped{i}", [P, HB, D1]) for i in range(2)]
        rot = [sb(f"rot{i}", [P, HB, D1]) for i in range(2)]
        qT, kT = ([sb(f"{n}{i}", [P, F1 // P, P]) for i in range(2)] for n in ("qT", "kT"))
        v = [sb(f"v{i}", [P, F1]) for i in range(2)]
        t = {n: [sb(f"{n}{i}", [P, H * T]) for i in range(2)] for n in ("sc", "shifted", "prob", "probT")}
        t |= {n: [sb(f"{n}{i}", [P, H]) for i in range(2)] for n in ("neg_max", "sums", "inv")}
        attn = sb("attn", [P, F1])
        attnT = Split(nc, stack, f"attnT_{tag}", [P, F1])
        R = P // D1
        NH = H // R
        ps_score = stack.enter_context(nc.psum_tensor(f"ps_score_{tag}", [P, R, 512], F32))
        ps_out = stack.enter_context(nc.psum_tensor(f"ps_out_{tag}", [P, F1], F32))
        banks = Banks([stack.enter_context(nc.psum_tensor(f"ps_{i}_{tag}", [P, 512], F32)) for i in range(4)])
        t["score"] = lambda g: ps_score[:, :, 0:NH * T].rearrange("p r (n q) -> p r n q", q=T)
        t["score_free"] = lambda g: [("s_masked", tag, g - 1, R - 1)] if g else []
        t["out"] = lambda g: ps_out[:, :].rearrange("p (h d) -> p h d", d=D1)
        t["out_free"] = lambda g: [("s_out", tag, g - 1)] if g else []
        turns = {"n": 0}

        def project(g, i, c):
            s, j = g // GPS, g % GPS
            name = "qkv"[i]
            readers = (("s_v", tag, g, c),) if i == 2 else (("turned", tag, g, i, c), ("swap1", tag, g, i, c))
            bank, free = banks.take(readers)
            p.wait("tensor", *[r for k in range(KD) for r in both("xT", tag, s, k)], *free, *ready_w)
            p.split_product(bank[:, :], lambda k: xT[s % 2].pair(lambda a: a[:, k, j * P:(j + 1) * P]),
                            lambda k: part(wqkv[i], k, c * 512, (c + 1) * 512), KD, ("s_qkv_ps", tag, g, i, c))
            if i == 2:
                p.wait("scalar", ("s_qkv_ps", tag, g, i, c))
                if g >= 2:
                    p.wait("scalar", ("s_pv", tag, g - 2))
                p.activation(v[g % 2][:, c * 512:(c + 1) * 512], bank[:, :], ACT.Copy, ("s_v", tag, g, c))
                return
            b3 = bank[:, :].rearrange("p (h d) -> p h d", d=D1)
            cos = consts["cos"][:, :].unsqueeze(1).to_broadcast([P, HB, D1])
            e = turns["n"] % 2
            old, turns["n"] = turns.get(e, []), turns["n"] + 1
            p.wait("vector", ("s_qkv_ps", tag, g, i, c), ("const_in",), *old)
            p.tensor_tensor(turned[e][:, :, :], b3, cos, ALU.mult, ("turned", tag, g, i, c))
            for a in range(2):
                sin = consts["sin"][:, a::2].unsqueeze(1).to_broadcast([P, HB, D1 // 2])
                p.tensor_tensor(swapped[e][:, :, a::2], b3[:, :, 1 - a::2], sin, ALU.mult, (f"swap{a}", tag, g, i, c))
            p.wait("gpsimd", ("turned", tag, g, i, c), ("swap1", tag, g, i, c))
            if old:
                p.wait("gpsimd", turns[("T", e)])
            p.tensor_tensor(rot[e][:, :, :], turned[e][:, :, :], swapped[e][:, :, :], ALU.add,
                            ("rot", tag, g, i, c), "gpsimd")
            turns[e] = [("rot", tag, g, i, c)]
            turns[("T", e)] = ("rot_T", tag, g, i, c)
            turns[("src", g, i, c)] = rot[e]

        def turn(g, i, c):
            dst = (qT, kT)[i][g % 2]
            bank, free = banks.take((("s_qkT", tag, g, i, c),))
            src = turns[("src", g, i, c)]
            p.wait("tensor", ("rot", tag, g, i, c), *free)
            for n in range(4):
                p.transpose(bank[:, n * P:(n + 1) * P], src[:, :, :].rearrange("p h d -> p (h d)")[:, n * P:(n + 1) * P],
                            consts["ident"][:, :], ("rot_T", tag, g, i, c) if n == 3 else None)
            p.wait("scalar", ("rot_T", tag, g, i, c))
            if g >= 2:
                p.wait("scalar", ("s_score", tag, g - 2))
            p.activation(dst[:, 4 * c:4 * c + 4, :], bank[:, :].rearrange("p (n q) -> p n q", q=P), ACT.Copy,
                         ("s_qkT", tag, g, i, c))

        def scores(g):
            ready = [("s_qkT", tag, g, 1, NB - 1), ("s_qkT", tag, g, 0, NB - 1)]
            attend(p, tag, g, lambda g: qT[g % 2], lambda g: kT[g % 2], None, D1, D1, t, D1 ** -0.5,
                   consts["causal"][:, :], ready)

        def finish(g):
            p.wait("vector", ("s_pv", tag, g), ("s_inv", tag, g))
            if g:
                p.wait("vector", ("attn_T", tag, g - 1, NB - 1))
            inv = by_head(t["inv"][g % 2][:, :], R)
            p.tensor_tensor(attn[:, :].rearrange("p (n r d) -> p n r d", r=R, d=D1),
                            t["out"](g).rearrange("p (n r) d -> p n r d", r=R),
                            inv.unsqueeze(3).to_broadcast([P, NH, R, D1]), ALU.mult, ("s_out", tag, g))

        def turn_out(g, c):
            bank, free = banks.take(both("s_attnT", tag, g, c))
            p.wait("tensor", ("s_out", tag, g), *free)
            for n in range(4):
                p.transpose(bank[:, n * P:(n + 1) * P], attn[:, c * 512 + n * P:c * 512 + (n + 1) * P],
                            consts["ident"][:, :], ("attn_T", tag, g, c) if n == 3 else None)
            old = [("s_o_ps", tag, g - 1)] if g else []
            attnT.fill(p, bank[:, :], lambda a: a[:, c * 512:(c + 1) * 512], ("s_attnT", tag, g, c),
                       [("attn_T", tag, g, c)], old)

        def add_out(g):
            bank, free = banks.take((("s_x", tag, g),))
            p.wait("tensor", *[r for c in range(NB) for r in both("s_attnT", tag, g, c)], *free)
            p.split_product(bank[:, 0:D], lambda k: attnT.pair(lambda a: a[:, k * P:(k + 1) * P]),
                            lambda k: part(wout, k, 0, D), F1 // P, ("s_o_ps", tag, g))
            p.wait("vector", ("s_o_ps", tag, g))
            p.tensor_tensor(X[:, g, :], X[:, g, :], bank[:, 0:D], ALU.add, ("s_x", tag, g))

        def prepare(s):
            ln.dest = xT[s % 2]
            ln.turn(s, banks, [("s_qkv_ps", tag, (s - 1) * GPS - 1, 2, NB - 1)] if s >= 2 else [])

        bit = BitLinear(p, nc, stack, X, consts, mats["bit"], banks, out)
        ln.normalise(0, [])
        prepare(0)
        for g in range(G + 2 + 2 * GPS):
            now, before, out = g < G, 1 <= g <= G, 2 <= g < G + 2
            if now:
                project(g, 0, 0)
                project(g, 0, 1)
            if out:
                turn_out(g - 2, 0)
            if now:
                project(g, 1, 0)
                project(g, 1, 1)
            if out:
                turn_out(g - 2, 1)
            if before:
                scores(g - 1)
            if now:
                turn(g, 0, 0)
                turn(g, 0, 1)
                project(g, 2, 0)
                turn(g, 1, 0)
            if out:
                add_out(g - 2)
            if now:
                turn(g, 1, 1)
                project(g, 2, 1)
            if before:
                p.wait("tensor", ("s_v", tag, g - 1, NB - 1))
                weigh_self(p, tag, g - 1, lambda g: v[g % 2], D1, D1, t)
                finish(g - 1)
            s = g // GPS + 1
            if s < SG:
                if g % GPS == 1:
                    ln.normalise(s, [])
                if g % GPS == 2:
                    prepare(s)
            done, j = divmod(g - GPS - 2, GPS)
            if 0 <= done < SG:
                if j == 0:
                    bit.normalise(done, ("s_x", tag, done * GPS + GPS - 1))
                if j == 1:
                    bit.quantise(done)
                if j == 2:
                    bit.round(done)
            if 0 <= g - GPS - 5 < G:
                bit.product(g - GPS - 5)
        p.wait("sync", ("stored", SG - 1))
        p.run()


def build(nc, a, out, phases=(1, 2, 3, 4, 5, 6)):
    with ExitStack() as stack:
        def sb(name, shape):
            return stack.enter_context(nc.sbuf_tensor(name, shape, F32))

        p = Program(nc, stack)
        X = sb("X", [P, G, D])
        consts = {n: sb("const_" + n, list(a["c_" + n].shape)) for n in
                  ("ident", "head_rows", "causal", "cos", "sin", "numbers", "ones", "minus_half", "same_query", "head_sum")}
        biases = {n: sb("bias_" + n, [P, KD] if n != "o" else [P, D]) for n in "qkvo"}

        for n, t in consts.items():
            p.dma(t[:, :], a["c_" + n], ("const", n))
        for n, t in biases.items():
            src = a["b_" + n]
            p.dma(t[:, :], src.partition_broadcast(P) if n == "o" else src, ("const", "bias_" + n))
        p.done[("const_in",)] = ("const", p.count["const"])
        for s in range(SG):
            p.dma(X[:, s * GPS:(s + 1) * GPS, :], a["x"][:, s * GPS:(s + 1) * GPS, :], (f"x_in{s}",))
        for e in ("tensor", "vector", "scalar", "gpsimd"):
            p.wait(e, ("const_in",))

        if 1 in phases:
            cross_attention(p, nc, "x0", X, a["ctx"], consts, {n: a["x0_" + n] for n in "qkvo"}, biases,
                            lambda s: (f"x_in{s}",))
        else:
            for e in ("tensor", "vector", "scalar", "gpsimd"):
                p.wait(e, *[(f"x_in{s}",) for s in range(SG)])
        if 2 in phases:
            self_attention_0(p, nc, X, consts, {n: a["s0_" + n] for n in "qkv"})
        if 3 in phases:
            experts(p, nc, X, consts, {n: a["moe_" + n] for n in ("router", "gate", "up", "down")})
        if 4 in phases:
            cross_attention(p, nc, "x1", X, a["ctx"], consts, {n: a["x1_" + n] for n in "qo"}, None,
                            lambda s: (f"x_in{s}",))
        if 5 in phases:
            mats = {"qkv": a["s1_qkv"], "out": a["s1_out"], "bit": a["bit_weight"]}
            self_attention_1(p, nc, X, consts, mats, out)
        else:
            p.dma(out, X[:, :, :], ("stored", 0))
            p.wait("sync", ("stored", 0))
            p.run()


def tables():
    rows = np.arange(P)
    position = rows % T
    freqs = 1.0 / 10000.0 ** (np.arange(0, D1, 2) / D1)
    angle = (np.arange(T)[:, None].astype(np.float32) * freqs[None, :].astype(np.float32))[position]
    sin = np.repeat(np.sin(angle), 2, axis=1)
    sin[:, 0::2] *= -1.0
    big = np.finfo(np.float32).max
    out = {
        "c_ident": np.eye(P),
        "c_head_rows": (rows[:, None] // XD == np.arange(HPH)[None, :]),
        "c_causal": np.where(position[:, None] >= np.arange(T)[None, :], big, NEG_INF),
        "c_cos": np.repeat(np.cos(angle), 2, axis=1),
        "c_sin": sin,
        "c_numbers": np.tile(np.arange(E), (P, 1)),
        "c_ones": np.ones((P, P)),
        "c_same_query": position[:, None] == np.arange(T)[None, :],
        "c_head_sum": np.concatenate([4 * n + rows[:, None] // T == rows[None, :] // XD for n in range(HG // KD)], 1),
        "c_minus_half": np.full((P, GPS), -0.5),
    }
    return {n: np.ascontiguousarray(t, dtype=np.float32) for n, t in out.items()}


def lay_out(i):
    def pieces(m):
        return m.reshape(m.shape[0] // P, P, m.shape[1]).transpose(1, 0, 2)

    def padded(m):
        wide = np.zeros((D, H, T), m.dtype)
        wide[:, :, :XD] = m.reshape(D, H, XD)
        return wide.reshape(D, H * T)

    a = {
        "x": i["x"].reshape(G, P, D).transpose(1, 0, 2),
        "ctx": i["ctx_1024"].transpose(0, 2, 1).reshape(G, BPG, KD, P, S).transpose(0, 3, 2, 1, 4),
        "x0_q": pieces(i["L0_xattn_Wq"].T), "x0_k": pieces(i["L0_xattn_Wk"].T),
        "x0_v": pieces(i["L0_xattn_Wv"].T), "x0_o": pieces(i["L0_xattn_Wo"].T),
        "b_q": i["L0_xattn_bq"].reshape(KD, P).T, "b_k": i["L0_xattn_bk"].reshape(KD, P).T,
        "b_v": i["L0_xattn_bv"].reshape(KD, P).T, "b_o": i["L0_xattn_bo"],
        "s0_q": pieces(padded(i["L0_attn_w_Q"])), "s0_k": pieces(padded(i["L0_attn_w_K"])),
        "s0_v": pieces(i["L0_attn_w_V"]),
        "moe_router": pieces(i["L0_ffn_router_w"].T),
        "moe_gate": np.stack([pieces(m.T) for m in i["L0_ffn_w_gate"]]),
        "moe_up": np.stack([pieces(m.T) for m in i["L0_ffn_w_up"]]),
        "moe_down": np.stack([pieces(m.T) for m in i["L0_ffn_w_down"]]),
        "x1_q": pieces(i["L1_xattn_Wq"].T), "x1_o": pieces(i["L1_xattn_Wo"].T),
        "s1_qkv": np.stack([pieces(m) for m in np.split(i["L1_attn_W_qkv"], 3, axis=1)]),
        "s1_out": pieces(i["L1_attn_W_out"]),
        "bit_weight": pieces(i["L1_ffn_weight"].T),
    }
    return {n: np.ascontiguousarray(t) for n, t in a.items()}


def kernel(**inputs):
    import concourse.bacc as _bacc
    from concourse.bass_utils import run_bass_kernel_spmd as _run

    nc = _bacc.Bacc("TRN2", target_bir_lowering=False, num_devices=1)
    arrays = {**lay_out({n: np.asarray(t) for n, t in inputs.items()}), **tables()}
    aps = {n: nc.dram_tensor(n, t.shape, F32, kind="ExternalInput").ap() for n, t in arrays.items()}
    out = nc.dram_tensor("out", (P, G, D), F32, kind="ExternalOutput").ap()
    build(nc, aps, out)
    r = _run(nc, [arrays], core_ids=[0])
    return r.results[0]["out"].transpose(1, 0, 2).reshape(B, T, D)
```

```python
from contextlib import ExitStack

import numpy as np

import concourse.bass as bass
from concourse import mybir

F32 = mybir.dt.float32
F32R = mybir.dt.float32r
BF16 = mybir.dt.bfloat16
U32 = mybir.dt.uint32
ALU = mybir.AluOpType
ACT = mybir.ActivationFunctionType
AX_X = mybir.AxisListType.X

P = 128
B, T, D = 128, 32, 256
S = 257
S_EVEN = S + 1
KD = D // P
H = 16
BPG = P // T
G = B * T // P
GPS = 4
SG = G // GPS
BPS = BPG * GPS
HPH = H // KD
XD = D // H
HG = 4
HPG = H // HG
CHUNKS = S // P
assert S == CHUNKS * P + 1
E, HID = 8, 512
KH = HID // P
D1 = 64
F1 = H * D1
LN_EPS = 1e-5
NEG_INF = -1e9
TABLES = {"ident": P, "head_rows": HPH, "causal": T, "cos": D1, "sin": D1, "numbers": E, "ones": P,
          "minus_half": GPS, "same_query": T, "head_sum": HG // KD * P, "of_pair": T // XD}
ROUND = 1.5 * 2.0 ** 23


class Program:

    def __init__(self, nc, stack):
        self.nc, self.stack = nc, stack
        self.sems, self.count, self.done = {}, {}, {}
        self.queues = {e: [] for e in ("tensor", "vector", "scalar", "gpsimd", "sync")}
        self.reached = {e: {} for e in self.queues}

    def do(self, engine, emit, done=None, inc=1):
        sem = None
        if done is not None:
            kind = done[0]
            if kind not in self.sems:
                self.sems[kind] = self.stack.enter_context(self.nc.semaphore(kind))
                self.count[kind] = 0
            self.count[kind] += inc
            assert done not in self.done, done
            self.done[done] = (kind, self.count[kind])
            sem = self.sems[kind]
        self.queues[engine].append((emit, sem, inc))

    def wait(self, engine, *names):
        self.queues[engine].append((None, names, 0))

    def _emit(self, engine, eng):
        reached = self.reached[engine]
        for emit, sem, inc in self.queues[engine]:
            if emit is None:
                for name in sem:
                    kind, value = self.done[name]
                    if reached.get(kind, 0) < value:
                        eng.wait_ge(self.sems[kind], value)
                        reached[kind] = value
                continue
            ins = emit(eng)
            if sem is not None:
                ins.then_inc(sem, inc)
        self.queues[engine] = []

    def run(self):
        with self.nc.Block() as block:
            @block.sync
            def _(eng):
                self._emit("sync", eng)

            @block.gpsimd
            def _(eng):
                self._emit("gpsimd", eng)

            @block.scalar
            def _(eng):
                self._emit("scalar", eng)

            @block.vector
            def _(eng):
                self._emit("vector", eng)

            @block.tensor
            def _(eng):
                self._emit("tensor", eng)

    def dma(self, out, in_, done):
        self.do("sync", lambda e: e.dma_start(out, in_), done, 16)

    def matmul(self, out, lhsT, rhs, start=True, stop=True, done=None):
        self.do("tensor", lambda e: e.matmul(out, lhsT, rhs, start=start, stop=stop), done)

    def transpose(self, out, in_, ident, done=None):
        self.do("tensor", lambda e: e.transpose(out, in_, ident), done)

    def activation(self, out, in_, func, done=None, **kw):
        self.do("scalar", lambda e: e.activation(out, in_, func, **kw), done)

    def tensor_tensor(self, out, in0, in1, op, done=None, engine="vector"):
        self.do(engine, lambda e: e.tensor_tensor(out, in0, in1, op), done)

    def tensor_scalar(self, out, in0, s1, s2, op0, op1=None, done=None):
        if op1 is None:
            self.do("vector", lambda e: e.tensor_scalar(out, in0, s1, s2, op0), done)
        else:
            self.do("vector", lambda e: e.tensor_scalar(out, in0, s1, s2, op0, op1), done)

    def scalar_tensor_tensor(self, out, in0, scalar, in1, op0, op1, done=None):
        self.do("vector", lambda e: e.scalar_tensor_tensor(out=out, in0=in0, scalar=scalar, in1=in1,
                                                           op0=op0, op1=op1), done)

    def reduce(self, out, in_, op, done=None, **kw):
        self.do("vector", lambda e: e.tensor_reduce(out, in_, AX_X, op, **kw), done)

    def reciprocal(self, out, in_, done=None):
        self.do("vector", lambda e: e.reciprocal(out, in_), done)

    def copy(self, out, in_, done=None, engine="vector"):
        self.do(engine, lambda e: e.tensor_copy(out, in_), done)

    def memset(self, out, value, done=None, engine="vector"):
        self.do(engine, lambda e: e.memset(out, value), done)

    def split_product(self, out, lhs, rhs, pieces, done=None):
        steps = []
        for k in range(pieces):
            (lh, ll), (rh, rl) = lhs(k), rhs(k)
            steps += [(lh, rh), (lh, rl), (ll, rh)]
        for n, (a, b) in enumerate(steps):
            last = n == len(steps) - 1
            self.matmul(out, a, b, start=n == 0, stop=last, done=done if last else None)


class Split:

    def __init__(self, nc, stack, name, shape):
        self.hi = stack.enter_context(nc.sbuf_tensor(name + "_hi", shape, F32R))
        self.lo = stack.enter_context(nc.sbuf_tensor(name + "_lo", shape, F32R))

    def fill(self, p, src, at, name, ready, free=(), bias=None, lo_engine="vector"):
        hi, lo = at(self.hi), at(self.lo)
        p.wait("scalar", *ready, *free)
        if bias is None:
            p.activation(hi, src, ACT.Copy, done=("hi_" + name[0], *name[1:]))
        else:
            p.activation(hi, src, ACT.Identity, bias=bias, done=("hi_" + name[0], *name[1:]))
        p.wait(lo_engine, *ready, *free, ("hi_" + name[0], *name[1:]))
        if bias is None:
            p.tensor_tensor(lo, src, hi.bitcast(F32), ALU.subtract, ("lo_" + name[0], *name[1:]), lo_engine)
        else:
            p.scalar_tensor_tensor(lo, src, bias, hi.bitcast(F32), ALU.add, ALU.subtract,
                                   done=("lo_" + name[0], *name[1:]))

    def pair(self, at):
        return at(self.hi), at(self.lo)


def both(kind, *rest):
    return ("hi_" + kind, *rest), ("lo_" + kind, *rest)


class Banks:

    def __init__(self, tiles):
        self.tiles, self.readers, self.n = tiles, [()] * len(tiles), 0

    def take(self, readers):
        slot = self.n % len(self.tiles)
        self.n += 1
        free, self.readers[slot] = self.readers[slot], readers
        return self.tiles[slot], free


class Weights:

    def __init__(self, p, nc, stack, tag):
        self.p, self.nc, self.stack, self.tag = p, nc, stack, tag

    def load(self, name, dram, stages):
        shape = list(dram.shape)
        w = Split(self.nc, self.stack, f"w_{name}_{self.tag}", [P, int(np.prod(shape[1:]))])
        w.name, w.width, w.ready = name, shape[2], both("w", self.tag, name, len(stages) - 1)
        w.stages, w.arrived = stages, (f"w_in_{name}_{self.tag}", len(stages) - 1)
        n = w.columns = int(np.prod(shape[1:])) // len(stages)
        for i, stage in enumerate(stages):
            self.p.dma(stage[:, 0:n], dram.rearrange("p a b -> p (a b)")[:, i * n:(i + 1) * n], (w.arrived[0], i))
        return w

    def split(self, *loaded):
        for w in loaded:
            for i, stage in enumerate(w.stages):
                c0 = i * w.columns
                w.fill(self.p, stage[:, 0:w.columns], lambda t, c0=c0, w=w: t[:, c0:c0 + w.columns],
                       ("w", self.tag, w.name, i), [w.arrived])


def part(w, k, c0, c1):
    return w.pair(lambda t: t[:, k * w.width + c0:k * w.width + c1])


class LayerNorm:

    def __init__(self, p, nc, stack, tag, X, consts, dest):
        self.p, self.tag, self.X, self.consts, self.dest = p, tag, X, consts, dest
        t = lambda n, s: stack.enter_context(nc.sbuf_tensor(f"ln_{n}_{tag}", s, F32))
        self.stats = t("stats", [P, GPS, 6])
        self.mv = t("mean_var", [P, GPS, 2])
        self.var = t("var", [P, GPS])
        self.rstd = t("rstd", [P, GPS])
        self.xn = t("xn", [P, GPS, D])

    def take_stats(self, s, j, ready=()):
        p, tag = self.p, self.tag
        src = self.X[:, GPS * s + j, :]
        p.wait("vector", *ready)
        p.do("vector", lambda e: e.bn_stats(self.stats[:, j, :], src), ("ln_stats", tag, s, j))
        p.wait("vector", ("ln_stats", tag, s, j))
        p.do("vector", lambda e: e.bn_aggr(self.mv[:, j, :], self.stats[:, j, :]), ("ln_aggr", tag, s, j))
        if j < GPS - 1:
            return
        p.wait("vector", ("ln_aggr", tag, s, j))
        p.tensor_scalar(self.var[:, :], self.mv[:, :, 1], LN_EPS, None, ALU.add, done=("ln_var", tag, s))
        p.wait("gpsimd", ("ln_var", tag, s))
        p.tensor_tensor(self.rstd[:, :], self.var[:, :], self.consts["minus_half"][:, :], ALU.pow,
                        done=("ln_rstd", tag, s), engine="gpsimd")

    def scale(self, s):
        p, tag = self.p, self.tag
        p.wait("vector", ("ln_rstd", tag, s))
        if s:
            p.wait("vector", *[("ln_T", tag, s - 1, k) for k in range(KD)])
        for j in range(GPS):
            p.tensor_scalar(self.xn[:, j, :], self.X[:, GPS * s + j, :], self.mv[:, j, 0:1],
                            self.rstd[:, j:j + 1], ALU.subtract, ALU.mult, done=("ln_xn", tag, s, j))

    def normalise(self, s, ready):
        for j in range(GPS):
            self.take_stats(s, j, ready)
        self.scale(s)

    def turn(self, s, banks, free, ks=range(KD)):
        p, tag = self.p, self.tag
        for k in ks:
            bank, bank_free = banks.take(both("xT", tag, s, k))
            p.wait("tensor", ("ln_xn", tag, s, GPS - 1), *bank_free)
            for j in range(GPS):
                p.transpose(bank[:, j * P:(j + 1) * P], self.xn[:, j, k * P:(k + 1) * P],
                            self.consts["ident"][:, :], ("ln_T", tag, s, k) if j == GPS - 1 else None)
            self.dest.fill(p, bank[:, :], lambda t, k=k: self.at(t, s, k), ("xT", tag, s, k),
                           [("ln_T", tag, s, k)], free)

    def at(self, t, s, k):
        return t[:, k, :] if t.shape[2] == GPS * P else t[:, k, s * GPS * P:(s + 1) * GPS * P]


def cross_attention(p, nc, tag, X, ctx, consts, mats, biases, x_ready, load_x):
    with ExitStack() as stack:
        def sb(name, shape, dt=F32):
            return stack.enter_context(nc.sbuf_tensor(f"{name}_{tag}", shape, dt))

        def split(name, shape):
            return Split(nc, stack, f"{name}_{tag}", shape)


        xT = split("xT", [P, KD, GPS * P])
        ln = LayerNorm(p, nc, stack, tag, X, consts, xT)
        q32 = sb("q32", [P, GPS * P])
        qT = [split(f"qT{i}", [P, KD, GPS * P]) for i in range(2)]
        q_diag = [split(f"q_diag{i}", [P, KD, HPH * T]) for i in range(2)]
        ctx_in = [sb(f"ctx_in{i}", [P, KD, BPG, S]) for i in range(2)]
        ctxT = [split(f"ctxT{i}", [P, KD, S_EVEN]) for i in range(3)]
        kT = [split(f"kT{i}", [P, KD, S_EVEN]) for i in range(2)]
        v = [split(f"v{i}", [P, CHUNKS, D]) for i in range(3)]
        neg_max = [sb(f"neg_max{i}", [P, HG]) for i in range(2)]
        sums = [sb(f"sums{i}", [P, HG]) for i in range(2)]
        inv = [sb(f"inv{i}", [P, HG]) for i in range(2)]
        prob = [sb(f"prob{i}", [P, HG, S]) for i in range(3)]
        probT = [split(f"probT{i}", [P, CHUNKS, HG * P]) for i in range(2)]
        attn32 = [sb(f"attn32{i}", [P, KD, P]) for i in range(2)]
        masked = sb("masked", [P, KD, HPH, T])
        ctx_last = split("ctx_last", [P, KD, BPG])

        loader = Weights(p, nc, stack, tag)
        flat = [t[:, :, :].rearrange("p a b -> p (a b)") for t in (*prob, attn32[0], attn32[1])]
        w = {n: loader.load(n, mats[n], [t]) if i < 3 else loader.load(n, mats[n], flat[3:])
             for i, (n, t) in enumerate(zip([n for n in "qkvo" if n in mats], flat))}
        matrices = list(w.values())
        v_is_k, v_banks = "v" not in mats, {}
        w.setdefault("k", w["q"])
        w.setdefault("v", w["q"])
        all_weights = [r for m in w.values() for r in m.ready]
        v_row = sb("v_row", [BPG, D])
        v_last = [sb(f"v_last{i}", [P, KD, BPG]) for i in range(2)]
        p_last = sb("p_last", [P, HG, BPG])
        last_spread = sb("last_spread", [P, HG * BPG, T])
        last_part = sb("last_part", [P, KD, BPG, T])
        attnT = split("attnT", [P, KD, P])

        ps_score = stack.enter_context(nc.psum_tensor(f"ps_score_{tag}", [P, HG, 512], F32))
        turn_banks = Banks([stack.enter_context(nc.psum_tensor(f"ps_pT{i}_{tag}", [P, 512], F32))
                             for i in range(2)])
        banks = Banks([stack.enter_context(nc.psum_tensor(f"ps_{i}_{tag}", [P, 512], F32)) for i in range(2)])

        for i in range(3):
            for t in (ctxT[i].hi, ctxT[i].lo):
                p.memset(t[:, :, S:S_EVEN].bitcast(F32), 0.0, ("pad", tag, i, t.name))
        pads = [("pad", tag, i, t.name) for i in range(3) for t in (ctxT[i].hi, ctxT[i].lo)]
        bias_ready = []
        if biases:
            bq4 = sb("bq4", [P, KD])
            p.wait("vector", ("const_in",))
            p.tensor_scalar(bq4[:, :], biases["q"][:, :], XD ** -0.5, None, ALU.mult, done=("bq4", tag))
            bias_ready = [("bq4", tag)]

        def load_ctx(g):
            if g >= 2:
                p.wait("sync", *both("ctx", tag, (g - 1) * BPG - 1))
                if not v_is_k:
                    p.wait("sync", *both("ctx_last", tag, g - 2))
            p.dma(ctx_in[g % 2][:, :, :, :], ctx[g], (f"ctx_in{g % 2}", tag, g))

        def split_ctx(b):
            g, j = b // BPG, b % BPG
            free = [("k_ps", tag, b - 3, 1), *([] if v_is_k else [("v_ps", tag, b - 3)])] if b >= 3 else []
            ctxT[b % 3].fill(p, ctx_in[g % 2][:, :, j, :], lambda t: t[:, :, 0:S], ("ctx", tag, b),
                             [(f"ctx_in{g % 2}", tag, g)], free, lo_engine="gpsimd")

        def project_k(b, m):
            bank, free = banks.take(both("k", tag, b, m))
            p.wait("tensor", *both("ctx", tag, b), *free, *all_weights, *pads)
            p.split_product(bank[:, 0:S_EVEN], lambda k: part(w["k"], k, m * P, (m + 1) * P),
                            lambda k: ctxT[b % 3].pair(lambda t: t[:, k, :]), KD, ("k_ps", tag, b, m))
            old = [("score", tag, b - 2, HG - 1), *([("v_T", tag, b - 2, 1), ("v_col", tag, b - 2)] if v_is_k else [])] if b >= 2 else []
            kT[b % 2].fill(p, bank[:, 0:S_EVEN], lambda t: t[:, m, :], ("k", tag, b, m),
                           [("k_ps", tag, b, m)], old, biases["k"][:, m:m + 1] if biases else None)

        def project_v(b):
            bank, free = turn_banks.take(both("v", tag, b))
            p.wait("tensor", *both("ctx", tag, b), *free)
            for c in range(CHUNKS):
                p.split_product(bank[:, c * D:(c + 1) * D],
                                lambda k: ctxT[b % 3].pair(lambda t: t[:, k, c * P:(c + 1) * P]),
                                lambda k: part(w["v"], k, 0, D), KD,
                                ("v_ps", tag, b) if c == CHUNKS - 1 else None)
            v_banks[0] = v_banks[1] = bank[:, :].rearrange("p (c d) -> p c d", d=D)

        def turn_k(b):
            for i, src in enumerate((kT[b % 2].hi, kT[b % 2].lo)):
                bank, free = turn_banks.take((both("v", tag, b)[i],))
                p.wait("tensor", *both("k", tag, b, KD - 1), *free)
                for c in range(CHUNKS):
                    for m in range(KD):
                        p.transpose(bank[:, c * D + m * P:c * D + (m + 1) * P],
                                    src[:, m, c * P:(c + 1) * P].bitcast(F32), consts["ident"][:, :],
                                    ("v_T", tag, b, i) if (c, m) == (CHUNKS - 1, KD - 1) else None)
                v_banks[i] = bank[:, :].rearrange("p (c d) -> p c d", d=D)

        def keep_v_col(b):
            g, j = b // BPG, b % BPG
            p.wait("gpsimd", *both("k", tag, b, KD - 1))
            if g >= 2:
                p.wait("gpsimd", ("last_part", tag, g - 2))
            hi, lo = kT[b % 2].pair(lambda t: t[:, :, S - 1].bitcast(F32))
            p.tensor_tensor(v_last[g % 2][:, :, j], hi, lo, ALU.add, ("v_col", tag, b), "gpsimd")

        def keep_v_hi(b):
            p.wait("scalar", ("v_T", tag, b, 0) if v_is_k else ("v_ps", tag, b))
            if b >= 3:
                p.wait("scalar", ("pv", tag, b - 3))
            p.activation(v[b % 3].hi[:, :, :], v_banks[0], ACT.Copy, ("hi_v", tag, b))

        def keep_v_lo(b):
            if b >= 3:
                p.wait("vector", ("pv", tag, b - 3))
            if v_is_k:
                p.wait("vector", ("v_T", tag, b, 1))
                p.copy(v[b % 3].lo[:, :, :], v_banks[1], ("lo_v", tag, b))
            else:
                p.wait("vector", ("hi_v", tag, b))
                p.tensor_tensor(v[b % 3].lo[:, :, :], v_banks[1], v[b % 3].hi[:, :, :].bitcast(F32), ALU.subtract,
                                ("lo_v", tag, b))

        def split_last(g):
            old = [("last_v_ps", tag, g - 1)] if g else []
            ctx_last.fill(p, ctx_in[g % 2][:, :, :, S - 1], lambda t: t[:, :, :], ("ctx_last", tag, g),
                          [(f"ctx_in{g % 2}", tag, g)], old, lo_engine="gpsimd")

        def project_last(g):
            bank, free = turn_banks.take((("v_row", tag, g),))
            p.wait("tensor", *both("ctx_last", tag, g), *free)
            p.split_product(bank[0:BPG, 0:D], lambda k: ctx_last.pair(lambda t: t[:, k, :]),
                            lambda k: part(w["v"], k, 0, D), KD, ("last_v_ps", tag, g))
            p.wait("scalar", ("last_v_ps", tag, g))
            if g:
                p.wait("scalar", ("v_last_T", tag, g - 1))
            p.activation(v_row[:, :], bank[0:BPG, 0:D], ACT.Copy, ("v_row", tag, g))

        def turn_last(g):
            bank, free = turn_banks.take((("v_last", tag, g),))
            p.wait("tensor", ("v_row", tag, g), *free)
            for m in range(KD):
                p.transpose(bank[:, m * BPG:(m + 1) * BPG], v_row[:, m * P:(m + 1) * P],
                            consts["ident"][0:BPG, 0:BPG], ("v_last_T", tag, g) if m == KD - 1 else None)
            p.wait("scalar", ("v_last_T", tag, g))
            if g >= 2:
                p.wait("scalar", ("last_part", tag, g - 2))
            p.activation(v_last[g % 2][:, :, :], bank[:, 0:KD * BPG].rearrange("p (m b) -> p m b", b=BPG), ACT.Copy,
                         ("v_last", tag, g))

        def keep_last(b):
            g, j = b // BPG, b % BPG
            p.wait("gpsimd", ("prob", tag, b))
            if g:
                p.wait("gpsimd", ("last_spread", tag, g - 1))
            p.copy(p_last[:, :, j], prob[b % 3][:, :, S - 1], ("p_last", tag, b), "gpsimd")

        def spread_last(g):
            shape = [P, HG * BPG, T]
            p.wait("gpsimd", ("p_last", tag, g * BPG + BPG - 1))
            if g:
                p.wait("gpsimd", ("last_ps", tag, g - 1))
            p.tensor_tensor(last_spread[:, :, :], p_last[:, :, :].rearrange("p h b -> p (h b)").unsqueeze(2).to_broadcast(shape),
                            consts["same_query"][:, :].unsqueeze(1).to_broadcast(shape), ALU.mult,
                            ("last_spread", tag, g), "gpsimd")

        def add_last(g):
            bank, free = banks.take((("last_part", tag, g),))
            p.wait("tensor", ("last_spread", tag, g), *free)
            for m in range(KD):
                for n in range(HG // KD):
                    hg = m * (HG // KD) + n
                    last = n == HG // KD - 1
                    p.matmul(bank[:, m * P:(m + 1) * P], consts["head_sum"][:, n * P:(n + 1) * P],
                             last_spread[:, hg * BPG:(hg + 1) * BPG, :], start=n == 0, stop=last,
                             done=("last_ps", tag, g) if last and m == KD - 1 else None)
            shape = [P, KD, BPG, T]
            p.wait("vector", ("last_ps", tag, g), ("v_col", tag, g * BPG + BPG - 1) if v_is_k else ("v_last", tag, g))
            p.tensor_tensor(last_part[:, :, :, :], bank[:, 0:KD * P].rearrange("p (m b q) -> p m b q", b=BPG, q=T),
                            v_last[g % 2][:, :, :].unsqueeze(3).to_broadcast(shape), ALU.mult, ("last_part", tag, g))
            p.wait("vector", ("last_part", tag, g), ("attn32", tag, g * BPG + BPG - 1))
            whole = attn32[g % 2][:, :, :].rearrange("p m n -> p (m n)")
            p.tensor_tensor(whole, whole, last_part[:, :, :, :].rearrange("p m b q -> p (m b q)"), ALU.add,
                            ("attn_sum", tag, g))

        def project_q(s, ms=range(KD)):
            for m in ms:
                bank, free = banks.take((("q32", tag, s, m),))
                p.wait("tensor", *[r for k in range(KD) for r in both("xT", tag, s, k)], *free, *all_weights)
                p.split_product(bank[:, :], lambda k: part(w["q"], k, m * P, (m + 1) * P),
                                lambda k: xT.pair(lambda t: t[:, k, :]), KD, ("q_ps", tag, s, m))
                p.wait("vector", ("q_ps", tag, s, m), *bias_ready)
                if (s, m) != (0, 0):
                    p.wait("vector", *both("q", tag, *((s, 0) if m else (s - 1, 1))))
                p.tensor_scalar(q32[:, :], bank[:, :], XD ** -0.5, bq4[:, m:m + 1] if biases else 0.0,
                                ALU.mult, ALU.add, done=("q32", tag, s, m))
                old = [("q_diag_lo", tag, (s - 1) * BPS - 1)] if s >= 2 else []
                qT[s % 2].fill(p, q32[:, :], lambda t: t[:, m, :], ("q", tag, s, m), [("q32", tag, s, m)], old)

        def spread_q(b):
            s, j = b // BPS, b % BPS
            p.wait("gpsimd", *[r for m in range(KD) for r in both("q", tag, s, m)], ("const_in",))
            if b >= 2:
                p.wait("gpsimd", ("score", tag, b - 2, HG - 1))
            shape = [P, KD, HPH, T]
            mask = consts["head_rows"][:, :].unsqueeze(1).unsqueeze(3).to_broadcast(shape)
            for name, src, dst in (("q_diag_hi", qT[s % 2].hi, q_diag[b % 2].hi),
                                   ("q_diag_lo", qT[s % 2].lo, q_diag[b % 2].lo)):
                src = src[:, :, j * T:(j + 1) * T].bitcast(F32).unsqueeze(2).to_broadcast(shape)
                p.tensor_tensor(dst[:, :, :].rearrange("p m (h q) -> p m h q", q=T), src, mask, ALU.mult,
                                done=(name, tag, b), engine="gpsimd")

        def scores(b):
            for hg in range(HG):
                m, c0 = hg // 2, hg % 2 * P
                p.wait("tensor", ("q_diag_lo", tag, b), *both("k", tag, b, m))
                if b:
                    p.wait("tensor", ("exp", tag, b - 1, hg))
                p.split_product(ps_score[:, hg, 0:S_EVEN], lambda k: q_diag[b % 2].pair(lambda t: t[:, m, c0:c0 + P]),
                                lambda k: kT[b % 2].pair(lambda t: t[:, m, :]), 1, ("score", tag, b, hg))

        def find_max(b, n):
            p.wait("vector", ("score", tag, b, 2 * n + 1))
            if b >= 2:
                p.wait("vector", ("exp", tag, b - 2, HG - 1))
            p.reduce(neg_max[b % 2][:, 2 * n:2 * n + 2], ps_score[:, 2 * n:2 * n + 2, 0:S], ALU.max,
                     ("neg_max", tag, b, n), negate=True)

        def exponentials(b, n):
            if b >= 2:
                p.wait("scalar", ("inv", tag, b - 2))
            if b >= 3:
                p.wait("scalar", ("prob_T", tag, b - 3, CHUNKS - 1), ("p_last", tag, b - 3))
            p.wait("scalar", ("neg_max", tag, b, n))
            for hg in (2 * n, 2 * n + 1):
                p.activation(prob[b % 3][:, hg, :], ps_score[:, hg, 0:S], ACT.Exp, ("exp", tag, b, hg),
                             bias=neg_max[b % 2][:, hg:hg + 1], accum_out=sums[b % 2][:, hg:hg + 1])

        def normalise(b):
            p.wait("vector", ("exp", tag, b, HG - 1))
            if b >= 2:
                p.wait("vector", ("prob", tag, b - 2))
            p.reciprocal(inv[b % 2][:, :], sums[b % 2][:, :], ("inv", tag, b))
            p.wait("gpsimd", ("inv", tag, b))
            t = prob[b % 3][:, :, :]
            p.tensor_tensor(t, t, inv[b % 2][:, :].unsqueeze(2).to_broadcast([P, HG, S]), ALU.mult,
                            ("prob", tag, b), "gpsimd")

        def turn_prob(b, c):
            bank, free = turn_banks.take(both("pT", tag, b, c))
            p.wait("tensor", ("prob", tag, b), *free)
            for hg in range(HG):
                p.transpose(bank[:, hg * P:(hg + 1) * P], prob[b % 3][:, hg, c * P:(c + 1) * P],
                            consts["ident"][:, :], ("prob_T", tag, b, c) if hg == HG - 1 else None)
            old = [("pv", tag, b - 2)] if b >= 2 else []
            probT[b % 2].fill(p, bank[:, :], lambda t: t[:, c, :], ("pT", tag, b, c),
                              [("prob_T", tag, b, c)], old)

        def weigh_v(b):
            g, j = b // BPG, b % BPG
            bank, free = banks.take((("masked", tag, b),))
            p.wait("tensor", *free, *[r for c in range(CHUNKS) for r in both("pT", tag, b, c)],
                   *both("v", tag, b))
            for m in range(KD):
                cols = lambda t, c: t[:, c, m * P:(m + 1) * P]
                rows = lambda t, c: t[:, c, m * HPH * T:(m + 1) * HPH * T]
                p.split_product(bank[:, m * HPH * T:(m + 1) * HPH * T], lambda c: v[b % 3].pair(lambda t: cols(t, c)),
                                lambda c: probT[b % 2].pair(lambda t: rows(t, c)), CHUNKS,
                                ("pv", tag, b) if m == KD - 1 else None)
            shape = [P, KD, HPH, T]
            p.wait("vector", ("pv", tag, b), ("const_in",))
            if b:
                p.wait("vector", ("attn32", tag, b - 1))
            p.tensor_tensor(masked[:, :, :, :], bank[:, :].rearrange("p (m h q) -> p m h q", m=KD, q=T),
                            consts["head_rows"][:, :].unsqueeze(1).unsqueeze(3).to_broadcast(shape), ALU.mult,
                            done=("masked", tag, b))
            p.wait("vector", ("masked", tag, b))
            if g >= 2:
                p.wait("vector", *both("attn", tag, g - 2))
            p.reduce(attn32[g % 2][:, :, j * T:(j + 1) * T], masked[:, :, :, :].rearrange("p m h q -> p m q h"),
                     ALU.add, ("attn32", tag, b))

        def split_attn(g):
            old = [("o_ps", tag, g - 1)] if g else []
            if biases:
                for m in range(KD):
                    attnT.fill(p, attn32[g % 2][:, m, :], lambda t: t[:, m, :],
                               ("attn" if m == KD - 1 else "attn_0", tag, g),
                               [("attn_sum", tag, g)], old, biases["v"][:, m:m + 1])
            else:
                attnT.fill(p, attn32[g % 2][:, :, :], lambda t: t[:, :, :], ("attn", tag, g),
                           [("attn_sum", tag, g)], old)

        def project_out(g):
            bank, free = banks.take((("x_out", tag, g),))
            p.wait("tensor", *both("attn", tag, g), *free)
            p.split_product(bank[:, 0:D], lambda k: attnT.pair(lambda t: t[:, k, :]),
                            lambda k: part(w["o"], k, 0, D), KD, ("o_ps", tag, g))
            p.wait("vector", ("o_ps", tag, g))
            p.tensor_tensor(X[:, g, :], X[:, g, :], bank[:, 0:D], ALU.add, done=("x_out", tag, g))
            if biases:
                p.wait("gpsimd", ("x_out", tag, g))
                p.tensor_tensor(X[:, g, :], X[:, g, :], biases["o"][:, :], ALU.add, ("x_bias", tag, g), "gpsimd")

        def free_xT(s):
            return [("q_ps", tag, s - 1, KD - 1)] if s else []

        load_ctx(0)
        load_ctx(1)
        if load_x:
            for s in range(1, SG):
                load_x(s)
        ln.normalise(0, [x_ready(0)])
        loader.split(*matrices)
        ln.turn(0, banks, free_xT(0))
        project_q(0)
        for b in range(2):
            split_ctx(b)
            spread_q(b)
        for m in range(KD):
            project_k(0, m)
        for i in range(B + BPG):
            now, after, before = i < B, i + 1 < B, 2 <= i < B + 2
            if before:
                for n in range(CHUNKS):
                    turn_prob(i - 2, n)
            for n in range(2):
                if after:
                    project_k(i + 1, n)
                if i + 2 < B and n == 0:
                    split_ctx(i + 2)
                    if (i + 3) % BPG == 0 and (i + 3) // BPG + 1 < G:
                        load_ctx((i + 3) // BPG + 1)
            if now:
                scores(i)
                if v_is_k:
                    turn_k(i)
                    keep_v_col(i)
                else:
                    project_v(i)
                keep_v_hi(i)
                for n in range(2):
                    find_max(i, n)
                    exponentials(i, n)
                keep_v_lo(i)
            if i + 2 < B:
                spread_q(i + 2)
            g, j = i // BPG, i % BPG
            if now and j == 2 and not v_is_k:
                project_last(g)
            if j == 3:
                if now and not v_is_k:
                    turn_last(g)
                if g >= 1:
                    project_out(g - 1)
            if j == 2 and g >= 1:
                add_last(g - 1)
                split_attn(g - 1)
            s = i // BPS + 1
            if s < SG and i % BPS in (4, 5):
                ln.turn(s, banks, free_xT(s), [i % BPS - 4])
            if s < SG and i % BPS in (8, 9):
                project_q(s, [i % BPS - 8])
            if before:
                weigh_v(i - 2)
            if now:
                normalise(i)
            if now:
                if j == 1 and not v_is_k:
                    split_last(g)
                keep_last(i)
                if j == BPG - 1:
                    spread_last(g)
            if s < SG and i % BPS in (1, 2):
                for k in range(GPS // 2):
                    ln.take_stats(s, (i % BPS - 1) * (GPS // 2) + k, [x_ready(s)])
            if s < SG and i % BPS == 3:
                ln.scale(s)
        p.run()


class HeadOrder:

    def __init__(self, R, head, cells):
        self.R, self.NH = R, H // R
        self.cells = cells
        self.column = {head(r, n): (r * self.NH + n) * T for r in range(R) for n in range(self.NH)}


def attend(p, tag, g, q_k, order, tiles, scale, bound, ready):
    R, NH, t = order.R, order.NH, tiles
    score = t["score"](g)
    p.wait("tensor", *ready, *t["score_free"](g))
    products = [(b, r, *x) for x in q_k(g) for b in range(BPG) for r in range(R)]
    for i, (b, r, heads, q, k) in enumerate(products):
        p.matmul(score[b * T:(b + 1) * T, r, heads, :], q(b, r), k(b, r),
                 done=("s_score", tag, g) if i == len(products) - 1 else None)
    src, grid = score, [P, R, NH, T]
    cell = lambda a: a.rearrange("p (r n q) -> p r n q", r=R, q=T)
    stat = lambda a: a.rearrange("p (r n) -> p r n", r=R)
    p.wait("vector", ("s_score", tag, g))
    e = g % 2
    if g >= 2:
        p.wait("vector", ("s_exp", tag, g - 2), ("s_probT", tag, g - 2), ("s_out", tag, g - 2))
    if bound is not None:
        for r in range(R):
            p.scalar_tensor_tensor(cell(t["shifted"][e][:, :])[:, r], score[:, r], scale,
                                   bound.unsqueeze(1).to_broadcast([P, NH, T]), ALU.mult, ALU.min,
                                   ("s_masked", tag, g, r))
        p.wait("vector", ("s_masked", tag, g, R - 1))
        src, scale = cell(t["shifted"][e][:, :]), 1.0
    p.reduce(stat(t["neg_max"][e][:, :]), src, ALU.max, ("s_max", tag, g), negate=True)
    p.wait("vector", ("s_max", tag, g))
    p.tensor_tensor(cell(t["shifted"][e][:, :]), src,
                    stat(t["neg_max"][e][:, :]).unsqueeze(3).to_broadcast(grid), ALU.add, ("s_shift", tag, g))
    p.wait("scalar", ("s_shift", tag, g))
    p.activation(t["prob"][e][:, :], t["shifted"][e][:, :], ACT.Exp, ("s_exp", tag, g), scale=scale)
    p.wait("vector", ("s_exp", tag, g))
    if g >= 2:
        p.wait("vector", ("s_pv", tag, g - 2))
    p.do("vector", lambda eng: eng.transpose(t["probT"][e][:, :], t["prob"][e][:, :]), ("s_probT", tag, g))
    p.reduce(t["sums"][e][:, :], t["prob"][e][:, :].rearrange("p (h q) -> p h q", q=T), ALU.add, ("s_sum", tag, g))
    p.wait("vector", ("s_sum", tag, g))
    own = order.cells(t["inv"][e][:, :])
    sums = stat(t["sums"][e][:, :])
    if len(own.shape) == 4:
        sums = sums.rearrange("p r (m e) -> p r m e", m=own.shape[2])
    p.reciprocal(own, sums, ("s_inv", tag, g))


def weigh_self(p, tag, g, v, dv, order, tiles):
    out, free = tiles["out"](g), tiles["out_free"](g)
    probT = tiles["probT"][g % 2]
    p.wait("tensor", ("s_probT", tag, g), *free)
    for h in range(H):
        c0 = order.column[h]
        for b in range(BPG):
            rows = slice(b * T, (b + 1) * T)
            p.matmul(out[rows, h, :], probT[rows, c0:c0 + T], v(g)[rows, h * dv:(h + 1) * dv],
                     done=("s_pv", tag, g) if (h, b) == (H - 1, BPG - 1) else None)


def self_attention_0(p, nc, X, consts, mats):
    tag = "s0"
    with ExitStack() as stack:
        def sb(name, shape, dt=F32):
            return stack.enter_context(nc.sbuf_tensor(f"{name}_{tag}", shape, dt))

        R, PAIR = P // T, T // XD
        loader = Weights(p, nc, stack, tag)
        xT = [Split(nc, stack, f"xT{i}_{tag}", [P, KD, GPS * P]) for i in range(2)]
        ln = LayerNorm(p, nc, stack, tag, X, consts, xT[0])
        qT = [sb(f"qT{i}", [P, KD, GPS * P]) for i in range(2)]
        kT = [sb(f"kT{i}", [P, KD, PAIR, GPS * P]) for i in range(2)]
        v = [sb(f"v{i}", [P, D]) for i in range(2)]
        t = {n: [sb(f"{n}{i}", [P, H * T]) for i in range(2)] for n in ("shifted", "prob", "probT")}
        t |= {n: [sb(f"{n}{i}", [P, H]) for i in range(2)] for n in ("neg_max", "sums", "inv")}
        add = [sb(f"add{i}", [P, D]) for i in range(2)]
        w = {n: loader.load(n, mats[n], [t[b][0]]) for n, b in zip("qkv", ("shifted", "prob", "probT"))}
        ready_w = [r for m in w.values() for r in m.ready]
        ps_score = stack.enter_context(nc.psum_tensor(f"ps_score_{tag}", [P, R, 512], F32))
        ps_out = stack.enter_context(nc.psum_tensor(f"ps_out_{tag}", [P, 2, 512], F32))
        banks = Banks([stack.enter_context(nc.psum_tensor(f"ps_{i}_{tag}", [P, 512], F32)) for i in range(2)])
        order = HeadOrder(R, lambda r, n: n // PAIR * HPH + r * PAIR + n % PAIR,
                          lambda a: a.rearrange("p (m r e) -> p r m e", r=R, m=KD))
        t["score"] = lambda g: ps_score[:, :, 0:order.NH * T].rearrange("p r (n q) -> p r n q", q=T)
        t["score_free"] = lambda g: [("s_shift", tag, g - 1)] if g else []
        t["out"] = lambda g: ps_out[:, g % 2, 0:D].rearrange("p (h d) -> p h d", d=XD)
        t["out_free"] = lambda g: [("s_out", tag, g - 2)] if g >= 2 else []
        vg = lambda g: v[g % 2]

        def q_k(g):
            q, k, c0 = qT[g // GPS % 2], kT[g // GPS % 2], g % GPS * P
            rows = lambda r: slice(r * T, (r + 1) * T)
            return [(slice(m * PAIR, (m + 1) * PAIR),
                     lambda b, r, m=m: q[rows(r), m, c0 + b * T:c0 + (b + 1) * T],
                     lambda b, r, m=m: k[rows(r), m, :, c0 + b * T:c0 + (b + 1) * T]) for m in range(KD)]

        def project(s, name, m):
            kind = f"s_{name}T"
            bank, free = banks.take(((kind, tag, s, m),))
            p.wait("tensor", *[r for k in range(KD) for r in both("xT", tag, s, k)], *free, *ready_w)
            p.split_product(bank[:, :], lambda k: part(w[name], k, m * P, (m + 1) * P),
                            lambda k: xT[s % 2].pair(lambda a: a[:, k, :]), KD, (kind + "_ps", tag, s, m))
            p.wait("scalar", (kind + "_ps", tag, s, m))
            if s >= 2:
                p.wait("scalar", ("s_score", tag, (s - 1) * GPS - 1))
            if name == "q":
                p.activation(qT[s % 2][:, m, :], bank[:, :], ACT.Copy, (kind, tag, s, m))
                return
            for e in range(PAIR):
                p.activation(kT[s % 2][:, m, e, :], bank[:, :], ACT.Copy,
                             (kind, tag, s, m) if e == PAIR - 1 else None, scale=consts["of_pair"][:, e:e + 1])

        def project_v(g):
            s, j = g // GPS, g % GPS
            bank, free = banks.take((("s_v", tag, g),))
            p.wait("tensor", *[r for k in range(KD) for r in both("xT", tag, s, k)], *free, *ready_w)
            p.split_product(bank[:, 0:D], lambda k: xT[s % 2].pair(lambda a: a[:, k, j * P:(j + 1) * P]),
                            lambda k: part(w["v"], k, 0, D), KD, ("s_v_ps", tag, g))
            p.wait("scalar", ("s_v_ps", tag, g))
            if g >= 2:
                p.wait("scalar", ("s_pv", tag, g - 2))
            p.activation(v[g % 2][:, :], bank[:, 0:D], ACT.Copy, ("s_v", tag, g))

        def finish(g):
            shape = [P, H, XD]
            p.wait("vector", ("s_pv", tag, g), ("s_inv", tag, g))
            if g >= 2:
                p.wait("vector", ("s_x", tag, g - 2))
            p.tensor_tensor(add[g % 2][:, :].rearrange("p (h d) -> p h d", d=XD), t["out"](g),
                            t["inv"][g % 2][:, :].unsqueeze(2).to_broadcast(shape), ALU.mult, ("s_out", tag, g))
            p.wait("gpsimd", ("s_out", tag, g))
            p.tensor_tensor(X[:, g, :], X[:, g, :], add[g % 2][:, :], ALU.add, ("s_x", tag, g), "gpsimd")

        def prepare(s):
            free = [("s_qT_ps", tag, s - 2, KD - 1), ("s_kT_ps", tag, s - 2, KD - 1),
                    ("s_v_ps", tag, (s - 1) * GPS - 1)] if s >= 2 else []
            ln.dest = xT[s % 2]
            ln.turn(s, banks, free)

        def scores(g):
            s = g // GPS
            ready = [(f"s_{n}T", tag, s, m) for n in "qk" for m in range(KD)]
            attend(p, tag, g, q_k, order, t, XD ** -0.5, None, ready)

        ln.normalise(0, [])
        loader.split(*w.values())
        prepare(0)
        parts = [(n, m) for n in "qk" for m in range(KD)]
        for n, m in parts:
            project(0, n, m)
        ln.normalise(1, [])
        for g in range(G + 1):
            s, j = g // GPS, g % GPS
            if g < G:
                project_v(g)
                scores(g)
            if s + 1 < SG:
                if j == 0:
                    prepare(s + 1)
                if j in (1, 2):
                    for m in range(KD):
                        project(s + 1, "qk"[j - 1], m)
            if g:
                p.wait("tensor", ("s_v", tag, g - 1))
                weigh_self(p, tag, g - 1, vg, XD, order, t)
                finish(g - 1)
            if s + 2 < SG:
                ln.take_stats(s + 2, j)
                if j == GPS - 1:
                    ln.scale(s + 2)
        p.run()


def experts(p, nc, X, consts, mats):
    tag = "moe"
    with ExitStack() as outer:
        xT = Split(nc, outer, f"xT_{tag}", [P, KD, B * T])
        keep = lambda n, shape, dt=F32: outer.enter_context(nc.sbuf_tensor(f"{n}_{tag}", shape, dt))
        share, logit, prob, hot = (keep(n, [P, G, E]) for n in ("share", "logit", "prob", "hot"))
        top = keep("top", [P, G, 8])
        which = keep("which", [P, G, 8], U32)
        which_f = keep("which_f", [P, G, 8])
        stat = keep("stat", [P, G])
        WN = KD * HID
        names = ("gate", "up", "down")
        stage = keep("w_stage", [P, 3, WN])
        w = [{n: Split(nc, outer, f"{n}{i}_{tag}", [P, WN]) for n in names} for i in range(2)]

        def route():
            spread = lambda a: a.unsqueeze(2).to_broadcast([P, G, E])
            p.wait("vector", ("logit", SG - 1))
            p.reduce(stat[:, :], logit[:, :, :], ALU.max, ("route", 0), negate=True)
            p.wait("vector", ("route", 0))
            p.tensor_tensor(logit[:, :, :], logit[:, :, :], spread(stat[:, :]), ALU.add, ("route", 1))
            p.wait("scalar", ("route", 1))
            p.activation(prob[:, :, :], logit[:, :, :], ACT.Exp, ("route_exp",))
            p.wait("vector", ("route_exp",))
            p.reduce(stat[:, :], prob[:, :, :], ALU.add, ("route", 2))
            p.wait("vector", ("route", 2))
            p.reciprocal(stat[:, :], stat[:, :], ("route", 3))
            p.wait("vector", ("route", 3))
            p.tensor_tensor(prob[:, :, :], prob[:, :, :], spread(stat[:, :]), ALU.mult, ("route", 4))
            p.wait("vector", ("route", 4))
            yield
            for g in range(G):
                p.do("vector", lambda e, g=g: e.max(top[:, g, :], prob[:, g, :]), ("route_top", g))
            p.wait("vector", ("route_top", G - 1))
            yield
            for g in range(G):
                p.do("vector", lambda e, g=g: e.max_index(which[:, g, :], top[:, g, :], prob[:, g, :]),
                     ("route_which", g))
            p.wait("vector", ("route_which", G - 1))
            yield
            p.copy(which_f[:, :, 0:2], which[:, :, 0:2], ("route", 5))
            p.tensor_tensor(stat[:, :], top[:, :, 0], top[:, :, 1], ALU.add, ("route", 6))
            p.wait("vector", ("route", 6))
            p.reciprocal(stat[:, :], stat[:, :], ("route", 7))
            p.wait("vector", ("route", 7))
            p.tensor_tensor(top[:, :, 0:2], top[:, :, 0:2], stat[:, :].unsqueeze(2).to_broadcast([P, G, 2]),
                            ALU.mult, ("route", 8))
            p.wait("vector", ("route", 8), ("const_in",))
            number = consts["numbers"][:, :].unsqueeze(1).to_broadcast([P, G, E])
            for n, dst in enumerate((share[:, :, :], hot[:, :, :])):
                p.tensor_tensor(dst, number, spread(which_f[:, :, n]), ALU.is_equal, ("route", 9 + 2 * n))
                p.wait("vector", ("route", 9 + 2 * n))
                p.tensor_tensor(dst, dst, spread(top[:, :, n]), ALU.mult, ("route", 10 + 2 * n))
            p.wait("vector", ("route", 12))
            p.tensor_tensor(share[:, :, :], share[:, :, :], hot[:, :, :], ALU.add, ("share",))
            yield

        def load(e):
            for i, n in enumerate(names):
                if e:
                    p.wait("sync", *both(f"w_{n}", e - 1))
                p.dma(stage[:, i, :], mats[n][e].rearrange("p a b -> p (a b)"), (f"w_{n}_in", e))

        def split_w(e, i):
            n = names[i]
            old = [("y_ps", (e - 1) * SG - 1, GPS - 1)] if e >= 2 else []
            w[e % 2][n].fill(p, stage[:, i, :], lambda t: t[:, :], (f"w_{n}", e), [(f"w_{n}_in", e)], old)

        with ExitStack() as stack:
            def sb(name, shape, dt=F32):
                return stack.enter_context(nc.sbuf_tensor(f"{name}_{tag}", shape, dt))

            loader = Weights(p, nc, stack, tag)
            router = loader.load("router", mats["router"], [sb("router_in", [P, KD * E])])
            loader.split(router)
            ln = LayerNorm(p, nc, stack, tag, X, consts, xT)
            logitT = [sb(f"logitT{i}", [E, GPS * P]) for i in range(2)]
            banks = Banks([stack.enter_context(nc.psum_tensor(f"ps_{i}_{tag}", [P, 512], F32)) for i in range(4)])

            def logits(s):
                bank, free = banks.take((("logitT", s),))
                p.wait("tensor", *[r for k in range(KD) for r in both("xT", tag, s, k)], *free, *router.ready)
                p.split_product(bank[0:E, :], lambda k: part(router, k, 0, E),
                                lambda k: xT.pair(lambda t: t[:, k, s * GPS * P:(s + 1) * GPS * P]), KD,
                                ("logit_ps", s))
                p.wait("scalar", ("logit_ps", s))
                if s >= 2:
                    p.wait("scalar", ("logit_T", s - 2))
                p.activation(logitT[s % 2][:, :], bank[0:E, :], ACT.Copy, ("logitT", s))
                bank, free = banks.take((("logit", s),))
                p.wait("tensor", ("logitT", s), *free)
                for j in range(GPS):
                    p.transpose(bank[:, j * E:(j + 1) * E], logitT[s % 2][:, j * P:(j + 1) * P],
                                consts["ident"][0:E, 0:E], ("logit_T", s) if j == GPS - 1 else None)
                p.wait("scalar", ("logit_T", s))
                p.activation(logit[:, s * GPS:(s + 1) * GPS, :],
                             bank[:, 0:GPS * E].rearrange("p (g e) -> p g e", e=E), ACT.Copy, ("logit", s))

            load(0)
            ln.normalise(0, [])
            for s in range(SG + 1):
                if s + 1 < SG:
                    for j in range(GPS):
                        ln.take_stats(s + 1, j)
                if s < SG:
                    ln.turn(s, banks, [])
                if s + 1 < SG:
                    ln.scale(s + 1)
                if s:
                    logits(s - 1)
                if SG - 3 <= s < SG:
                    split_w(0, s - (SG - 3))
            load(1)
            p.run()

        with ExitStack() as stack:
            def sb(name, shape, dt=F32):
                return stack.enter_context(nc.sbuf_tensor(f"{name}_{tag}", shape, dt))

            silu = [sb(f"silu{i}", [P, GPS * P]) for i in range(2)]
            hid32 = [sb(f"hid32{i}", [P, GPS * P]) for i in range(2)]
            hid = [Split(nc, stack, f"hid{i}_{tag}", [P, KH, GPS * P]) for i in range(2)]
            gate_banks, up_banks, y_banks = (
                Banks([stack.enter_context(nc.psum_tensor(f"ps_{n}{i}_{tag}", [P, 512], F32)) for i in range(c)])
                for n, c in (("gate", 2), ("up", 2), ("y", 4)))
            NS = E * SG

            def gate_up(n, h):
                e, s = n // SG, n % SG
                i = (n * KH + h) % 2
                readers = {"gate": (("silu", n, h),), "up": (("hid32", n, h),)}
                got = {}
                for name, bk in (("gate", gate_banks), ("up", up_banks)):
                    bank, free = bk.take(readers[name])
                    p.wait("tensor", *both(f"w_{name}", e), *free)
                    p.split_product(bank[:, :], lambda k: w[e % 2][name].pair(
                        lambda t: t[:, k * HID + h * P:k * HID + (h + 1) * P]),
                        lambda k: xT.pair(lambda t: t[:, k, s * GPS * P:(s + 1) * GPS * P]), KD, (name + "_ps", n, h))
                    got[name] = bank
                before = ((n * KH + h) - 2) // KH, ((n * KH + h) - 2) % KH
                p.wait("scalar", ("gate_ps", n, h))
                if before[0] >= 0:
                    p.wait("scalar", ("hid32", *before))
                p.activation(silu[i][:, :], got["gate"][:, :], ACT.Silu, ("silu", n, h))
                p.wait("vector", ("silu", n, h), ("up_ps", n, h))
                if before[0] >= 0:
                    p.wait("vector", *both("hid", *before))
                p.tensor_tensor(hid32[i][:, :], got["up"][:, :], silu[i][:, :], ALU.mult, ("hid32", n, h))
                old = [("y_ps", n - 2, GPS - 1)] if n >= 2 else []
                hid[n % 2].fill(p, hid32[i][:, :], lambda t: t[:, h, :], ("hid", n, h), [("hid32", n, h)], old)

            def down(n, j):
                e, s = n // SG, n % SG
                g = s * GPS + j
                bank, free = y_banks.take((("y", n, j),))
                p.wait("tensor", *both("hid", n, KH - 1), *both("w_down", e), *free)
                p.split_product(bank[:, 0:D], lambda k: hid[n % 2].pair(lambda t: t[:, k, j * P:(j + 1) * P]),
                                lambda k: w[e % 2]["down"].pair(lambda t: t[:, k * D:(k + 1) * D]), KH,
                                ("y_ps", n, j))
                p.wait("vector", ("y_ps", n, j))
                if e:
                    p.wait("vector", ("y", n - SG, j))
                p.scalar_tensor_tensor(X[:, g, :], bank[:, 0:D], share[:, g, e:e + 1], X[:, g, :],
                                       ALU.mult, ALU.add, ("y", n, j))

            routing = route()
            for n in range(NS + 1):
                for h in range(KH):
                    if n < NS:
                        gate_up(n, h)
                    if n == 0:
                        next(routing)
                    if n and h % 2:
                        down(n - 1, h - 1)
                        down(n - 1, h)
                e, s = n // SG + 1, n % SG
                if e < E and 2 <= s < 5:
                    split_w(e, s - 2)
                if s == 6 and e + 1 < E:
                    load(e + 1)
            p.run()


class BitLinear:

    def __init__(self, p, nc, stack, X, consts, weight, banks, out):
        tag = "bit"

        def sb(name, shape, dt=F32):
            return stack.enter_context(nc.sbuf_tensor(f"{name}_{tag}", shape, dt))

        w32 = sb("w32", [P, KD * D])
        row = sb("row", [P, 1])
        scale, inv_scale = sb("scale", [P, 1]), sb("inv_scale", [P, 1])
        wq = sb("wq", [P, KD * D], BF16)
        stats, mv, = sb("stats", [P, G, 6]), sb("mv", [P, G, 2])
        var, rstd, top, inv, back = (sb(n, [P, G]) for n in ("var", "rstd", "top", "inv", "back"))
        xn = [sb(f"xn{i}", [P, GPS, D]) for i in range(2)]
        zT = [sb(f"zT{i}", [P, D], BF16) for i in range(3)]
        sum_bank, sum_free = banks.take((("bit_w", 1),))

        p.dma(w32[:, :], weight.rearrange("p a b -> p (a b)"), ("bit_w_in",))
        p.wait("vector", ("bit_w_in",))
        p.reduce(row[:, :], w32[:, :], ALU.add, ("bit_w", 0), apply_absolute_value=True)
        p.wait("tensor", ("bit_w", 0), *sum_free)
        p.matmul(sum_bank[:, 0:1], consts["ones"][:, :], row[:, :], done=("bit_sum",))
        p.wait("vector", ("bit_sum",))
        p.tensor_scalar(scale[:, :], sum_bank[:, 0:1], 1.0 / (D * D), 1e-8, ALU.mult, ALU.add, ("bit_w", 1))
        p.wait("vector", ("bit_w", 1))
        p.reciprocal(inv_scale[:, :], scale[:, :], ("bit_w", 2))
        p.wait("vector", ("bit_w", 2))
        p.tensor_scalar(w32[:, :], w32[:, :], inv_scale[:, 0:1], ROUND, ALU.mult, ALU.add, ("bit_w", 3))
        p.wait("vector", ("bit_w", 3))
        p.tensor_scalar(w32[:, :], w32[:, :], ROUND, 1.0, ALU.subtract, ALU.min, ("bit_w", 4))
        p.wait("vector", ("bit_w", 4))
        p.tensor_scalar(wq[:, :], w32[:, :], -1.0, None, ALU.max, done=("bit_w", 5))

        def take_stats(g, ready):
            p.wait("vector", ready)
            p.do("vector", lambda e: e.bn_stats(stats[:, g, :], X[:, g, :]), ("bit_stats", g))
            p.wait("vector", ("bit_stats", g))
            p.do("vector", lambda e: e.bn_aggr(mv[:, g, :], stats[:, g, :]), ("bit_aggr", g))
            if g % GPS < GPS - 1:
                return
            s, sg = g // GPS, slice(g - GPS + 1, g + 1)
            p.wait("vector", ("bit_aggr", g))
            p.tensor_scalar(var[:, sg], mv[:, sg, 1], LN_EPS, None, ALU.add, done=("bit_var", s))
            p.wait("gpsimd", ("bit_var", s))
            p.tensor_tensor(rstd[:, sg], var[:, sg], consts["minus_half"][:, :], ALU.pow, ("bit_rstd", s), "gpsimd")

        def quantise(s):
            groups = range(s * GPS, (s + 1) * GPS)
            sg, i = slice(groups[0], groups[-1] + 1), s % 2
            p.wait("vector", ("bit_rstd", s))
            if s >= 2:
                p.wait("vector", ("bit_T", groups[0] - GPS - 1))
            for j, g in enumerate(groups):
                p.tensor_scalar(xn[i][:, j, :], X[:, g, :], mv[:, g, 0:1], rstd[:, g:g + 1], ALU.subtract, ALU.mult,
                                ("bit_xn", g))
            p.wait("vector", ("bit_xn", groups[-1]))
            p.reduce(top[:, sg], xn[i][:, :, :], ALU.max, ("bit_top", s), apply_absolute_value=True)
            p.wait("vector", ("bit_top", s))
            p.tensor_scalar(top[:, sg], top[:, sg], 1e-8, None, ALU.add, done=("bit_a", s))
            p.wait("vector", ("bit_a", s))
            p.reciprocal(inv[:, sg], top[:, sg], ("bit_inv", s))
            p.tensor_scalar(back[:, sg], top[:, sg], scale[:, 0:1], 1.0 / 127.0, ALU.mult, ALU.mult,
                            ("bit_back", s))

        def round_z(s):
            groups, i = range(s * GPS, (s + 1) * GPS), s % 2
            p.wait("vector", ("bit_inv", s))
            for j, g in enumerate(groups):
                p.tensor_scalar(xn[i][:, j, :], xn[i][:, j, :], inv[:, g:g + 1], 127.0, ALU.mult, ALU.mult,
                                ("bit_z0", g))
            p.wait("vector", ("bit_z0", groups[-1]))
            p.tensor_scalar(xn[i][:, :, :], xn[i][:, :, :], 127.0, -128.0, ALU.min, ALU.max, ("bit_z1", s))
            p.wait("vector", ("bit_z1", s))
            p.tensor_scalar(xn[i][:, :, :], xn[i][:, :, :], ROUND, ROUND, ALU.add, ALU.subtract, ("bit_z", s))

        def turn(g):
            i, s, j = g % 3, g // GPS, g % GPS
            bank, free = banks.take((("bit_zT", g),))
            p.wait("tensor", ("bit_z", s), *free)
            for k in range(KD):
                p.transpose(bank[:, k * P:(k + 1) * P], xn[s % 2][:, j, k * P:(k + 1) * P], consts["ident"][:, :],
                            ("bit_T", g) if k == KD - 1 else None)
            p.wait("scalar", ("bit_T", g))
            if g >= 3:
                p.wait("scalar", ("bit_y_ps", g - 3))
            p.activation(zT[i][:, :], bank[:, 0:D], ACT.Copy, ("bit_zT", g))

        def product(g):
            i, s, j = g % 3, g // GPS, g % GPS
            bank, free = banks.take((("bit_x", g),))
            p.wait("tensor", ("bit_zT", g), ("bit_w", 5), *free)
            for k in range(KD):
                p.matmul(bank[:, 0:D], zT[i][:, k * P:(k + 1) * P], wq[:, k * D:(k + 1) * D],
                         start=k == 0, stop=k == KD - 1, done=("bit_y_ps", g) if k == KD - 1 else None)
            p.wait("vector", ("bit_y_ps", g), ("bit_back", s))
            p.scalar_tensor_tensor(X[:, g, :], bank[:, 0:D], back[:, g:g + 1], X[:, g, :], ALU.mult, ALU.add,
                                   ("bit_x", g))
            if j == GPS - 1:
                p.wait("sync", ("bit_x", g))
                p.dma(out[:, s * GPS:(s + 1) * GPS, :], X[:, s * GPS:(s + 1) * GPS, :], ("stored", s))

        self.xn = xn
        self.take_stats, self.quantise, self.round, self.turn, self.product = take_stats, quantise, round_z, turn, product


def self_attention_1(p, nc, X, consts, mats, out):
    tag = "s1"
    with ExitStack() as stack:
        def sb(name, shape, dt=F32):
            return stack.enter_context(nc.sbuf_tensor(f"{name}_{tag}", shape, dt))

        loader = Weights(p, nc, stack, tag)
        xT = [Split(nc, stack, f"xT{i}_{tag}", [P, KD, GPS * P]) for i in range(2)]
        ln = LayerNorm(p, nc, stack, tag, X, consts, xT[0])
        HB = 512 // D1
        NB = F1 // 512
        turned = [sb(f"turned{i}", [P, HB, D1]) for i in range(2)]
        swapped = [sb(f"swapped{i}", [P, HB, D1]) for i in range(2)]
        rot = [sb(f"rot{i}", [P, HB, D1]) for i in range(2)]
        qT, kT = ([sb(f"{n}{i}", [P, F1 // P, P]) for i in range(2)] for n in ("qT", "kT"))
        v = [sb(f"v{i}", [P, F1]) for i in range(2)]
        t = {n: [sb(f"{n}{i}", [P, H * T]) for i in range(2)] for n in ("shifted", "prob", "probT")}
        t |= {n: [sb(f"{n}{i}", [P, H]) for i in range(2)] for n in ("neg_max", "sums", "inv")}
        attn = sb("attn", [P, F1])
        attnT = Split(nc, stack, f"attnT_{tag}", [P, F1])
        R = P // D1
        order = HeadOrder(R, lambda r, n: n * R + r, lambda a: a.rearrange("p (n r) -> p r n", r=R))
        ps_score = stack.enter_context(nc.psum_tensor(f"ps_score_{tag}", [P, R, 512], F32))
        ps_out = stack.enter_context(nc.psum_tensor(f"ps_out_{tag}", [P, F1], F32))
        banks = Banks([stack.enter_context(nc.psum_tensor(f"ps_{i}_{tag}", [P, 512], F32)) for i in range(4)])
        t["score"] = lambda g: ps_score[:, :, 0:order.NH * T].rearrange("p r (n q) -> p r n q", q=T)
        t["score_free"] = lambda g: [("s_masked", tag, g - 1, R - 1)] if g else []
        t["out"] = lambda g: ps_out[:, :].rearrange("p (h d) -> p h d", d=D1)
        t["out_free"] = lambda g: [("s_out", tag, g - 1)] if g else []
        turns = {"n": 0}

        def project(g, i, c):
            s, j = g // GPS, g % GPS
            name = "qkv"[i]
            readers = (("s_v", tag, g, c),) if i == 2 else (("turned", tag, g, i, c), ("swap1", tag, g, i, c))
            bank, free = banks.take(readers)
            p.wait("tensor", *[r for k in range(KD) for r in both("xT", tag, s, k)], *free, *wqkv[i].ready)
            p.split_product(bank[:, :], lambda k: xT[s % 2].pair(lambda a: a[:, k, j * P:(j + 1) * P]),
                            lambda k: part(wqkv[i], k, c * 512, (c + 1) * 512), KD, ("s_qkv_ps", tag, g, i, c))
            if i == 2:
                p.wait("scalar", ("s_qkv_ps", tag, g, i, c))
                if g >= 2:
                    p.wait("scalar", ("s_pv", tag, g - 2))
                p.activation(v[g % 2][:, c * 512:(c + 1) * 512], bank[:, :], ACT.Copy, ("s_v", tag, g, c))
                return
            b3 = bank[:, :].rearrange("p (h d) -> p h d", d=D1)
            cos = consts["cos"][:, :].unsqueeze(1).to_broadcast([P, HB, D1])
            e = turns["n"] % 2
            old, turns["n"] = turns.get(e, []), turns["n"] + 1
            p.wait("vector", ("s_qkv_ps", tag, g, i, c), ("const_in",), *old)
            p.tensor_tensor(turned[e][:, :, :], b3, cos, ALU.mult, ("turned", tag, g, i, c))
            for a in range(2):
                sin = consts["sin"][:, a::2].unsqueeze(1).to_broadcast([P, HB, D1 // 2])
                p.tensor_tensor(swapped[e][:, :, a::2], b3[:, :, 1 - a::2], sin, ALU.mult, (f"swap{a}", tag, g, i, c))
            p.wait("gpsimd", ("turned", tag, g, i, c), ("swap1", tag, g, i, c))
            if old:
                p.wait("gpsimd", turns[("T", e)])
            p.tensor_tensor(rot[e][:, :, :], turned[e][:, :, :], swapped[e][:, :, :], ALU.add,
                            ("rot", tag, g, i, c), "gpsimd")
            turns[e] = [("rot", tag, g, i, c)]
            turns[("T", e)] = ("rot_T", tag, g, i, c)
            turns[("src", g, i, c)] = rot[e]

        def turn(g, i, c):
            dst = (qT, kT)[i][g % 2]
            bank, free = banks.take((("s_qkT", tag, g, i, c),))
            src = turns[("src", g, i, c)]
            p.wait("tensor", ("rot", tag, g, i, c), *free)
            for n in range(4):
                p.transpose(bank[:, n * P:(n + 1) * P], src[:, :, :].rearrange("p h d -> p (h d)")[:, n * P:(n + 1) * P],
                            consts["ident"][:, :], ("rot_T", tag, g, i, c) if n == 3 else None)
            p.wait("scalar", ("rot_T", tag, g, i, c))
            if g >= 2:
                p.wait("scalar", ("s_score", tag, g - 2))
            p.activation(dst[:, 4 * c:4 * c + 4, :], bank[:, :].rearrange("p (n q) -> p n q", q=P), ACT.Copy,
                         ("s_qkT", tag, g, i, c))

        def q_k(g):
            at = lambda a, n: (lambda b, r: a[g % 2][r * D1:(r + 1) * D1, n, b * T:(b + 1) * T])
            return [(n, at(qT, n), at(kT, n)) for n in range(order.NH)]

        def scores(g):
            ready = [("s_qkT", tag, g, 1, NB - 1), ("s_qkT", tag, g, 0, NB - 1)]
            attend(p, tag, g, q_k, order, t, D1 ** -0.5, consts["causal"][:, :], ready)

        def finish(g):
            p.wait("vector", ("s_pv", tag, g), ("s_inv", tag, g))
            if g:
                p.wait("vector", ("attn_T", tag, g - 1, NB - 1))
            p.tensor_tensor(attn[:, :].rearrange("p (h d) -> p h d", d=D1), t["out"](g),
                            t["inv"][g % 2][:, :].unsqueeze(2).to_broadcast([P, H, D1]), ALU.mult,
                            ("s_out", tag, g))

        def turn_out(g, c):
            bank, free = banks.take(both("s_attnT", tag, g, c))
            p.wait("tensor", ("s_out", tag, g), *free)
            for n in range(4):
                p.transpose(bank[:, n * P:(n + 1) * P], attn[:, c * 512 + n * P:c * 512 + (n + 1) * P],
                            consts["ident"][:, :], ("attn_T", tag, g, c) if n == 3 else None)
            old = [("s_o_ps", tag, g - 1)] if g else []
            attnT.fill(p, bank[:, :], lambda a: a[:, c * 512:(c + 1) * 512], ("s_attnT", tag, g, c),
                       [("attn_T", tag, g, c)], old)

        def add_out(g):
            bank, free = banks.take((("s_x", tag, g),))
            p.wait("tensor", *[r for c in range(NB) for r in both("s_attnT", tag, g, c)], *free, *wout.ready)
            p.split_product(bank[:, 0:D], lambda k: attnT.pair(lambda a: a[:, k * P:(k + 1) * P]),
                            lambda k: part(wout, k, 0, D), F1 // P, ("s_o_ps", tag, g))
            p.wait("vector", ("s_o_ps", tag, g))
            p.tensor_tensor(X[:, g, :], X[:, g, :], bank[:, 0:D], ALU.add, ("s_x", tag, g))

        def prepare(s):
            ln.dest = xT[s % 2]
            ln.turn(s, banks, [("s_qkv_ps", tag, (s - 1) * GPS - 1, 2, NB - 1)] if s >= 2 else [])

        bit = BitLinear(p, nc, stack, X, consts, mats["bit"], banks, out)
        flat = lambda t: t[:, :, :].rearrange("p a b -> p (a b)")
        wqkv = [loader.load(f"qkv{i}", mats["qkv"][i], m)
                for i, m in enumerate(([flat(a) for a in qT], [flat(a) for a in kT], v))]
        wout = loader.load("out", mats["out"], [flat(a) for a in bit.xn])
        ln.normalise(0, [])
        loader.split(wqkv[0])
        prepare(0)
        loader.split(*wqkv[1:], wout)
        for g in range(G + 2 + 2 * GPS):
            now, before, out = g < G, 1 <= g <= G, 2 <= g < G + 2
            if now:
                project(g, 0, 0)
                project(g, 0, 1)
            if out:
                turn_out(g - 2, 0)
            if now:
                project(g, 1, 0)
                project(g, 1, 1)
            if out:
                turn_out(g - 2, 1)
            if now:
                turn(g, 0, 0)
                turn(g, 0, 1)
            if before:
                scores(g - 1)
            if now:
                project(g, 2, 0)
                turn(g, 1, 0)
            if out:
                add_out(g - 2)
            s, j = g // GPS + 1, g % GPS
            if s < SG and j == 3:
                prepare(s)
            if s < SG and j == 1:
                for i in range(GPS):
                    ln.take_stats(s, i)
            if s < SG and j == 2:
                ln.scale(s)
            if 0 <= g - 3 < G:
                bit.take_stats(g - 3, ("s_x", tag, g - 3))
            done, j = divmod(g - GPS - 2, GPS)
            if 0 <= done < SG:
                if j == 1:
                    bit.quantise(done)
                if j == 2:
                    bit.round(done)
            if now:
                turn(g, 1, 1)
                project(g, 2, 1)
            if 0 <= g - GPS - 5 < G:
                bit.turn(g - GPS - 5)
            if before:
                p.wait("tensor", ("s_v", tag, g - 1, NB - 1))
                weigh_self(p, tag, g - 1, lambda g: v[g % 2], D1, order, t)
                finish(g - 1)
            if 0 <= g - GPS - 5 < G:
                bit.product(g - GPS - 5)
        p.wait("sync", ("stored", SG - 1))
        p.run()


def build(nc, a, out):
    with ExitStack() as stack:
        def sb(name, shape):
            return stack.enter_context(nc.sbuf_tensor(name, shape, F32))

        p = Program(nc, stack)
        X = sb("X", [P, G, D])
        table = sb("constants", list(a["tables"].shape))
        starts = np.cumsum([0, *TABLES.values()])
        consts = {n: table[:, c:c + w] for (n, w), c in zip(TABLES.items(), starts.tolist())}
        biases = {n: sb("bias_" + n, [P, KD] if n != "o" else [P, D]) for n in "qkvo"}

        def load_x(s):
            p.dma(X[:, s * GPS:(s + 1) * GPS, :], a["x"][:, s * GPS:(s + 1) * GPS, :], (f"x_in{s}",))

        load_x(0)
        p.dma(table[:, :], a["tables"], ("const", "tables"))
        for n, t in biases.items():
            src = a["b_" + n]
            p.dma(t[:, :], src.partition_broadcast(P) if n == "o" else src, ("const", "bias_" + n))
        p.done[("const_in",)] = ("const", p.count["const"])
        for e in ("tensor", "vector", "scalar", "gpsimd"):
            p.wait(e, ("const_in",))

        x_ready = lambda s: (f"x_in{s}",)
        cross_attention(p, nc, "x0", X, a["ctx"], consts, {n: a["x0_" + n] for n in "qkvo"}, biases, x_ready, load_x)
        self_attention_0(p, nc, X, consts, {n: a["s0_" + n] for n in "qkv"})
        experts(p, nc, X, consts, {n: a["moe_" + n] for n in ("router", "gate", "up", "down")})
        cross_attention(p, nc, "x1", X, a["ctx"], consts, {n: a["x1_" + n] for n in "qo"}, None, x_ready, None)
        self_attention_1(p, nc, X, consts, {"qkv": a["s1_qkv"], "out": a["s1_out"], "bit": a["bit_weight"]}, out)


def tables():
    rows = np.arange(P)
    position = rows % T
    freqs = 1.0 / 10000.0 ** (np.arange(0, D1, 2) / D1)
    angle = (np.arange(T)[:, None].astype(np.float32) * freqs[None, :].astype(np.float32))[position]
    sin = np.repeat(np.sin(angle), 2, axis=1)
    sin[:, 0::2] *= -1.0
    big = np.finfo(np.float32).max
    out = {
        "ident": np.eye(P),
        "head_rows": (rows[:, None] // XD == np.arange(HPH)[None, :]),
        "causal": np.where(position[:, None] >= np.arange(T)[None, :], big, NEG_INF),
        "cos": np.repeat(np.cos(angle), 2, axis=1),
        "sin": sin,
        "numbers": np.tile(np.arange(E), (P, 1)),
        "ones": np.ones((P, P)),
        "same_query": position[:, None] == np.arange(T)[None, :],
        "head_sum": np.concatenate([4 * n + rows[:, None] // T == rows[None, :] // XD for n in range(HG // KD)], 1),
        "of_pair": rows[:, None] // XD % 2 == np.arange(2)[None, :],
        "minus_half": np.full((P, GPS), -0.5),
    }
    assert {n: t.shape[1] for n, t in out.items()} == TABLES
    return {"tables": np.concatenate([out[n] for n in TABLES], axis=1).astype(np.float32)}


def lay_out(i):
    def pieces(m):
        return m.reshape(m.shape[0] // P, P, m.shape[1]).transpose(1, 0, 2)

    a = {
        "x": i["x"].reshape(G, P, D).transpose(1, 0, 2),
        "ctx": i["ctx_1024"].transpose(0, 2, 1).reshape(G, BPG, KD, P, S).transpose(0, 3, 2, 1, 4),
        "x0_q": pieces(i["L0_xattn_Wq"].T), "x0_k": pieces(i["L0_xattn_Wk"].T),
        "x0_v": pieces(i["L0_xattn_Wv"].T), "x0_o": pieces(i["L0_xattn_Wo"].T),
        "b_q": i["L0_xattn_bq"].reshape(KD, P).T, "b_k": i["L0_xattn_bk"].reshape(KD, P).T,
        "b_v": i["L0_xattn_bv"].reshape(KD, P).T, "b_o": i["L0_xattn_bo"],
        "s0_q": pieces(i["L0_attn_w_Q"]), "s0_k": pieces(i["L0_attn_w_K"]),
        "s0_v": pieces(i["L0_attn_w_V"]),
        "moe_router": pieces(i["L0_ffn_router_w"].T),
        "moe_gate": np.stack([pieces(m.T) for m in i["L0_ffn_w_gate"]]),
        "moe_up": np.stack([pieces(m.T) for m in i["L0_ffn_w_up"]]),
        "moe_down": np.stack([pieces(m.T) for m in i["L0_ffn_w_down"]]),
        "x1_q": pieces(i["L1_xattn_Wq"].T), "x1_o": pieces(i["L1_xattn_Wo"].T),
        "s1_qkv": np.stack([pieces(m) for m in np.split(i["L1_attn_W_qkv"], 3, axis=1)]),
        "s1_out": pieces(i["L1_attn_W_out"]),
        "bit_weight": pieces(i["L1_ffn_weight"].T),
    }
    return {n: np.ascontiguousarray(t) for n, t in a.items()}


def kernel(**inputs):
    import concourse.bacc as _bacc
    from concourse.bass_utils import run_bass_kernel_spmd as _run

    nc = _bacc.Bacc("TRN2", target_bir_lowering=False, num_devices=1)
    arrays = {**lay_out({n: np.asarray(t) for n, t in inputs.items()}), **tables()}
    aps = {n: nc.dram_tensor(n, t.shape, F32, kind="ExternalInput").ap() for n, t in arrays.items()}
    out = nc.dram_tensor("out", (P, G, D), F32, kind="ExternalOutput").ap()
    build(nc, aps, out)
    r = _run(nc, [arrays], core_ids=[0])
    return r.results[0]["out"].transpose(1, 0, 2).reshape(B, T, D)
```
